# Optimizing a Trainium2 kernel written in Bass

```python
import numpy as np
import jax
import jax.numpy as jnp

def _softmax(x, axis=-1):
    return jax.nn.softmax(x, axis=axis)

def _gelu(x):
    return jax.nn.gelu(x, approximate=True)

def _silu(x):
    return jax.nn.silu(x)

def _sigmoid(x):
    return jax.nn.sigmoid(x)

def _layernorm(x, axis=-1, eps=1e-05):
    m = jnp.mean(x, axis=axis, keepdims=True)
    v = jnp.var(x, axis=axis, keepdims=True)
    return (x - m) / jnp.sqrt(v + eps)

def _scatter_add(tgt, idx, src, axis=0):
    return tgt.at[idx].add(src)

def _segment_sum(src, seg, n):
    return jax.ops.segment_sum(src, seg, n)
kernel_name = 'mk_conv_preact_d4_conv_nchw384_r2_eb9fee'

def setup_inputs(seed: int=0):
    np.random.seed(seed)
    _w = jnp.asarray

    def _rec_inputs():
        import jax
        import jax.numpy as jnp
        _gk = jax.random.key(seed)
        x = -0.0004039 + 1 * jax.random.normal(jax.random.fold_in(_gk, 1), (2, 192, 64, 64), jnp.float32)
        return x
    x = _rec_inputs()

    def _L0_conv_setup():
        import jax, jax.numpy as jnp
        import numpy as np
        from jax import lax

        def _conv1x1(x, w):
            return jnp.einsum('bchw,oc->bohw', x, w)

        def _dwconv(x, w, pad):
            return lax.conv_general_dilated(x, w, window_strides=(1, 1), padding=[(pad, pad), (pad, pad)], dimension_numbers=('NCHW', 'OIHW', 'NCHW'), feature_group_count=w.shape[0])

        def _l2norm(x, axis=-1, eps=1e-12):
            n = jnp.sqrt(jnp.sum(x * x, axis=axis, keepdims=True))
            return x / jnp.maximum(n, eps)

        def _topk_masked_softmax(attn, k):
            B, H, C, _ = attn.shape
            flat = attn.reshape(B * H * C, C)
            vals, idx = lax.top_k(flat, k)
            rows = jnp.arange(flat.shape[0])[:, None]
            scat = jnp.full_like(flat, -jnp.inf).at[rows, idx].set(vals)
            return jax.nn.softmax(scat, axis=-1).reshape(B, H, C, C)
        key = jax.random.key(seed)
        ks = jax.random.split(key, 7)
        dim, heads = (192, 8)
        x = jax.random.normal(ks[0], (2, dim, 64, 64), jnp.float32)
        s = 0.02
        w_qkv = jax.random.normal(ks[1], (dim * 3, dim), jnp.float32) * s
        w_dw3 = jax.random.normal(ks[2], (dim * 3, 1, 3, 3), jnp.float32) * s
        w_dw5 = jax.random.normal(ks[3], (dim * 3, 1, 5, 5), jnp.float32) * s
        w_dw7 = jax.random.normal(ks[4], (dim * 3, 1, 7, 7), jnp.float32) * s
        w_pconv = jax.random.normal(ks[5], (dim * 3, dim * 9), jnp.float32) * s
        w_proj = jax.random.normal(ks[6], (dim, dim), jnp.float32) * s
        temperature = jnp.ones((heads, 1, 1), jnp.float32)
        attn_scales = jnp.full((3,), 0.2, jnp.float32)
        return {'x': x, 'w_qkv': w_qkv, 'w_dw3': w_dw3, 'w_dw5': w_dw5, 'w_dw7': w_dw7, 'w_pconv': w_pconv, 'w_proj': w_proj, 'temperature': temperature, 'attn_scales': attn_scales}
    _L0_conv_all = _L0_conv_setup()
    _L0_conv_in = {k: v for k, v in _L0_conv_all.items() if k in ('w_qkv', 'w_dw3', 'w_dw5', 'w_dw7', 'w_pconv', 'w_proj', 'temperature', 'attn_scales')}
    del _L0_conv_all

    def _L1_conv_setup():
        import jax, jax.numpy as jnp
        import numpy as np
        NUM_HEADS = 8
        EPS = 1e-12

        def _l2norm(t):
            n = jnp.sqrt(jnp.sum(t * t, axis=-1, keepdims=True))
            return t / jnp.maximum(n, EPS)
        key = jax.random.key(seed)
        k1, k2 = jax.random.split(key)
        x = jax.random.normal(k1, (8, 192, 64, 64), dtype=jnp.float32)
        w_qkv = jax.random.normal(k2, (576, 192), dtype=jnp.float32) * (1.0 / np.sqrt(192))
        return {'x': x, 'w_qkv': w_qkv}
    _L1_conv_all = _L1_conv_setup()
    _L1_conv_in = {k: v for k, v in _L1_conv_all.items() if k in ('w_qkv',)}
    del _L1_conv_all

    def _L2_conv_setup():
        import jax, jax.numpy as jnp
        import numpy as np
        DIM = 192
        D_STATE = 16

        def _selective_scan(x_in, delta, A, Bm, Cm, D):
            Bsz, L, dim = x_in.shape
            n = A.shape[1]

            def step(h, inp):
                d_t, x_t, b_t, c_t = inp
                h = jnp.exp(d_t[..., None] * A) * h + (d_t * x_t)[..., None] * b_t[:, None, :]
                y_t = jnp.einsum('bdn,bn->bd', h, c_t)
                return (h, y_t)
            h0 = jnp.zeros((Bsz, dim, n), dtype=x_in.dtype)
            xs = (jnp.swapaxes(delta, 0, 1), jnp.swapaxes(x_in, 0, 1), jnp.swapaxes(Bm, 0, 1), jnp.swapaxes(Cm, 0, 1))
            _, ys = jax.lax.scan(step, h0, xs)
            y = jnp.swapaxes(ys, 0, 1)
            return y + x_in * D
        key = jax.random.key(seed)
        ks = jax.random.split(key, 8)
        B, C, H, W = (4, DIM, 32, 32)
        x = jax.random.normal(ks[0], (B, C, H, W), dtype=jnp.float32)
        P = 2 * DIM + 2 * D_STATE
        W_proj = jax.random.normal(ks[1], (P, DIM), dtype=jnp.float32) * 0.02
        b_proj = jnp.zeros((P,), dtype=jnp.float32)
        A_log = jnp.log(jax.random.uniform(ks[2], (DIM, D_STATE), dtype=jnp.float32) + 0.0001)
        D = jnp.ones((DIM,), dtype=jnp.float32)
        dt_bias = jnp.zeros((DIM,), dtype=jnp.float32)
        W_out = jax.random.normal(ks[3], (DIM, DIM), dtype=jnp.float32) * 0.02
        b_out = jnp.zeros((DIM,), dtype=jnp.float32)
        return {'x': x, 'W_proj': W_proj, 'b_proj': b_proj, 'A_log': A_log, 'D': D, 'dt_bias': dt_bias, 'W_out': W_out, 'b_out': b_out}
    _L2_conv_all = _L2_conv_setup()
    _L2_conv_in = {k: v for k, v in _L2_conv_all.items() if k in ('W_proj', 'b_proj', 'A_log', 'D', 'dt_bias', 'W_out', 'b_out')}
    del _L2_conv_all

    def _L3_conv_setup():
        import jax, jax.numpy as jnp
        import numpy as np
        C = 192
        K = 7
        S = 1
        P = K // 2
        key = jax.random.key(seed)
        k1, k2, k3 = jax.random.split(key, 3)
        x = jax.random.normal(k1, (16, C, 64, 64), dtype=jnp.float32)
        w = jax.random.normal(k2, (C, 1, K, K), dtype=jnp.float32) * (1.0 / K)
        b = jax.random.normal(k3, (C,), dtype=jnp.float32) * 0.01
        return {'x': x, 'w': w, 'b': b}
    _L3_conv_all = _L3_conv_setup()
    _L3_conv_in = {k: v for k, v in _L3_conv_all.items() if k in ('w', 'b')}
    del _L3_conv_all
    return {'x': x, 'L0_conv_w_qkv': _L0_conv_in['w_qkv'], 'L0_conv_w_dw3': _L0_conv_in['w_dw3'], 'L0_conv_w_dw5': _L0_conv_in['w_dw5'], 'L0_conv_w_dw7': _L0_conv_in['w_dw7'], 'L0_conv_w_pconv': _L0_conv_in['w_pconv'], 'L0_conv_w_proj': _L0_conv_in['w_proj'], 'L0_conv_temperature': _L0_conv_in['temperature'], 'L0_conv_attn_scales': _L0_conv_in['attn_scales'], 'L1_conv_w_qkv': _L1_conv_in['w_qkv'], 'L2_conv_W_proj': _L2_conv_in['W_proj'], 'L2_conv_b_proj': _L2_conv_in['b_proj'], 'L2_conv_A_log': _L2_conv_in['A_log'], 'L2_conv_D': _L2_conv_in['D'], 'L2_conv_dt_bias': _L2_conv_in['dt_bias'], 'L2_conv_W_out': _L2_conv_in['W_out'], 'L2_conv_b_out': _L2_conv_in['b_out'], 'L3_conv_w': _L3_conv_in['w'], 'L3_conv_b': _L3_conv_in['b']}

def reference(x, L0_conv_w_qkv, L0_conv_w_dw3, L0_conv_w_dw5, L0_conv_w_dw7, L0_conv_w_pconv, L0_conv_w_proj, L0_conv_temperature, L0_conv_attn_scales, L1_conv_w_qkv, L2_conv_W_proj, L2_conv_b_proj, L2_conv_A_log, L2_conv_D, L2_conv_dt_bias, L2_conv_W_out, L2_conv_b_out, L3_conv_w, L3_conv_b):
    import jax
    import jax.numpy as jnp

    def _L0_conv_ref(x, w_qkv, w_dw3, w_dw5, w_dw7, w_pconv, w_proj, temperature, attn_scales):
        import jax, jax.numpy as jnp
        import numpy as np
        from jax import lax

        def _conv1x1(x, w):
            return jnp.einsum('bchw,oc->bohw', x, w)

        def _dwconv(x, w, pad):
            return lax.conv_general_dilated(x, w, window_strides=(1, 1), padding=[(pad, pad), (pad, pad)], dimension_numbers=('NCHW', 'OIHW', 'NCHW'), feature_group_count=w.shape[0])

        def _l2norm(x, axis=-1, eps=1e-12):
            n = jnp.sqrt(jnp.sum(x * x, axis=axis, keepdims=True))
            return x / jnp.maximum(n, eps)

        def _topk_masked_softmax(attn, k):
            B, H, C, _ = attn.shape
            flat = attn.reshape(B * H * C, C)
            vals, idx = lax.top_k(flat, k)
            rows = jnp.arange(flat.shape[0])[:, None]
            scat = jnp.full_like(flat, -jnp.inf).at[rows, idx].set(vals)
            return jax.nn.softmax(scat, axis=-1).reshape(B, H, C, C)
        b, c, h, w = x.shape
        heads = temperature.shape[0]
        base = _conv1x1(x, w_qkv)
        qkv = jnp.concatenate([_dwconv(base, w_dw3, 1), _dwconv(base, w_dw5, 2), _dwconv(base, w_dw7, 3)], axis=1)
        qkv = _conv1x1(qkv, w_pconv)
        q, k, v = jnp.split(qkv, 3, axis=1)

        def heads_split(t):
            return t.reshape(b, heads, c // heads, h * w)
        q, k, v = (heads_split(q), heads_split(k), heads_split(v))
        q = _l2norm(q)
        k = _l2norm(k)
        attn = jnp.einsum('bhcn,bhdn->bhcd', q, k) * temperature
        C = q.shape[2]
        out = jnp.zeros_like(v)
        for i, top_k in enumerate([int(C / 2), int(C * 2 / 3), int(C * 3 / 4)]):
            a = _topk_masked_softmax(attn, top_k)
            out = out + attn_scales[i] * jnp.einsum('bhcd,bhdn->bhcn', a, v)
        out = out.reshape(b, c, h, w)
        return _conv1x1(out, w_proj)

    def _L1_conv_ref(x, w_qkv):
        import jax, jax.numpy as jnp
        import numpy as np
        NUM_HEADS = 8
        EPS = 1e-12

        def _l2norm(t):
            n = jnp.sqrt(jnp.sum(t * t, axis=-1, keepdims=True))
            return t / jnp.maximum(n, EPS)
        B, C, H, W = x.shape
        hw = H * W
        head_c = C // NUM_HEADS
        qkv = jnp.einsum('bchw,oc->bohw', x, w_qkv)
        q, k, v = jnp.split(qkv, 3, axis=1)

        def rs(t):
            return t.reshape(B, NUM_HEADS, head_c, hw)
        q, k, v = (rs(q), rs(k), rs(v))
        q = _l2norm(q)
        k = _l2norm(k)
        scale = jnp.sqrt(jnp.float32(hw))
        attn = jnp.einsum('bhcn,bhdn->bhcd', q, k) / scale
        attn = jax.nn.softmax(attn, axis=-1)
        out = jnp.einsum('bhcd,bhdn->bhcn', attn, v)
        return out.reshape(B, C, H, W)

    def _L2_conv_ref(x, W_proj, b_proj, A_log, D, dt_bias, W_out, b_out):
        import jax, jax.numpy as jnp
        import numpy as np
        DIM = 192
        D_STATE = 16

        def _selective_scan(x_in, delta, A, Bm, Cm, D):
            Bsz, L, dim = x_in.shape
            n = A.shape[1]

            def step(h, inp):
                d_t, x_t, b_t, c_t = inp
                h = jnp.exp(d_t[..., None] * A) * h + (d_t * x_t)[..., None] * b_t[:, None, :]
                y_t = jnp.einsum('bdn,bn->bd', h, c_t)
                return (h, y_t)
            h0 = jnp.zeros((Bsz, dim, n), dtype=x_in.dtype)
            xs = (jnp.swapaxes(delta, 0, 1), jnp.swapaxes(x_in, 0, 1), jnp.swapaxes(Bm, 0, 1), jnp.swapaxes(Cm, 0, 1))
            _, ys = jax.lax.scan(step, h0, xs)
            y = jnp.swapaxes(ys, 0, 1)
            return y + x_in * D
        B, C, H, W = x.shape
        L = H * W
        seq = x.reshape(B, C, L).transpose(0, 2, 1)
        proj = seq @ W_proj.T + b_proj
        x_in = proj[..., :DIM]
        delta = proj[..., DIM:2 * DIM]
        Bm = proj[..., 2 * DIM:2 * DIM + D_STATE]
        Cm = proj[..., 2 * DIM + D_STATE:]
        A = -jnp.exp(A_log)
        delta = jax.nn.softplus(delta + dt_bias)
        y = _selective_scan(x_in, delta, A, Bm, Cm, D)
        out = y @ W_out.T + b_out
        return out.transpose(0, 2, 1).reshape(B, C, H, W)

    def _L3_conv_ref(x, w, b):
        import jax, jax.numpy as jnp
        import numpy as np
        C = 192
        K = 7
        S = 1
        P = K // 2
        xp = jnp.pad(x, ((0, 0), (0, 0), (P, P), (P, P)), mode='reflect')
        out = jax.lax.conv_general_dilated(xp, w, window_strides=(S, S), padding='VALID', dimension_numbers=('NCHW', 'OIHW', 'NCHW'), feature_group_count=C)
        return out + b[None, :, None, None]

    def _gn(v, G=32, eps=1e-05):
        B_, C_, H_, W_ = v.shape
        g = v.reshape(B_, G, C_ // G, H_, W_)
        m = jnp.mean(g, axis=(2, 3, 4), keepdims=True)
        s = jnp.var(g, axis=(2, 3, 4), keepdims=True)
        return ((g - m) / jnp.sqrt(s + eps)).reshape(v.shape)

    def _ln_c(v, eps=1e-06):
        m = jnp.mean(v, axis=1, keepdims=True)
        s = jnp.var(v, axis=1, keepdims=True)
        return (v - m) / jnp.sqrt(s + eps)

    def _ln_t(v, eps=1e-05):
        m = jnp.mean(v, axis=-1, keepdims=True)
        s = jnp.var(v, axis=-1, keepdims=True)
        return (v - m) / jnp.sqrt(s + eps)

    def _to_tokens(v):
        B_, C_, H_, W_ = v.shape
        return v.reshape(B_, C_, H_ * W_).transpose(0, 2, 1)

    def _from_tokens(t, like):
        B_, C_, H_, W_ = like.shape
        return t.transpose(0, 2, 1).reshape(B_, C_, H_, W_)
    x = x + _L0_conv_ref(_gn(x), L0_conv_w_qkv, L0_conv_w_dw3, L0_conv_w_dw5, L0_conv_w_dw7, L0_conv_w_pconv, L0_conv_w_proj, L0_conv_temperature, L0_conv_attn_scales)
    x = x + _L1_conv_ref(_gn(x), L1_conv_w_qkv)
    x = x + _L2_conv_ref(_gn(x), L2_conv_W_proj, L2_conv_b_proj, L2_conv_A_log, L2_conv_D, L2_conv_dt_bias, L2_conv_W_out, L2_conv_b_out)
    x = x + _L3_conv_ref(_gn(x), L3_conv_w, L3_conv_b)
    return x

_drawn_inputs = setup_inputs


def setup_inputs(seed=0):
    import zlib

    import numpy as np

    out = dict(_drawn_inputs(seed))
    spreads = {'L0_conv_temperature': (1.0, 0.6),
     'L0_conv_attn_scales': (0.20000000298023224, 0.6),
     'L2_conv_b_proj': (0.0, 0.1),
     'L2_conv_D': (1.0, 0.6),
     'L2_conv_dt_bias': (0.0, 2.0),
     'L2_conv_b_out': (0.0, 0.302)}
    factors = {'L0_conv_w_qkv': 8.0,
     'L0_conv_w_dw3': 8.0,
     'L0_conv_w_dw5': 8.0,
     'L0_conv_w_dw7': 8.0,
     'L0_conv_w_pconv': 8.0,
     'L0_conv_w_proj': 8.0,
     'L3_conv_b': 21.358}
    for name, (base, spread) in spreads.items():
        noise = np.random.default_rng([zlib.crc32(name.encode()), seed]).standard_normal(out[name].shape)
        drawn = base * np.exp(spread * noise) if base else spread * noise
        out[name] = jnp.asarray(drawn.astype(out[name].dtype))
    for name, factor in factors.items():
        out[name] = (out[name] * factor).astype(out[name].dtype)
    return out
```

```python
import concourse.bass as bass
from concourse import mybir
from contextlib import ExitStack

F32 = mybir.dt.float32
BF16 = mybir.dt.bfloat16
ALU = mybir.AluOpType
ACT = mybir.ActivationFunctionType
AX = mybir.AxisListType.X

B, C, H, W = 2, 192, 64, 64
HW = H * W
HC = C // 2
QKV = 3 * C
HEADS, HD = 8, 24
HH = HC // HD
EPS_GN = 1e-5
BH = 2 * B

NT = 3

NTT, NG, CG = 3, 3, 64
R = 8
NS = H // R
RB = R + 6
PW_ = W + 6
PX = R * W
KS = [3, 5, 7]
TAPS = [k * k for k in KS]
NTAP = sum(TAPS)
SLOTS = 28
TSL = 6
KT = 15
KG75, KG3 = 9, 12
OPS = NTT * NTAP + NG * TSL

N_STATE = 16
CH = 1024
ROWS_V = 40


def depthwise_plan():
    def chain(src, ktile, taps):
        return [(src, ktile, n == 0, dy, dx, w) for n, (dy, dx, w) in enumerate(taps)]

    def tile(t):
        cs, w0 = [], 0
        for k in range(3):
            s, p = KS[k], KS[k] // 2
            cs.append(chain(("T", t), 3 * t + k,
                            [(3 - p + a, 3 - p + b, t * NTAP + w0 + a * s + b) for a in range(s) for b in range(s)]))
            w0 += TAPS[k]
        return cs[0] + cs[1], cs[2]

    def merge(a, b):
        out = []
        for n in range(max(len(a), len(b))):
            out += a[n:n + 1] + b[n:n + 1]
        return out

    group = [chain(("G", g), KG3 + g, [(2 + a, 2 + 2 * j, g * TSL + 2 * a + j) for a in range(3) for j in range(2)])
             for g in range(NG)]
    return merge(*tile(0)) + merge(group[0] + group[1], group[2]) + merge(*tile(1)) + merge(*tile(2))


PLAN = depthwise_plan()
LAST = {}
PREV = []
for _n, _o in enumerate(PLAN):
    PREV.append(LAST.get(_o[1], 0))
    LAST[_o[1]] = _n + 1
SRC_LAST = {}
for _n, _o in enumerate(PLAN):
    SRC_LAST[_o[0]] = _n + 1


class Arena:

    def __init__(self, mem, size):
        self.mem, self.size, self.at = mem, size, 0

    def take(self, *dims):
        n = 1
        for d in dims:
            n *= d
        v = self.mem[:, self.at:self.at + n]
        self.at += n
        assert self.at <= self.size, (self.at, self.size)
        if len(dims) == 2:
            v = v.rearrange("p (a b) -> p a b", a=dims[0])
        if len(dims) == 3:
            v = v.rearrange("p (a b c) -> p a b c", a=dims[0], b=dims[1])
        return v

    def take_bf16(self, *dims):
        n = 1
        for d in dims:
            n *= d
        v = self.mem[:, self.at:self.at + n // 2].bitcast(BF16)
        self.at += n // 2
        assert self.at <= self.size
        if len(dims) == 2:
            v = v.rearrange("p (a b) -> p a b", a=dims[0])
        if len(dims) == 3:
            v = v.rearrange("p (a b c) -> p a b c", a=dims[0], b=dims[1])
        return v


def pieces(t):
    if t < 2:
        return [(0, t, 0, 128)]
    return [(0, 0, 128, 64), (64, 1, 128, 64)]


def linear(nc, out, wa, wc, o0, t, src, n0, n):
    last = None
    if t < 2:
        lo = 64 * t
        nc.tensor.matmul(out, wa[:, o0:o0 + 128], src[:, t, n0:n0 + n], start=True, stop=False)
        return nc.tensor.matmul(out, wc[lo:lo + 64, o0:o0 + 128], src[lo:lo + 64, 2, n0:n0 + n], start=False, stop=True)
    for b in range(B):
        lo = 64 * b
        nc.tensor.matmul(out[lo:lo + 64], wa[:, o0 + 128:o0 + 192], src[:, b, n0:n0 + n], start=True, stop=False)
        last = nc.tensor.matmul(out[lo:lo + 64], wc[lo:lo + 64, o0 + 128:o0 + 192], src[lo:lo + 64, 2, n0:n0 + n],
                                start=False, stop=True)
    return last


def build(nc, inp, out):
    with ExitStack() as ctx:
        SIZE = 53100
        mem = ctx.enter_context(nc.sbuf_tensor("mem", [128, SIZE], F32))
        ps = ctx.enter_context(nc.psum_tensor("ps", [128, 8, 512], F32))
        n_sem = [0]

        def sem(name):
            n_sem[0] += 1
            return ctx.enter_context(nc.semaphore(f"{name}_{n_sem[0]}"))

        def dram(name, shape):
            return nc.dram_tensor(name, shape, F32).ap()

        xnp = dram("xn_padded", [B, C, H + 6, W])
        x1 = dram("x_after_0", [B, C, HW])
        x2 = dram("x_after_1", [B, C, HW])
        x3 = dram("x_after_2", [B, C, HW])
        xin = inp["x"].rearrange("b c h w -> b c (h w)")
        xout = out.rearrange("b c h w -> b c (h w)")

        ar = Arena(mem, SIZE)
        ident = ar.take(128)
        gacc = ar.take(BH, 3 * HC)
        attn_w = ar.take(BH, HC)
        keep = ar.at

        def fresh():
            a = Arena(mem, SIZE)
            a.at = keep
            return a

        group_norm(nc, sem, fresh(), ps, inp, xin, 0, ident, xnp)
        layer0_conv(nc, sem, fresh(), ps, inp, xnp, ident, gacc, attn_w, xin, x1)
        layer1(nc, sem, fresh(), ps, inp, x1, x2, ident, gacc, attn_w)
        layer2(nc, sem, fresh(), ps, inp, x2, x3, ident)
        layer3(nc, sem, fresh(), ps, inp, x3, xout, ident)


def group_norm(nc, sem, ar, ps, inp, x_dram, layer, ident, xnp=None, xt=None, padded=None):
    if xt is None:
        xt = ar.take(NT, HW)
    gm = ar.take(2 * 192)
    stats = ar.take(NT * 8, 6)
    mv = ar.take(NT, 2)
    sq = ar.take(NT, 1)
    gst = ar.take(NT, 2)
    var = ar.take(NT)
    msq = ar.take(NT)
    sd = ar.take(NT)
    rs = ar.take(NT)
    t1 = ar.take(NT)
    nb = ar.take(NT)
    zero = ar.take(3 * W)
    loaded = [sem(f"norm{layer}_x_loaded") for _ in range(NT)]
    consts = sem(f"norm{layer}_consts")
    stat_done = sem(f"norm{layer}_stats")
    chain = sem(f"norm{layer}_vector_chain")
    averaged = sem(f"norm{layer}_averaged")
    rooted = sem(f"norm{layer}_rooted")
    ready = sem(f"norm{layer}_scale_ready")
    normed = [sem(f"norm{layer}_tile{t}_done") for t in range(NT)]
    stored = sem(f"norm{layer}_stored")
    zeroed = sem(f"norm{layer}_zeroed")

    def dest(t):
        if padded is None:
            return xt[:, t, :]
        return padded[:, t * 4900:(t + 1) * 4900].rearrange("p (r w) -> p r w", r=70)[:, 3:67, 3:67]

    def source(t):
        if padded is None:
            return xt[:, t, :]
        return xt[:, t, :].rearrange("p (r w) -> p r w", r=H)

    with nc.Block() as block:
        @block.sync
        def _(sp):
            for t in range(NT):
                for p0, b, c0, n in pieces(t):
                    sp.dma_start(xt[p0:p0 + n, t, :], x_dram[b, c0:c0 + n, :]).then_inc(loaded[t], 16)
            if layer == 0:
                sp.dma_start(ident, inp["ident"]).then_inc(consts, 16)
            sp.dma_start(gm, inp["gmat"]).then_inc(consts, 16)
            if xnp is not None:
                sp.wait_ge(zeroed, 1)
                for b in range(B):
                    for r0 in (0, H + 3):
                        sp.dma_start(xnp[b, :, r0:r0 + 3, :].rearrange("(h p) r w -> p h (r w)", h=2)[:, 0], zero[0:HC]).then_inc(stored, 16)
                        sp.dma_start(xnp[b, :, r0:r0 + 3, :].rearrange("(h p) r w -> p h (r w)", h=2)[:, 1], zero[0:HC]).then_inc(stored, 16)
                n_st = 8
                for t in range(NT):
                    sp.wait_ge(normed[t], 1)
                    for p0, b, c0, n in pieces(t):
                        sp.dma_start(xnp[b, c0:c0 + n, 3:H + 3, :].rearrange("c r w -> c (r w)"),
                                     xt[p0:p0 + n, t, :]).then_inc(stored, 16)
                        n_st += 1
                sp.wait_ge(stored, 16 * n_st)

        @block.vector
        def _(dve):
            n = [0]

            def step(ins):
                ins.then_inc(chain, 1)
                n[0] += 1
                dve.wait_ge(chain, n[0])

            if xnp is not None:
                nc.vector.memset(zero, 0.0).then_inc(zeroed, 1)
            for t in range(NT):
                dve.wait_ge(loaded[t], 16 * len(pieces(t)))
                for k in range(8):
                    last = nc.vector.bn_stats(stats[:, t * 8 + k, :], xt[:, t, 512 * k:512 * k + 512])
                    last.then_inc(chain, 1)
                    n[0] += 1
            dve.wait_ge(chain, n[0])
            for t in range(NT):
                ins = nc.vector.bn_aggr(mv[:, t, :], stats[:, t * 8:t * 8 + 8, :].rearrange("p a b -> p (a b)"))
                ins.then_inc(chain, 1)
                n[0] += 1
            dve.wait_ge(chain, n[0])
            step(nc.vector.tensor_tensor(sq[:, :, 0], mv[:, :, 0], mv[:, :, 0], ALU.mult))
            nc.vector.tensor_tensor(mv[:, :, 1], mv[:, :, 1], sq[:, :, 0], ALU.add).then_inc(stat_done, 1)
            dve.wait_ge(averaged, 1)
            step(nc.vector.tensor_copy(gst, ps[:, 0:NT, 0:2]))
            step(nc.vector.tensor_tensor(msq, gst[:, :, 0], gst[:, :, 0], ALU.mult))
            step(nc.vector.tensor_tensor(var, gst[:, :, 1], msq, ALU.subtract))
            step(nc.vector.tensor_scalar(var, var, EPS_GN, None, ALU.add))
            nc.vector.tensor_copy(t1, var).then_inc(ready, 1)
            dve.wait_ge(rooted, 1)
            step(nc.vector.reciprocal(rs, sd))
            step(nc.vector.tensor_tensor(sd, rs, rs, ALU.mult))
            step(nc.vector.tensor_tensor(sd, sd, var, ALU.mult))
            step(nc.vector.tensor_scalar(sd, sd, -0.5, 1.5, ALU.mult, ALU.add))
            step(nc.vector.tensor_tensor(rs, rs, sd, ALU.mult))
            step(nc.vector.tensor_tensor(nb, gst[:, :, 0], rs, ALU.mult))
            step(nc.vector.tensor_scalar(nb, nb, -1.0, None, ALU.mult))
            nc.vector.tensor_scalar(dest(0), source(0), rs[:, 0:1], nb[:, 0:1], ALU.mult, ALU.add).then_inc(normed[0], 1)
            nc.vector.tensor_scalar(dest(1), source(1), rs[:, 1:2], nb[:, 1:2], ALU.mult, ALU.add).then_inc(normed[1], 1)

        @block.tensor
        def _(pe):
            pe.wait_ge(consts, 32 if layer == 0 else 16)
            pe.wait_ge(stat_done, 1)
            for t in range(NT):
                last = linear(nc, ps[:, t, 0:2], gm[:, 0:192], gm[:, 192:384], 0, t, mv, 0, 2)
            last.then_inc(averaged, 1)

        @block.scalar
        def _(act):
            act.wait_ge(ready, 1)
            nc.scalar.activation(sd, var, ACT.Sqrt).then_inc(rooted, 1)
            act.wait_ge(chain, NT * 8 + NT + 1 + 4 + 7)
            nc.scalar.activation(dest(2), source(2), ACT.Identity, bias=nb[:, 2:3],
                                 scale=rs[:, 2:3]).then_inc(normed[2], 1)


def layer0_conv(nc, sem, ar, ps, inp, xnp, ident, gacc, attn_w, xin, x1):
    vt = ar.take(B * NS * 4, C)
    loop_at = ar.at
    wbase = ar.take(2, 2 * NTT * 128)
    wt = ar.take(NTT * NTAP)
    wg3 = ar.take(NG * TSL)
    pw = ar.take(KT, QKV)
    diag = ar.take(NG * SLOTS, 128)
    wd = ar.take(NG * SLOTS, 2)
    mask2 = ar.take(CG)
    xs = ar.take(2, RB * W)
    baseT = ar.take(NTT, RB * PW_)
    baseG = ar.take(NG, RB * PW_)
    dbuf = ar.take(KT, PX)
    qk = ar.take(4, 2 * C)
    gtmp = ar.take(2, 3 * HC)

    def slot(k):
        return dbuf[:, k, :]

    psb = ps[:, 0:2, :]
    psd = ps[:, 2, :]
    psa = ps[:, 3:7, :]
    psv = ps[:, 7, 0:4 * CG].rearrange("p (a c) -> p a c", a=4)

    weights = sem("l0_weights_loaded")
    diag_ready = sem("l0_diagonals_ready")
    cleared = sem("l0_borders_cleared")
    gcleared = sem("l0_gram_cleared")
    xs_loaded = sem("l0_strip_loaded")
    xs_used = sem("l0_strip_used")
    base_sum = sem("l0_base_in_psum")
    base_out = sem("l0_base_in_sbuf")
    dw_ops = sem("l0_vector_depthwise_ops")
    gdw_sum = sem("l0_group_depthwise_in_psum")
    gdw_out = sem("l0_group_depthwise_in_sbuf")
    acc_done = sem("l0_pconv_done")
    qkv_out = sem("l0_qkv_in_sbuf")
    gram_sum = sem("l0_gram_in_psum")
    gram_out = sem("l0_gram_in_sbuf")
    gram_add = sem("l0_gram_added")

    ORDER = {("T", 0): 0, ("G", 0): 1, ("T", 1): 2, ("G", 1): 3, ("G", 2): 4, ("T", 2): 5}

    def buf(kind, n):
        return (baseT if kind == "T" else baseG)[:, n, :].rearrange("p (r w) -> p r w", r=RB)

    with nc.Block() as block:
        @block.sync
        def _(sp):
            for dst, name in ((wbase[0:HC], "wbase"), (wt, "wt"), (wg3, "wg3"), (wd, "wd"), (mask2, "mask2"), (pw, "pw")):
                sp.dma_start(dst, inp[name]).then_inc(weights, 16)
            for b in range(B):
                with sp.Fori(0, NS) as s:
                    i = s + NS * b
                    sp.wait_ge(xs_used, i + 1)
                    sp.dma_start(xs[0:HC], xnp[b, :, bass.ds(s * R, RB), :].rearrange("(h p) r w -> p h (r w)", h=2)
                                 ).then_inc(xs_loaded, 16)

        @block.gpsimd
        def _(pool):
            nc.gpsimd.memset(baseT, 0.0).then_inc(cleared, 1)
            nc.gpsimd.memset(baseG, 0.0).then_inc(cleared, 1)
            nc.gpsimd.memset(gacc, 0.0).then_inc(gcleared, 1)
            pool.wait_ge(weights, 96)
            for g in range(NG):
                nc.gpsimd.tensor_tensor(
                    diag[:, g * SLOTS:(g + 1) * SLOTS, :].rearrange("p s (u c) -> p (s u) c", u=2),
                    mask2.unsqueeze(1).to_broadcast([128, 2 * SLOTS, CG]),
                    wd[:, g * SLOTS:(g + 1) * SLOTS, :].rearrange("p s u -> p (s u)").unsqueeze(2).to_broadcast([128, 2 * SLOTS, CG]),
                    ALU.mult).then_inc(diag_ready, 1)
            pool.wait_ge(gcleared, 1)
            pool.sem_inc(gram_add, 1)
            for b in range(B):
                with pool.Fori(0, NS) as s:
                    i = s + NS * b
                    pool.wait_ge(gram_out, i + 2)
                    nc.gpsimd.tensor_tensor(gacc[0:HC, 2 * b:2 * b + 2, :], gacc[0:HC, 2 * b:2 * b + 2, :],
                                            gtmp[0:HC], ALU.add).then_inc(gram_add, 1)
                    pool.wait_ge(gram_add, i + 2)

        @block.vector
        def _(dve):
            dve.sem_inc(dw_ops, OPS)
            dve.wait_ge(weights, 96)

            def strip(i):
                for n, (src, ktile, first, r0, c0, w) in enumerate(PLAN):
                    if src[1] == 0 and src[0] == "T" and n == 0 or n and PLAN[n - 1][0] != src:
                        dve.wait_ge(base_out, 6 * i + ORDER[src] + 1)
                    x = buf(*src)[:, r0:r0 + R, c0:c0 + W]
                    o = slot(ktile).rearrange("p (r w) -> p r w", r=R)
                    if first:
                        ins = nc.vector.tensor_scalar(o, x, (wt if src[0] == "T" else wg3)[:, w:w + 1], None, ALU.mult)
                    else:
                        dve.wait_ge(dw_ops, OPS * (i + 1) + PREV[n])
                        ins = nc.vector.scalar_tensor_tensor(out=o, in0=x, scalar=(wt if src[0] == "T" else wg3)[:, w:w + 1],
                                                             in1=o, op0=ALU.mult, op1=ALU.add)
                    ins.then_inc(dw_ops, 1)

            with dve.Fori(0, B * NS) as s:
                strip(s)

        @block.scalar
        def _(act):
            act.wait_ge(cleared, 2)
            act.sem_inc(gram_out, 1)
            act.sem_inc(qkv_out, 1)

            def base_copy(i, kind, n):
                act.wait_ge(base_sum, 6 * i + ORDER[kind, n] + 1)
                act.wait_ge(dw_ops, OPS * i + SRC_LAST[kind, n])
                src = psb[:, :, 0:RB // 2 * W].rearrange("p a (r w) -> p a r w", w=W)
                if kind == "T":
                    dst = buf(kind, n)[:, :, 3:3 + W].rearrange("p (a r) w -> p a r w", a=2)
                    nc.scalar.copy(dst, src).then_inc(base_out, 1)
                else:
                    d0 = buf(kind, n)[0:CG, :, 3:3 + W].rearrange("p (a r) w -> p a r w", a=2)
                    d1 = buf(kind, n)[CG:128, :, 2:2 + W].rearrange("p (a r) w -> p a r w", a=2)
                    nc.scalar.copy(d0, src[0:CG])
                    nc.scalar.copy(d1, src[CG:128]).then_inc(base_out, 1)

            def group_copy(i3, g):
                act.wait_ge(gdw_sum, i3)
                nc.scalar.copy(slot(KG75 + g), psd).then_inc(gdw_out, 1)

            def body(b, s, last):
                i = s + NS * b
                base_copy(i, "T", 1)
                base_copy(i, "G", 1)
                base_copy(i, "G", 2)
                group_copy(3 * i + 2, 1)
                base_copy(i, "T", 2)
                group_copy(3 * i + 3, 2)
                if not last:
                    base_copy(i + 1, "T", 0)
                    base_copy(i + 1, "G", 0)
                    group_copy(3 * i + 4, 0)
                act.wait_ge(acc_done, i + 1)
                nc.scalar.copy(qk, psa[:, :, 0:2 * C])
                k0 = 4 * s + 4 * NS * b
                nc.scalar.copy(vt[:, bass.ds(k0, 4), 0:128], psa[:, :, 2 * C:512])
                nc.scalar.copy(vt[:, bass.ds(k0, 4), 128:192], psv).then_inc(qkv_out, 1)
                act.wait_ge(gram_sum, i + 1)
                act.wait_ge(gram_add, i + 1)
                nc.scalar.copy(gtmp[0:HC, :, 0:2 * HC], psb[0:HC, 0, 0:4 * HC].rearrange("p (a c) -> p a c", a=2))
                nc.scalar.copy(gtmp[0:HC, :, 2 * HC:3 * HC], psb[0:HC, 1, 0:2 * HC].rearrange("p (a c) -> p a c", a=2)
                               ).then_inc(gram_out, 1)

            base_copy(0, "T", 0)
            base_copy(0, "G", 0)
            group_copy(1, 0)
            with act.Fori(0, NS) as s:
                body(0, s, False)
            with act.Fori(0, NS - 1) as s:
                body(1, s, False)
            body(1, NS - 1, True)

        @block.tensor
        def _(pe):
            def base(i, kind, n):
                m = 6 * i + ORDER[kind, n]
                pe.wait_ge(base_out, m)
                if (kind, n) == ("T", 1):
                    pe.wait_ge(gram_out, i + 1)
                if (kind, n) == ("T", 0):
                    pe.wait_ge(xs_loaded, 16 * (i + 1))
                o0 = (n if kind == "T" else NTT + n) * 128
                for h in range(2):
                    for a in range(2):
                        ins = nc.tensor.matmul(psb[:, a, 0:RB // 2 * W], wbase[0:HC, h, o0:o0 + 128],
                                               xs[0:HC, h, a * RB // 2 * W:(a + 1) * RB // 2 * W],
                                               start=(h == 0), stop=(h == 1))
                ins.then_inc(base_sum, 1)

            def group_depthwise(i, g, m):
                pe.wait_ge(base_out, 6 * i + ORDER["G", g] + 1)
                pe.wait_ge(gdw_out, m)
                for sl in range(SLOTS):
                    dy, dx = sl // 4, 2 * (sl % 4)
                    ins = nc.tensor.matmul(psd.rearrange("p (r w) -> p r w", r=R), diag[:, g * SLOTS + sl, :],
                                           buf("G", g)[:, dy:dy + R, dx:dx + W], start=(sl == 0), stop=(sl == SLOTS - 1))
                ins.then_inc(gdw_sum, 1)

            def pconv(k, first=False, last=False):
                d = slot(k)
                for p in range(4):
                    nc.tensor.matmul(psa[:, p, :], d[:, 128 * p:128 * p + 128], pw[:, k, 0:512], start=first, stop=last)
                    ins = nc.tensor.matmul(psv[:, p, :], d[:, 128 * p:128 * p + 128], pw[:, k, 512:QKV],
                                           start=first and p == 0, stop=last, skip_group_check=True)
                return ins

            def tiles(i, ks):
                for k in ks:
                    pe.wait_ge(dw_ops, OPS * (i + 1) + LAST[k])
                    ins = pconv(k, last=(k == 8))
                return ins

            def gram(i):
                pe.wait_ge(qkv_out, i + 2)
                for p in range(4):
                    for h in range(2):
                        sel = qk[:, p, :].rearrange("p (a c) -> p a c", a=2)[:, :, h * HC:(h + 1) * HC]
                        nc.tensor.matmul(psb[0:HC, 0, 2 * HC * h:2 * HC * (h + 1)].rearrange("p (a c) -> p a c", a=2),
                                         qk[:, p, h * HC:(h + 1) * HC], sel,
                                         start=(p == 0 and h == 0), stop=(p == 3), skip_group_check=True)
                        ks = qk[:, p, C + h * HC:C + (h + 1) * HC]
                        ins = nc.tensor.matmul(psb[0:HC, 1, HC * h:HC * (h + 1)], ks, ks,
                                               start=(p == 0 and h == 0), stop=(p == 3), skip_group_check=True)
                ins.then_inc(gram_sum, 1)

            def body(i, last):
                pe.wait_ge(gdw_out, 3 * i + 1)
                pe.wait_ge(qkv_out, i + 1)
                pconv(KG75, first=True)
                base(i, "T", 1)
                base(i, "G", 1)
                base(i, "G", 2)
                group_depthwise(i, 1, 3 * i + 1)
                base_t2 = base(i, "T", 2)
                pe.wait_ge(base_out, 6 * i + 6)
                pe.sem_inc(xs_used, 1)
                pe.wait_ge(gdw_out, 3 * i + 2)
                pconv(KG75 + 1)
                tiles(i, [0, 1, 2, KG3, KG3 + 1, KG3 + 2])
                group_depthwise(i, 2, 3 * i + 2)
                if not last:
                    base(i + 1, "T", 0)
                    base(i + 1, "G", 0)
                pe.wait_ge(gdw_out, 3 * i + 3)
                pconv(KG75 + 2)
                tiles(i, [3, 4, 5])
                if not last:
                    group_depthwise(i + 1, 0, 3 * i + 3)
                tiles(i, [6, 7, 8]).then_inc(acc_done, 1)
                gram(i)

            pe.sem_inc(xs_used, 1)
            pe.wait_ge(weights, 96)
            base(0, "T", 0)
            base(0, "G", 0)
            pe.wait_ge(diag_ready, NG)
            group_depthwise(0, 0, 0)
            with pe.Fori(0, NS) as s:
                body(s, False)
            with pe.Fori(0, NS - 1) as s:
                body(s + NS, False)
            body(2 * NS - 1, True)

    ar.at = loop_at
    attention(nc, sem, ar, ps, inp, ident, gacc, attn_w, 0)

    m0 = ar.take(BH, C)
    wp = ar.take(2, C)
    vs = ar.take(4, PX)
    xr = ar.take(4, PX)
    wp_loaded = sem("l0_wproj_loaded")
    m_sum = sem("l0_m_in_psum")
    m_out = sem("l0_m_in_sbuf")
    x_loaded = [sem("l0_x_loaded") for _ in range(2)]
    v_sum = sem("l0_v_transposed")
    v_out = sem("l0_v_in_sbuf")
    o_sum = sem("l0_out_in_psum")
    o_add = sem("l0_out_added")
    o_st = sem("l0_out_stored")

    with nc.Block() as block:
        def store(sp, i):
            b, s, j = i // NS, i % NS, i % 2
            sp.wait_ge(o_add, i + 1)
            sp.dma_start(x1[b, :, s * PX:(s + 1) * PX].rearrange("(h p) n -> p h n", h=2),
                         xr[0:HC, 2 * j:2 * j + 2, :]).then_inc(o_st, 16)

        @block.sync
        def _(sp):
            sp.dma_start(wp[0:HC], inp["wproj0"]).then_inc(wp_loaded, 16)
            for i in range(B * NS):
                j = i % 2
                if i >= 2:
                    sp.wait_ge(o_st, 16 * (i - 1))
                b, s = i // NS, i % NS
                sp.dma_start(xr[0:HC, 2 * j:2 * j + 2, :],
                             xin[b, :, s * PX:(s + 1) * PX].rearrange("(h p) n -> p h n", h=2)).then_inc(x_loaded[j], 16)
                if i >= 1:
                    store(sp, i - 1)
            store(sp, B * NS - 1)
            sp.wait_ge(o_st, 16 * B * NS)

        @block.tensor
        def _(pe):
            pe.wait_ge(wp_loaded, 16)
            for bh in range(BH):
                ins = nc.tensor.matmul(ps[0:HC, bh, 0:C], attn_w[0:HC, bh, :], wp[0:HC, bh % 2, :], start=True, stop=True)
            ins.then_inc(m_sum, 1)
            pe.wait_ge(m_out, 1)
            for i in range(B * NS + 1):
                if i < B * NS:
                    if i >= 2:
                        pe.wait_ge(v_out, i - 1)
                    for h in range(2):
                        for p in range(4):
                            ins = nc.tensor.transpose(ps[0:HC, 2 * (i % 2) + h, 128 * p:128 * p + 128],
                                                      vt[:, 4 * i + p, HC * h:HC * h + HC], ident)
                    ins.then_inc(v_sum, 1)
                if i >= 1:
                    k = i - 1
                    pe.wait_ge(v_out, k + 1)
                    if k >= 2:
                        pe.wait_ge(o_add, k - 1)
                    for oc in range(2):
                        for h in range(2):
                            ins = nc.tensor.matmul(ps[0:HC, 4 + 2 * (k % 2) + oc, :],
                                                   m0[0:HC, 2 * (k // NS) + h, oc * HC:(oc + 1) * HC],
                                                   vs[0:HC, 2 * (k % 2) + h, :], start=(h == 0), stop=(h == 1))
                    ins.then_inc(o_sum, 1)

        @block.scalar
        def _(act):
            act.wait_ge(m_sum, 1)
            nc.scalar.copy(m0[0:HC], ps[0:HC, 0:BH, 0:C]).then_inc(m_out, 1)
            for i in range(B * NS):
                act.wait_ge(v_sum, i + 1)
                if i >= 2:
                    act.wait_ge(o_sum, i - 1)
                nc.scalar.copy(vs[0:HC, 2 * (i % 2):2 * (i % 2) + 2, :], ps[0:HC, 2 * (i % 2):2 * (i % 2) + 2, :]
                               ).then_inc(v_out, 1)

        @block.vector
        def _(dve):
            for i in range(B * NS):
                j = i % 2
                dve.wait_ge(o_sum, i + 1)
                dve.wait_ge(x_loaded[j], 16 * (i // 2 + 1))
                nc.vector.tensor_tensor(xr[0:HC, 2 * j:2 * j + 2, :], ps[0:HC, 4 + 2 * j:6 + 2 * j, :],
                                        xr[0:HC, 2 * j:2 * j + 2, :], ALU.add).then_inc(o_add, 1)


def attention(nc, sem, ar, ps, inp, ident, gacc, attn_w, layer):
    at = ar.at
    tmp = ar.take(BH, HC)
    ssq = ar.take(2, BH)
    nrm = ar.take(2, BH)
    rcp = ar.take(2, BH)
    dg = ar.take(BH, HC)
    sc = ar.take(BH, HC)
    bm = ar.take(HH)
    a = ar.take(BH, HD)
    e = ar.take(BH, HD)
    mx = ar.take(BH)
    ones = ar.take(HC)
    temp = ar.take(2)
    scl = ar.take(3)
    tri = ar.take(HD, HD)
    cmp = ar.take(BH * HD, HD)
    eq = ar.take(BH * HD, HD)
    rank = ar.take(BH, HD)
    em = ar.take(BH, HD)
    se = ar.take(BH)
    wsum = ar.take(BH, HD)
    ar.at = at

    consts = sem(f"attn{layer}_consts")
    chain = sem(f"attn{layer}_chain")
    sums = sem(f"attn{layer}_square_sums")
    roots = sem(f"attn{layer}_roots")
    diag_k = sem(f"attn{layer}_k_diagonal")
    bcast = sem(f"attn{layer}_k_broadcast")
    centred = sem(f"attn{layer}_centred")
    exped = sem(f"attn{layer}_exp")
    P_ = slice(0, HC)

    def bc(v, shape):
        return v.to_broadcast(shape)

    with nc.Block() as block:
        @block.sync
        def _(sp):
            sp.dma_start(bm[P_], inp["head_mask"]).then_inc(consts, 16)
            sp.dma_start(temp[P_], inp["temperature_rows"]).then_inc(consts, 16)
            sp.dma_start(scl[P_], inp["scales_rows"]).then_inc(consts, 16)
            sp.dma_start(tri[P_], inp["tri"]).then_inc(consts, 16)

        @block.tensor
        def _(pe):
            pe.wait_ge(diag_k, 1)
            nc.tensor.matmul(ps[P_, 0, 0:BH * HC], ones[P_, :], dg[P_].rearrange("p a c -> p (a c)"),
                             start=True, stop=True).then_inc(bcast, 1)

        @block.scalar
        def _(act):
            act.wait_ge(sums, 1)
            nc.scalar.activation(nrm[P_], ssq[P_], ACT.Sqrt).then_inc(roots, 1)
            act.wait_ge(centred, 1)
            nc.scalar.activation(e[P_], em[P_], ACT.Exp).then_inc(exped, 1)

        @block.vector
        def _(dve):
            n = [0]

            def step(ins):
                ins.then_inc(chain, 1)
                n[0] += 1
                dve.wait_ge(chain, n[0])

            V = nc.vector
            dve.wait_ge(consts, 64)
            step(V.memset(ones[P_], 1.0))
            idb = bc(ident[P_, 0:HC].unsqueeze(1), [HC, BH, HC])
            for x, lo in ((0, 0), (1, 2 * HC)):
                step(V.tensor_tensor(tmp[P_], gacc[P_, :, lo:lo + HC], idb, ALU.mult))
                step(V.tensor_reduce(ssq[P_, x, :], tmp[P_], AX, ALU.add))
            V.tensor_copy(rcp[P_], ssq[P_]).then_inc(sums, 1)
            dve.wait_ge(roots, 1)
            step(V.tensor_scalar(nrm[P_], nrm[P_], 1e-12, None, ALU.max))
            step(V.reciprocal(rcp[P_], nrm[P_]))
            V.tensor_tensor(dg[P_], idb, bc(rcp[P_, 1, :].unsqueeze(2), [HC, BH, HC]), ALU.mult).then_inc(diag_k, 1)
            dve.wait_ge(bcast, 1)
            step(V.tensor_tensor(sc[P_], gacc[P_, :, HC:2 * HC], ps[P_, 0, 0:BH * HC].rearrange("p (a c) -> p a c", a=BH), ALU.mult))
            step(V.tensor_tensor(sc[P_].rearrange("p b (h j) -> p b h j", h=HH), sc[P_].rearrange("p b (h j) -> p b h j", h=HH),
                                 bc(bm[P_].unsqueeze(1).unsqueeze(3), [HC, BH, HH, HD]), ALU.mult))
            step(V.tensor_reduce(a[P_], sc[P_].rearrange("p b (h j) -> p b j h", h=HH), AX, ALU.add))
            step(V.tensor_tensor(a[P_], a[P_], bc(rcp[P_, 0, :].unsqueeze(2), [HC, BH, HD]), ALU.mult))
            if layer == 0:
                step(V.tensor_tensor(a[P_].rearrange("p (b h) j -> p b h j", b=B), a[P_].rearrange("p (b h) j -> p b h j", b=B),
                                     bc(temp[P_].unsqueeze(1).unsqueeze(3), [HC, B, 2, HD]), ALU.mult))
            else:
                step(V.tensor_scalar(a[P_], a[P_], 1.0 / float(HW) ** 0.5, None, ALU.mult))
            step(V.tensor_reduce(mx[P_], a[P_], AX, ALU.max))
            V.tensor_tensor(em[P_], a[P_], bc(mx[P_].unsqueeze(2), [HC, BH, HD]), ALU.subtract).then_inc(centred, 1)
            if layer == 0:
                for b in range(BH):
                    ai = bc(a[P_, b, :].unsqueeze(2), [HC, HD, HD])
                    aj = bc(a[P_, b, :].unsqueeze(1), [HC, HD, HD])
                    cb, eb = cmp[P_, b * HD:(b + 1) * HD, :], eq[P_, b * HD:(b + 1) * HD, :]
                    step(V.tensor_tensor(cb, aj, ai, ALU.is_gt))
                    step(V.tensor_tensor(eb, aj, ai, ALU.is_equal))
                    step(V.tensor_tensor(eb, eb, tri[P_], ALU.mult))
                    step(V.tensor_tensor(cb, cb, eb, ALU.add))
                step(V.tensor_reduce(rank[P_], cmp[P_].rearrange("p (b i) j -> p b i j", b=BH), AX, ALU.add))
            dve.wait_ge(exped, 1)
            parts = [HD // 2, HD * 2 // 3, HD * 3 // 4] if layer == 0 else [HD]
            for k, top in enumerate(parts):
                if layer == 0:
                    step(V.tensor_scalar(em[P_], rank[P_], float(top), None, ALU.is_lt))
                    step(V.tensor_tensor(em[P_], em[P_], e[P_], ALU.mult))
                else:
                    step(V.tensor_copy(em[P_], e[P_]))
                step(V.tensor_reduce(se[P_], em[P_], AX, ALU.add))
                step(V.reciprocal(se[P_], se[P_]))
                if layer == 0:
                    step(V.tensor_scalar(se[P_], se[P_], scl[P_, k:k + 1], None, ALU.mult))
                dst = wsum if k == 0 else em
                step(V.tensor_tensor(dst[P_], em[P_], bc(se[P_].unsqueeze(2), [HC, BH, HD]), ALU.mult))
                if k:
                    step(V.tensor_tensor(wsum[P_], wsum[P_], em[P_], ALU.add))
            for b in range(BH):
                step(V.tensor_tensor(attn_w[P_, b, :].rearrange("p (h j) -> p h j", h=HH),
                                     bc(wsum[P_, b, :].unsqueeze(1), [HC, HH, HD]),
                                     bc(bm[P_].unsqueeze(2), [HC, HH, HD]), ALU.mult))


def residual_block(nc, sem, ps, tag, res_dram, out_dram, xr, linear_of, bias=None):
    NP = NT * 2
    loaded = [sem(f"{tag}_residual_loaded") for _ in range(2)]
    summed = sem(f"{tag}_sum_in_psum")
    added = sem(f"{tag}_added")
    stored = sem(f"{tag}_stored")
    n_st = [0]
    after = []
    for i in range(NP):
        n_st[0] += len(pieces(i // 2))
        after.append(n_st[0])

    with nc.Block() as block:
        def store(sp, i):
            t, n0 = i // 2, (i % 2) * 2048
            sp.wait_ge(added, 4 * (i + 1))
            for p0, b, c0, n in pieces(t):
                sp.dma_start(out_dram[b, c0:c0 + n, n0:n0 + 2048], xr[p0:p0 + n, i % 2, :]).then_inc(stored, 16)

        @block.sync
        def _(sp):
            for i in range(NP):
                t, n0 = i // 2, (i % 2) * 2048
                if i >= 2:
                    sp.wait_ge(stored, 16 * after[i - 2])
                for p0, b, c0, n in pieces(t):
                    sp.dma_start(xr[p0:p0 + n, i % 2, :], res_dram[b, c0:c0 + n, n0:n0 + 2048]).then_inc(loaded[i % 2], 16)
                if i >= 1:
                    store(sp, i - 1)
            store(sp, NP - 1)
            sp.wait_ge(stored, 16 * after[-1])

        @block.tensor
        def _(pe):
            for m in range(NP * 4):
                if m >= 8:
                    pe.wait_ge(added, m - 7)
                linear_of(ps[:, m % 8, :], m // 8, (m % 8) * 512).then_inc(summed, 1)

        @block.vector
        def _(dve):
            need = [0, 0]
            for m in range(NP * 4):
                i = m // 4
                if m % 4 == 0:
                    need[i % 2] += 16 * len(pieces(i // 2))
                    dve.wait_ge(loaded[i % 2], need[i % 2])
                dve.wait_ge(summed, m + 1)
                x = xr[:, i % 2, (m % 4) * 512:(m % 4) * 512 + 512]
                if bias is None:
                    ins = nc.vector.tensor_tensor(x, ps[:, m % 8, :], x, ALU.add)
                else:
                    ins = nc.vector.scalar_tensor_tensor(out=x, in0=ps[:, m % 8, :], scalar=bias[:, m // 8:m // 8 + 1],
                                                         in1=x, op0=ALU.add, op1=ALU.add)
                ins.then_inc(added, 1)


def layer1(nc, sem, ar, ps, inp, x1, x2, ident, gacc, attn_w):
    xn = ar.take(NT, HW)
    at = ar.at
    group_norm(nc, sem, ar, ps, inp, x1, 1, ident, xt=xn)
    ar.at = at
    SRC = [0, 2, 1]
    NB = HW // 128
    xt = ar.take(2, 2 * C)
    xx = ar.take(B * 2, C)
    wqk = ar.take(2, 2 * C)
    tt = ar.take(B * 2, 2 * C)
    wv = ar.take(2, C)
    wload = sem("l1_weights")
    tsum = sem("l1_transposed")
    tout = sem("l1_transposed_out")
    xxsum = sem("l1_xx_sum")
    xxout = sem("l1_xx_out")
    tts = sem("l1_t_sum")
    tto = sem("l1_t_out")
    gsum = sem("l1_gram_sum")

    def parts(b):
        if b == 0:
            return [(0, 0, 0, 128), (1, 128, 128, 64)]
        return [(0, 256, 64, 128), (1, 192, 0, 64)]

    with nc.Block() as block:
        @block.sync
        def _(sp):
            sp.dma_start(wqk[:, 0, :], inp["w1qk"][0:128, :]).then_inc(wload, 16)
            sp.dma_start(wqk[0:64, 1, :], inp["w1qk"][128:192, :]).then_inc(wload, 16)
            sp.dma_start(wv[0:HC], inp["w1v"]).then_inc(wload, 16)

        @block.tensor
        def _(pe):
            for k in range(NB + 1):
                if k < NB:
                    if k >= 2:
                        pe.wait_ge(tout, k - 1)
                    for m, t in enumerate(SRC):
                        ins = nc.tensor.transpose(ps[:, k % 2, 128 * m:128 * m + 128], xn[:, t, 128 * k:128 * k + 128], ident)
                    ins.then_inc(tsum, 1)
                if k >= 1:
                    j = k - 1
                    pe.wait_ge(tout, j + 1)
                    for b in range(B):
                        for rb, x0, _, n in parts(b):
                            ins = nc.tensor.matmul(ps[0:n, 2 + rb, C * b:C * b + C], xt[:, j % 2, x0:x0 + n],
                                                   xt[:, j % 2, C * b:C * b + C],
                                                   start=(j == 0 and b == 0), stop=(j == NB - 1), skip_group_check=True)
                    if j == NB - 1:
                        ins.then_inc(xxsum, 1)
            pe.wait_ge(wload, 48)
            pe.wait_ge(xxout, 2)
            for b in range(B):
                for rb, _, c0, n in parts(b):
                    for kb in range(2):
                        kn = 64 if kb else 128
                        ins = nc.tensor.matmul(ps[0:n, 4 + 2 * b + rb, 0:2 * C], xx[0:kn, 2 * b + kb, c0:c0 + n],
                                               wqk[0:kn, kb, :], start=(kb == 0), stop=(kb == 1))
            ins.then_inc(tts, 1)
            pe.wait_ge(tto, 1)
            for b in range(B):
                for h in range(2):
                    for kb in range(2):
                        kn = 64 if kb else 128
                        t = tt[0:kn, 2 * b + kb, :]
                        nc.tensor.matmul(ps[0:HC, 2 * b + h, 0:2 * HC].rearrange("p (a c) -> p a c", a=2),
                                         wqk[0:kn, kb, h * HC:(h + 1) * HC],
                                         t.rearrange("p (a c) -> p a c", a=2)[:, :, h * HC:(h + 1) * HC],
                                         start=(kb == 0), stop=(kb == 1), skip_group_check=True)
                    for kb in range(2):
                        kn = 64 if kb else 128
                        ins = nc.tensor.matmul(ps[0:HC, 4 + 2 * b + h, 0:HC], wqk[0:kn, kb, C + h * HC:C + (h + 1) * HC],
                                               tt[0:kn, 2 * b + kb, C + h * HC:C + (h + 1) * HC],
                                               start=(kb == 0), stop=(kb == 1), skip_group_check=True)
            ins.then_inc(gsum, 1)

        @block.scalar
        def _(act):
            for k in range(NB):
                act.wait_ge(tsum, k + 1)
                nc.scalar.copy(xt[:, k % 2, :], ps[:, k % 2, 0:2 * C]).then_inc(tout, 1)
            act.wait_ge(xxsum, 1)
            nc.scalar.copy(xx.rearrange("p (b r) c -> p b r c", b=B)[:, :, 0, :],
                           ps[:, 2, 0:2 * C].rearrange("p (b c) -> p b c", b=B)).then_inc(xxout, 1)
            nc.scalar.copy(xx.rearrange("p (b r) c -> p b r c", b=B)[0:64, :, 1, :],
                           ps[0:64, 3, 0:2 * C].rearrange("p (b c) -> p b c", b=B)).then_inc(xxout, 1)
            act.wait_ge(tts, 1)
            nc.scalar.copy(tt.rearrange("p (b r) c -> p b r c", b=B)[:, :, 0, :],
                           ps[:, 4:8, 0:2 * C].rearrange("p (b r) c -> p b r c", b=B)[:, :, 0, :])
            nc.scalar.copy(tt.rearrange("p (b r) c -> p b r c", b=B)[0:64, :, 1, :],
                           ps[0:64, 4:8, 0:2 * C].rearrange("p (b r) c -> p b r c", b=B)[:, :, 1, :]).then_inc(tto, 1)
            act.wait_ge(gsum, 1)
            nc.scalar.copy(gacc[0:HC, :, 0:2 * HC], ps[0:HC, 0:4, 0:2 * HC])
            nc.scalar.copy(gacc[0:HC, :, 2 * HC:3 * HC], ps[0:HC, 4:8, 0:HC])

    ar.at = at + 2 * 2 * C
    keep_wv = ar.take(2, C)
    wv_at = ar.at
    del keep_wv
    ar.at = at + 2 * 2 * C + B * 2 * C + 2 * 2 * C + B * 2 * 2 * C + 2 * C
    attention(nc, sem, ar, ps, inp, ident, gacc, attn_w, 1)

    awt = ar.take(BH, HC)
    ma = ar.take(B, C)
    mc = ar.take(C)
    a_sum = sem("l1_attn_transposed")
    a_out = sem("l1_attn_out")
    m_sum = sem("l1_m_sum")
    m_out = sem("l1_m_out")
    with nc.Block() as block:
        @block.tensor
        def _(pe):
            for bh in range(BH):
                ins = nc.tensor.transpose(ps[0:HC, 0, bh * HC:(bh + 1) * HC], attn_w[0:HC, bh, :], ident[0:HC, 0:HC])
            ins.then_inc(a_sum, 1)
            pe.wait_ge(a_out, 1)
            for b in range(B):
                for h in range(2):
                    nc.tensor.matmul(ps[:, 1 + b, h * HC:(h + 1) * HC], wv[0:HC, h, 0:128], awt[0:HC, 2 * b + h, :],
                                     start=(h == 0), stop=True, skip_group_check=True)
                    ins = nc.tensor.matmul(ps[64 * b:64 * b + 64, 3 + b, h * HC:(h + 1) * HC], wv[0:HC, h, 128:192],
                                           awt[0:HC, 2 * b + h, :], start=(h == 0), stop=True, skip_group_check=True)
            ins.then_inc(m_sum, 1)

        @block.scalar
        def _(act):
            act.wait_ge(a_sum, 1)
            nc.scalar.copy(awt[0:HC], ps[0:HC, 0, 0:BH * HC].rearrange("p (a c) -> p a c", a=BH)).then_inc(a_out, 1)
            act.wait_ge(m_sum, 1)
            nc.scalar.copy(ma, ps[:, 1:3, 0:C])
            for b in range(B):
                nc.scalar.copy(mc[64 * b:64 * b + 64], ps[64 * b:64 * b + 64, 3 + b, 0:C]).then_inc(m_out, 1)

    def lin(out, t, n0):
        if t < 2:
            lo = 64 * t
            nc.tensor.matmul(out, ma[:, t, 0:128], xn[:, t, n0:n0 + 512], start=True, stop=False)
            return nc.tensor.matmul(out, mc[lo:lo + 64, 0:128], xn[lo:lo + 64, 2, n0:n0 + 512], start=False, stop=True)
        for b in range(B):
            lo = 64 * b
            nc.tensor.matmul(out[lo:lo + 64], ma[:, b, 128:192], xn[:, b, n0:n0 + 512], start=True, stop=False)
            ins = nc.tensor.matmul(out[lo:lo + 64], mc[lo:lo + 64, 128:192], xn[lo:lo + 64, 2, n0:n0 + 512],
                                   start=False, stop=True)
        return ins

    xr = ar.take(2, 2048)
    residual_block(nc, sem, ps, "l1", x1, x2, xr, lin)


def layer2(nc, sem, ar, ps, inp, x2, x3, ident):
    xn = ar.take(NT, HW)
    at = ar.at
    group_norm(nc, sem, ar, ps, inp, x2, 2, ident, xt=xn)
    ar.at = at
    NP2 = 2 * C + 4 * 32
    y = ar.take(NT, HW)
    wa = ar.take(NP2)
    wc = ar.take(NP2)
    woa = ar.take(C)
    woc = ar.take(C)
    cols = ar.take(16)
    na = ar.take(NT, N_STATE)
    sel32 = ar.take(NT * N_STATE * 128 // 2)
    sel = sel32.bitcast(BF16).rearrange("p (a c) -> p a c", a=NT * N_STATE)
    bc3 = ar.take_bf16(2, HW)
    hs = ar.take(N_STATE)
    z = ar.take(HW)
    dx = ar.take(HW)
    ring_at = ar.at
    bias_s = ar.take(8)

    loaded = sem("l2_weights")
    selc = sem("l2_selector_ready")
    bcs = sem("l2_bc_sum")
    bch = sem("l2_bc_parts")
    bcv = sem("l2_bc_chain")
    moved = sem("l2_bc_moved")
    prep = sem("l2_prepared")

    scratch = Arena(ar.mem, at + 2 * HW)
    scratch.at = at
    parts = scratch.take_bf16(3, HW)
    full = scratch.take(512)
    scratch = Arena(ar.mem, ring_at)
    scratch.at = ring_at - 2 * HW
    stage = scratch.take(NT * N_STATE * 128)
    with nc.Block() as block:
        @block.sync
        def _(sp):
            for dst, name in ((wa, "w2a"), (wc, "w2c"), (woa, "wo2a"), (woc, "wo2c"), (cols[:, 0:15], "cols2"),
                              (na, "alog2"), (stage[0:96], "sel2"), (bias_s[0:64, 0:1], "bcbias2")):
                sp.dma_start(dst, inp[name]).then_inc(loaded, 16)
            sp.wait_ge(bcv, 5 * 8)
            for part in range(3):
                for x in range(2):
                    sp.dma_start(bc3[32 * part:32 * part + 32, x, :], parts[32 * x:32 * x + 32, part, :]).then_inc(moved, 16)
            sp.wait_ge(moved, 96)

        @block.tensor
        def _(pe):
            pe.wait_ge(loaded, 128)
            for k in range(8):
                if k >= 2:
                    pe.wait_ge(bch, k - 1)
                for x in range(2):
                    o0 = 2 * C + 64 * x
                    for b in range(B):
                        nc.tensor.matmul(ps[32 * x:32 * x + 32, k % 2, :], wa[:, o0 + 32 * b:o0 + 32 * b + 32],
                                         xn[:, b, 512 * k:512 * k + 512], start=(b == 0), stop=False)
                    ins = nc.tensor.matmul(ps[32 * x:32 * x + 32, k % 2, :], wc[:, o0:o0 + 32],
                                           xn[:, 2, 512 * k:512 * k + 512], start=False, stop=True)
                ins.then_inc(bcs, 1)

        @block.scalar
        def _(act):
            act.wait_ge(loaded, 128)
            nc.scalar.activation(na, na, ACT.Exp).then_inc(prep, 1)
            nc.scalar.copy(sel32.bitcast(BF16)[0:96], stage[0:96]).then_inc(selc, 1)

        @block.vector
        def _(dve):
            V = nc.vector
            dve.wait_ge(loaded, 128)
            dve.wait_ge(prep, 1)
            V.tensor_scalar(na, na, -1.0, None, ALU.mult).then_inc(prep, 1)
            for t in range(NT):
                V.tensor_tensor(cols[:, 5 * t + 1:5 * t + 2], cols[:, 5 * t + 1:5 * t + 2], cols[:, 5 * t + 2:5 * t + 3], ALU.add).then_inc(prep, 1)
            n = 0
            for k in range(8):
                s = slice(512 * k, 512 * k + 512)
                dve.wait_ge(bcs, k + 1)
                if k:
                    dve.wait_ge(bcv, 5 * k)
                V.tensor_scalar(full[0:64], ps[0:64, k % 2, :], bias_s[0:64, 0:1], None, ALU.add).then_inc(bch, 1)
                dve.wait_ge(bch, k + 1)
                for part in range(3):
                    if part:
                        dve.wait_ge(bcv, n)
                        V.tensor_tensor(full[0:64], full[0:64], parts[0:64, part - 1, s], ALU.subtract).then_inc(bcv, 1)
                        n += 1
                        dve.wait_ge(bcv, n)
                    V.tensor_copy(parts[0:64, part, s], full[0:64]).then_inc(bcv, 1)
                    n += 1

    ar.at = ring_at
    da = ar.take(2, CH)
    dbx = ar.take(2, CH)
    hh = ar.take(2, CH)
    hc = ar.take(2, CH)
    l2_sems = [sem(n) for n in ("l2_proj_sum", "l2_xin_out", "l2_delta_out", "l2_vector_chain", "l2_scalar_chain", "l2_b_broadcast", "l2_c_broadcast", "l2_decay", "l2_input", "l2_scan", "l2_h_times_c", "l2_y_accumulated", "l2_state_carried", "l2_y_added")]
    for t in range(NT):
        layer2_tile(nc, l2_sems, ps, t, xn, y, wa, wc, cols, na, sel, bc3, hs, z, dx, da, dbx, hh, hc, ident)

    ar.at = ring_at
    xr = ar.take(2, 2048)

    def lin(out, t, n0):
        return linear(nc, out, woa, woc, 0, t, y, n0, 512)

    bo = cols[:, 0:15].rearrange("p (t k) -> p t k", t=NT)[:, :, 4]
    residual_block(nc, sem, ps, "l2", x2, x3, xr, lin, bias=bo)


def layer2_tile(nc, sems, ps, t, xn, y, wa, wc, cols, na, sel, bc3, hs, z, dx, da, dbx, hh, hc, ident):
    NC = HW // 512
    psum_in, x_out, d_out, vch, ach = sems[0:5]
    bsum, csum, exp_done, dbx_done, scan_done, hc_done, ysum, carried, yadd = sems[5:]
    m0, j0 = N_STATE * (HW // CH) * t, (HW // CH) * t
    lg = [(da.rearrange("p a b -> p (a b)"), 0), (dbx.rearrange("p a b -> p (a b)"), 2 * CH)]

    with nc.Block() as block:
        @block.tensor
        def _(pe):
            for k in range(NC):
                for x in range(2):
                    if k >= 4:
                        pe.wait_ge(x_out if x == 0 else d_out, NC * t + k - 3)
                    linear(nc, ps[:, 2 * (k % 4) + x, :], wa, wc, C * x, t, xn, 512 * k, 512).then_inc(psum_in, 1)

        @block.scalar
        def _(act):
            for k in range(NC):
                s = slice(512 * k, 512 * k + 512)
                act.wait_ge(psum_in, 2 * NC * t + 2 * k + 2)
                nc.scalar.activation(z[:, s], ps[:, 2 * (k % 4) + 1, :], ACT.Identity, bias=cols[:, 5 * t + 1:5 * t + 2]
                                     ).then_inc(d_out, 1)
            act.wait_ge(d_out, NC * (t + 1))
            n = 6 * t
            for func, kw in ((ACT.Abs, {}), (ACT.Exp, dict(scale=-1.0)), (ACT.Ln, dict(bias=1.0))):
                for buf, c0 in lg:
                    src = z[:, c0:c0 + 2 * CH] if func == ACT.Abs else buf
                    if func != ACT.Abs:
                        act.wait_ge(ach, n - 1)
                    nc.scalar.activation(buf, src, func, **kw).then_inc(ach, 1)
                    n += 1

        @block.vector
        def _(dve):
            V = nc.vector
            for k in range(NC):
                s = slice(512 * k, 512 * k + 512)
                dve.wait_ge(psum_in, 2 * NC * t + 2 * k + 1)
                V.tensor_scalar(y[:, t, s], ps[:, 2 * (k % 4), :], cols[:, 5 * t:5 * t + 1], None, ALU.add).then_inc(x_out, 1)
            n = 6 * t
            for i, (buf, c0) in enumerate(lg):
                s = slice(c0, c0 + 2 * CH)
                dve.wait_ge(ach, 6 * t + 5 + i)
                V.scalar_tensor_tensor(out=z[:, s], in0=z[:, s], scalar=0.0, in1=buf, op0=ALU.max, op1=ALU.add).then_inc(vch, 1)
                n += 1
                dve.wait_ge(vch, n)
                dve.wait_ge(x_out, NC * (t + 1))
                V.tensor_tensor(dx[:, s], z[:, s], y[:, t, s], ALU.mult).then_inc(vch, 1)
                n += 1
                dve.wait_ge(vch, n)
                V.tensor_scalar(y[:, t, s], y[:, t, s], cols[:, 5 * t + 3:5 * t + 4], None, ALU.mult).then_inc(vch, 1)
                n += 1
            V.memset(hs, 0.0)

    N = N_STATE
    pb = [ps[:, 0:2, :], ps[:, 2:4, :]]
    pc = ps[:, 4:6, :]
    py = ps[:, 6:8, :]

    def halves(v):
        return v.rearrange("p (a c) -> p a c", a=2)

    with nc.Block() as block:
        @block.tensor
        def _(pe):
            def b_bcast(j, n):
                m = m0 + N * j + n
                pe.wait_ge(dbx_done, m + 1)
                for a in range(2):
                    ins = nc.tensor.matmul(pb[n % 2][:, a, :], sel[0:96, N * t + n, :], bc3[0:96, 0, bass.ds(j * CH + 512 * a, 512)],
                                           start=True, stop=True)
                ins.then_inc(bsum, 1)

            def c_bcast(j, n):
                pe.wait_ge(hc_done, m0 + N * j + n + 2)
                for a in range(2):
                    ins = nc.tensor.matmul(pc[:, a, :], sel[0:96, N * t + n, :], bc3[0:96, 1, bass.ds(j * CH + 512 * a, 512)],
                                           start=True, stop=True)
                ins.then_inc(csum, 1)

            def accumulate(j, n):
                pe.wait_ge(hc_done, m0 + N * j + n + 3)
                if n == 0:
                    pe.wait_ge(yadd, j0 + j + 1)
                for a in range(2):
                    ins = nc.tensor.matmul(py[:, a, :], ident, hc[:, n % 2, 512 * a:512 * a + 512], start=(n == 0), stop=(n == N - 1))
                ins.then_inc(ysum, 1)

            with pe.Fori(0, HW // CH) as j:
                b_bcast(j, 0)
                for n in range(N):
                    if n + 1 < N:
                        b_bcast(j, n + 1)
                    c_bcast(j, n)
                    if n:
                        accumulate(j, n - 1)
                accumulate(j, N - 1)

        @block.scalar
        def _(act):
            with act.Fori(0, HW // CH) as j:
                for n in range(N):
                    m = m0 + N * j + n
                    act.wait_ge(scan_done, m + 1)
                    act.nop(nofuse=True)
                    nc.scalar.activation(da[:, n % 2, :], z[:, bass.ds(j * CH, CH)], ACT.Exp, scale=na[:, t, n:n + 1]
                                         ).then_inc(exp_done, 1)
                    if n >= 1:
                        act.wait_ge(scan_done, m + 2)
                        nc.scalar.copy(hs[:, n - 1:n], hh[:, (n - 1) % 2, CH - 1:CH]).then_inc(carried, 1)
                act.wait_ge(scan_done, m0 + N * j + N + 2)
                nc.scalar.copy(hs[:, N - 1:N], hh[:, (N - 1) % 2, CH - 1:CH]).then_inc(carried, 1)

        @block.vector
        def _(dve):
            V = nc.vector
            if t == 0:
                for s in (dbx_done, scan_done, hc_done, carried, ysum):
                    dve.sem_inc(s, 2)
                dve.sem_inc(yadd, 1)

            def product(j, n):
                m = m0 + N * j + n
                dve.wait_ge(bsum, m + 1)
                dve.wait_ge(scan_done, m + 1)
                V.tensor_tensor(halves(dbx[:, n % 2, :]), pb[n % 2], halves(dx[:, bass.ds(j * CH, CH)]), ALU.mult).then_inc(dbx_done, 1)

            def scan(j, n):
                m = m0 + N * j + n
                dve.wait_ge(dbx_done, m + 3)
                dve.wait_ge(exp_done, m + 1)
                dve.wait_ge(hc_done, m + 1)
                dve.wait_ge(carried, m + 1)
                V.tensor_tensor_scan(hh[:, n % 2, :], da[:, n % 2, :], dbx[:, n % 2, :], hs[:, n:n + 1],
                                     ALU.mult, ALU.add).then_inc(scan_done, 1)

            def times_c(j, n):
                m = m0 + N * j + n
                dve.wait_ge(csum, m + 1)
                dve.wait_ge(scan_done, m + 3)
                dve.wait_ge(ysum, m + 1)
                V.tensor_tensor(halves(hc[:, n % 2, :]), halves(hh[:, n % 2, :]), pc, ALU.mult).then_inc(hc_done, 1)

            with dve.Fori(0, HW // CH) as j:
                product(j, 0)
                for n in range(N):
                    if n + 1 < N:
                        product(j, n + 1)
                    scan(j, n)
                    times_c(j, n)
                dve.wait_ge(ysum, m0 + N * j + N + 2)
                V.tensor_tensor(halves(y[:, t, bass.ds(j * CH, CH)]), py, halves(y[:, t, bass.ds(j * CH, CH)]), ALU.add).then_inc(yadd, 1)


def layer3(nc, sem, ar, ps, inp, x3, xout, ident):
    xt = ar.take(NT, HW)
    pad = ar.take(NT * 4900)
    at = ar.at
    group_norm(nc, sem, ar, ps, inp, x3, 3, ident, xt=xt, padded=pad)
    ar.at = at
    wts = ar.take(NT, 49)
    bias = ar.take(NT)
    diag = ar.take(2 * 49, 128)
    loaded = sem("l3_weights")
    chain = sem("l3_mirror_chain")
    diag_ready = sem("l3_diagonals")
    psum_done = sem("l3_sum_in_psum")
    added = sem("l3_added")
    biased = sem("l3_biased")
    taps = sem("l3_taps")
    stored = sem("l3_stored")
    VP = ROWS_V * W
    NCH = (H - ROWS_V) // R

    def img(t):
        return pad[:, t * 4900:(t + 1) * 4900].rearrange("p (r w) -> p r w", r=70)

    with nc.Block() as block:
        @block.sync
        def _(sp):
            sp.dma_start(wts, inp["w3"]).then_inc(loaded, 16)
            sp.dma_start(bias, inp["b3"]).then_inc(loaded, 16)
            n = 0
            for t in range(NT):
                sp.wait_ge(added, NCH * (t + 1))
                for p0, b, c0, m in pieces(t):
                    sp.dma_start(xout[b, c0:c0 + m, VP:HW], xt[p0:p0 + m, t, VP:HW]).then_inc(stored, 16)
                    n += 1
            sp.wait_ge(taps, NT * 49)
            for t in range(NT):
                for p0, b, c0, m in pieces(t):
                    sp.dma_start(xout[b, c0:c0 + m, 0:VP], xt[p0:p0 + m, t, 0:VP]).then_inc(stored, 16)
                    n += 1
            sp.wait_ge(stored, 16 * n)

        @block.gpsimd
        def _(pool):
            pool.wait_ge(loaded, 32)
            for t in range(NT):
                if t >= 2:
                    pool.wait_ge(psum_done, NCH * (t - 1))
                nc.gpsimd.tensor_tensor(diag[:, 49 * (t % 2):49 * (t % 2) + 49, :],
                                        ident.unsqueeze(1).to_broadcast([128, 49, 128]),
                                        wts[:, t, :].unsqueeze(2).to_broadcast([128, 49, 128]), ALU.mult).then_inc(diag_ready, 1)

        @block.scalar
        def _(act):
            act.wait_ge(loaded, 32)
            for t in range(NT):
                nc.scalar.activation(xt[:, t, :], xt[:, t, :], ACT.Identity, bias=bias[:, t:t + 1]).then_inc(biased, 1)

        @block.tensor
        def _(pe):
            pe.wait_ge(chain, 12 * NT)
            for m in range(NT * NCH):
                t, k = m // NCH, m % NCH
                pe.wait_ge(diag_ready, t + 1)
                if m >= 8:
                    pe.wait_ge(added, m - 7)
                r0 = ROWS_V + R * k
                for a in range(49):
                    ins = nc.tensor.matmul(ps[:, m % 8, :].rearrange("p (r w) -> p r w", r=R), diag[:, 49 * (t % 2) + a, :],
                                           img(t)[:, r0 + a // 7:r0 + a // 7 + R, a % 7:a % 7 + W], start=(a == 0), stop=(a == 48))
                ins.then_inc(psum_done, 1)

        @block.vector
        def _(dve):
            V = nc.vector
            n = 0
            for t in range(NT):
                for i in range(3):
                    V.tensor_copy(img(t)[:, 3:67, i], img(t)[:, 3:67, 6 - i]).then_inc(chain, 1)
                    V.tensor_copy(img(t)[:, 3:67, 69 - i], img(t)[:, 3:67, 63 + i]).then_inc(chain, 1)
                    n += 2
                dve.wait_ge(chain, n)
                for i in range(3):
                    V.tensor_copy(img(t)[:, i, :], img(t)[:, 6 - i, :]).then_inc(chain, 1)
                    V.tensor_copy(img(t)[:, 69 - i, :], img(t)[:, 63 + i, :]).then_inc(chain, 1)
                    n += 2
                dve.wait_ge(chain, n)
            dve.wait_ge(biased, NT)
            m = 0
            for a in range(49):
                for t in range(NT):
                    o = xt[:, t, 0:VP].rearrange("p (r w) -> p r w", w=W)
                    if a:
                        dve.wait_ge(taps, NT * (a - 1) + t + 1)
                    V.scalar_tensor_tensor(out=o, in0=img(t)[:, a // 7:a // 7 + ROWS_V, a % 7:a % 7 + W], scalar=wts[:, t, a:a + 1],
                                           in1=o, op0=ALU.mult, op1=ALU.add).then_inc(taps, 1)
                if a % 5 == 4 and m < NT * NCH:
                    tail_add(nc, dve, ps, xt, m, NCH, VP, psum_done, added)
                    m += 1
            while m < NT * NCH:
                tail_add(nc, dve, ps, xt, m, NCH, VP, psum_done, added)
                m += 1


def tail_add(nc, dve, ps, xt, m, NCH, VP, psum_done, added):
    t, k = m // NCH, m % NCH
    x = xt[:, t, VP + k * PX:VP + (k + 1) * PX]
    dve.wait_ge(psum_done, m + 1)
    nc.vector.tensor_tensor(x, ps[:, m % 8, :], x, ALU.add).then_inc(added, 1)


def layouts(v):
    import numpy as np
    f = np.float32
    o = {"x": v["x"], "ident": np.eye(128, dtype=f)}

    def packed_rows(w):
        return w[0:128], np.concatenate([w[128:192], w[128:192]], 0)

    def packed_vec(w):
        return np.stack([w[0:128], w[0:128], np.concatenate([w[128:192], w[128:192]], 0)], 1)

    g = np.kron(np.eye(32), np.full((6, 6), 1.0 / 6.0)).astype(f)
    o["gmat"] = np.concatenate(packed_rows(g), 1)

    wq = v["L0_conv_w_qkv"].T
    cols = [wq[:, 128 * t:128 * t + 128] for t in range(NTT)]
    for k in range(NG):
        c = wq[:, 384 + CG * k:384 + CG * k + CG]
        cols += [c, c]
    o["wbase"] = np.concatenate(cols, 1).reshape(2, HC, 768).transpose(1, 0, 2)
    dws = [v["L0_conv_w_dw3"][:, 0], v["L0_conv_w_dw5"][:, 0], v["L0_conv_w_dw7"][:, 0]]
    flat = np.concatenate([d.reshape(QKV, -1) for d in dws], 1)
    o["wt"] = flat[0:384].reshape(NTT, 128, NTAP).transpose(1, 0, 2).reshape(128, NTT * NTAP)
    wg3 = np.zeros((2, CG, NG, 3, 2), f)
    wd = np.zeros((2, CG, NG, 7, 4, 2), f)
    for k in range(NG):
        ch = slice(384 + CG * k, 384 + CG * k + CG)
        wg3[0, :, k, :, 0] = dws[0][ch, :, 0]
        wg3[1, :, k, :, 0] = dws[0][ch, :, 1]
        wg3[0, :, k, :, 1] = dws[0][ch, :, 2]
        for s in range(2):
            for j in range(4):
                dx = -3 + 2 * j + s
                if dx <= 3:
                    wd[s, :, k, :, j, 0] = dws[2][ch, :, dx + 3]
                if -2 <= dx <= 2:
                    wd[s, :, k, 1:6, j, 1] = dws[1][ch, :, dx + 2]
    o["wg3"] = wg3.reshape(128, NG * TSL)
    o["wd"] = wd.reshape(128, NG * SLOTS, 2)
    o["mask2"] = np.concatenate([np.eye(CG, dtype=f)] * 2, 0)
    pT = v["L0_conv_w_pconv"].T
    tiles = [pT[k * QKV + 128 * t:k * QKV + 128 * t + 128] for t in range(NTT) for k in range(3)]
    for k in range(NG):
        c = 384 + CG * k
        tiles.append(np.concatenate([pT[2 * QKV + c:2 * QKV + c + CG], pT[QKV + c:QKV + c + CG]], 0))
    for k in range(NG):
        c = 384 + CG * k
        tiles.append(np.concatenate([pT[c:c + CG]] * 2, 0))
    o["pw"] = np.stack(tiles, 1)
    o["wproj0"] = v["L0_conv_w_proj"].T.reshape(2, HC, C).transpose(1, 0, 2)
    o["head_mask"] = np.kron(np.eye(HH), np.ones((HD, 1))).astype(f)
    o["temperature_rows"] = np.repeat(v["L0_conv_temperature"].reshape(2, HH), HD, 1).T
    o["scales_rows"] = np.broadcast_to(v["L0_conv_attn_scales"], (HC, 3))
    o["tri"] = np.broadcast_to(np.tril(np.ones((HD, HD), f), -1), (HC, HD, HD))

    w1 = v["L1_conv_w_qkv"]
    o["w1qk"] = w1[0:2 * C].T
    o["w1v"] = w1[2 * C:].reshape(2, HC, C).transpose(1, 0, 2)

    w2 = v["L2_conv_W_proj"].T
    z = np.zeros((C, N_STATE), f)
    bm, cm = w2[:, 2 * C:2 * C + N_STATE], w2[:, 2 * C + N_STATE:]
    w2p = np.concatenate([w2[:, 0:2 * C], bm, z, z, bm, cm, z, z, cm], 1)
    o["w2a"], o["w2c"] = packed_rows(w2p)
    for n, m in enumerate((bm, cm)):
        c0 = 2 * C + 64 * n
        o["w2c"][:, c0:c0 + 64] = 0
        o["w2c"][0:64, c0:c0 + N_STATE] = m[128:192]
        o["w2c"][64:128, c0 + N_STATE:c0 + 2 * N_STATE] = m[128:192]
    o["wo2a"], o["wo2c"] = packed_rows(v["L2_conv_W_out"].T)
    bp = v["L2_conv_b_proj"]
    five = np.stack([bp[0:C], bp[C:2 * C], v["L2_conv_dt_bias"], v["L2_conv_D"], v["L2_conv_b_out"]], 1)
    o["cols2"] = packed_vec(five).reshape(128, 15)
    bb, cb = bp[2 * C:2 * C + N_STATE], bp[2 * C + N_STATE:]
    o["bcbias2"] = np.concatenate([bb, bb, cb, cb]).reshape(64, 1)
    o["alog2"] = packed_vec(v["L2_conv_A_log"])
    sel = np.zeros((3, 32, NT, N_STATE, 128), f)
    for n in range(N_STATE):
        sel[:, n, 0, n, :] = 1
        sel[:, 16 + n, 1, n, :] = 1
        sel[:, n, 2, n, 0:64] = 1
        sel[:, 16 + n, 2, n, 64:128] = 1
    o["sel2"] = sel.reshape(96, NT * N_STATE * 128)
    o["w3"] = packed_vec(v["L3_conv_w"].reshape(C, 49))
    o["b3"] = packed_vec(v["L3_conv_b"])
    return o


def kernel(**inputs):
    import numpy as np
    import concourse.bacc as bacc
    from concourse.bass_utils import run_bass_kernel_spmd

    nc = bacc.Bacc("TRN2", target_bir_lowering=False, num_devices=1)
    arrays, aps = {}, {}
    for name, a in layouts({k: np.asarray(a) for k, a in inputs.items()}).items():
        a = np.ascontiguousarray(a)
        arrays[f"in_{name}"] = a
        aps[name] = nc.dram_tensor(f"in_{name}", a.shape, mybir.dt.from_np(a.dtype), kind="ExternalInput").ap()
    res = nc.dram_tensor("out_0", (B, C, H, W), F32, kind="ExternalOutput").ap()
    build(nc, aps, res)
    r = run_bass_kernel_spmd(nc, [arrays], core_ids=[0])
    return r.results[0]["out_0"]
```

```python
import concourse.bass as bass
from concourse import mybir
from contextlib import ExitStack

F32 = mybir.dt.float32
BF16 = mybir.dt.bfloat16
F16 = mybir.dt.float16
ALU = mybir.AluOpType
ACT = mybir.ActivationFunctionType
AX = mybir.AxisListType.X

B, C, H, W = 2, 192, 64, 64
HW = H * W
HC = C // 2
QKV = 3 * C
HEADS, HD = 8, 24
HH = HC // HD
EPS_GN = 1e-5
BH = 2 * B

NT = 3

NTT, TCH = 2, 256
CG = 16
NSH = 128 // CG
P_GROUPS = [8, 8, 4]
G0 = [0, 8, 16]
NG = sum(P_GROUPS)
MG = 6 * CG
R = 8
NS = H // R
RB = R + 6
PADW = W + 6
PW2 = PADW // 2
PX = R * W
GW = (RB - 1) * PW2 + W // 2
KS = [3, 5, 7]
TAPS = [k * k for k in KS]
NTAP = sum(TAPS)
KT = 14
OPS = NTT * NTAP

N_STATE = 16
CH = 1024
ROWS_V = 40


def depthwise_plan():
    def chain(src, ktile, taps):
        return [(src, ktile, n == 0, dy, dx, w) for n, (dy, dx, w) in enumerate(taps)]

    def tile(t):
        cs, w0 = [], 0
        for k in range(3):
            s, p = KS[k], KS[k] // 2
            cs.append(chain(("T", t), 3 * t + k,
                            [(3 - p + a, 3 - p + b, t * NTAP + w0 + a * s + b) for a in range(s) for b in range(s)]))
            w0 += TAPS[k]
        return cs[0] + cs[1], cs[2]

    def merge(a, b):
        out = []
        for n in range(max(len(a), len(b))):
            out += a[n:n + 1] + b[n:n + 1]
        return out

    return merge(*tile(0)) + merge(*tile(1))


PLAN = depthwise_plan()
LAST = {}
PREV = []
for _n, _o in enumerate(PLAN):
    PREV.append(LAST.get(_o[1], 0))
    LAST[_o[1]] = _n + 1
SRC_LAST = {}
for _n, _o in enumerate(PLAN):
    SRC_LAST[_o[0]] = _n + 1


class Arena:

    def __init__(self, mem, size):
        self.mem, self.size, self.at = mem, size, 0

    def take(self, *dims):
        n = 1
        for d in dims:
            n *= d
        v = self.mem[:, self.at:self.at + n]
        self.at += n
        assert self.at <= self.size, (self.at, self.size)
        if len(dims) == 2:
            v = v.rearrange("p (a b) -> p a b", a=dims[0])
        if len(dims) == 3:
            v = v.rearrange("p (a b c) -> p a b c", a=dims[0], b=dims[1])
        return v

    def take16(self, *dims, dt=BF16):
        n = 1
        for d in dims:
            n *= d
        v = self.mem[:, self.at:self.at + n // 2].bitcast(dt)
        self.at += n // 2
        assert self.at <= self.size
        if len(dims) == 2:
            v = v.rearrange("p (a b) -> p a b", a=dims[0])
        if len(dims) == 3:
            v = v.rearrange("p (a b c) -> p a b c", a=dims[0], b=dims[1])
        return v


def pieces(t):
    if t < 2:
        return [(0, t, 0, 128)]
    return [(0, 0, 128, 64), (64, 1, 128, 64)]


def linear(nc, out, wa, wc, o0, t, src, n0, n):
    last = None
    if t < 2:
        lo = 64 * t
        nc.tensor.matmul(out, wa[:, o0:o0 + 128], src[:, t, n0:n0 + n], start=True, stop=False)
        return nc.tensor.matmul(out, wc[lo:lo + 64, o0:o0 + 128], src[lo:lo + 64, 2, n0:n0 + n], start=False, stop=True)
    for b in range(B):
        lo = 64 * b
        nc.tensor.matmul(out[lo:lo + 64], wa[:, o0 + 128:o0 + 192], src[:, b, n0:n0 + n], start=True, stop=False)
        last = nc.tensor.matmul(out[lo:lo + 64], wc[lo:lo + 64, o0 + 128:o0 + 192], src[lo:lo + 64, 2, n0:n0 + n],
                                start=False, stop=True)
    return last


def build(nc, inp, out):
    with ExitStack() as ctx:
        SIZE = 53100
        mem = ctx.enter_context(nc.sbuf_tensor("mem", [128, SIZE], F32))
        ps = ctx.enter_context(nc.psum_tensor("ps", [128, 8, 512], F32))
        n_sem = [0]

        def sem(name):
            n_sem[0] += 1
            return ctx.enter_context(nc.semaphore(f"{name}_{n_sem[0]}"))

        sem.norm = ([sem("norm_x_loaded") for _ in range(NT)], sem("norm_consts"), sem("norm_moments"),
                    sem("norm_vector_chain"), sem("norm_averaged"), sem("norm_rooted"), sem("norm_var_ready"),
                    [sem("norm_tile_done") for _ in range(NT)])

        def dram(name, shape):
            return nc.dram_tensor(name, shape, F32).ap()

        base_t = dram("base_T", [B, TCH, H + 6, PADW])
        base_p = nc.dram_tensor("base_P", [B, QKV - TCH, 4, (H + 6) * PW2], F16).ap()
        x2 = dram("x_after_1", [B, C, HW])
        xin = inp["x"].rearrange("b c h w -> b c (h w)")
        xout = out.rearrange("b c h w -> b c (h w)")

        ar = Arena(mem, SIZE)
        ident = ar.take(128)
        gacc = ar.take(BH, 3 * HC)
        attn_w = ar.take(BH, HC)
        keep = ar.at

        def fresh():
            a = Arena(mem, SIZE)
            a.at = keep
            return a

        layer0_base(nc, sem, fresh(), ps, inp, xin, ident, base_t, base_p)
        v_dram = dram("v_pixels", [B * NS, 128, 4 * C])
        layer0_conv(nc, sem, fresh(), ps, inp, base_t, base_p, gacc, v_dram, dram)
        ar = fresh()
        xt = ar.take(NT, HW)
        keep = ar.at
        layer0_attention(nc, sem, fresh(), ps, inp, v_dram, ident, gacc, attn_w, xin, xt)
        layer1(nc, sem, fresh(), ps, inp, xt, x2, ident, gacc, attn_w)
        layer2(nc, sem, fresh(), ps, inp, xt, x2, ident)
        layer3(nc, sem, fresh(), ps, inp, xt, xout, ident)


def group_norm(nc, sem, ar, ps, inp, layer, ident, xt, x_dram=None, padded=None, dst=None):
    gm = ar.take(2 * 192)
    stats = ar.take(NT * 8, 6)
    mv = ar.take(NT, 2)
    sq = ar.take(NT, 1)
    gst = ar.take(NT, 2)
    var = ar.take(NT)
    msq = ar.take(NT)
    sd = ar.take(NT)
    rs = ar.take(NT)
    t1 = ar.take(NT)
    nb = ar.take(NT)
    (loaded, consts, stat_done, chain, averaged, rooted, ready, normed) = sem.norm
    steps = NT * 8 + NT + 1 + 4 + 7
    L = layer

    def dest(t):
        if padded is None:
            return (xt if dst is None else dst)[:, t, :]
        return padded[:, t * 4900:(t + 1) * 4900].rearrange("p (r w) -> p r w", r=70)[:, 3:67, 3:67]

    def source(t):
        if padded is None:
            return xt[:, t, :]
        return xt[:, t, :].rearrange("p (r w) -> p r w", r=H)

    with nc.Block() as block:
        @block.sync
        def _(sp):
            if x_dram is not None:
                for t in range(NT):
                    for p0, b, c0, n in pieces(t):
                        sp.dma_start(xt[p0:p0 + n, t, :], x_dram[b, c0:c0 + n, :]).then_inc(loaded[t], 16)
            sp.dma_start(ident, inp["ident"]).then_inc(consts, 16)
            sp.dma_start(gm, inp["gmat"]).then_inc(consts, 16)
        @block.vector
        def _(dve):
            n = [steps * L]

            def step(ins):
                ins.then_inc(chain, 1)
                n[0] += 1
                dve.wait_ge(chain, n[0])

            for t in range(NT):
                if x_dram is not None:
                    dve.wait_ge(loaded[t], 16 * len(pieces(t)))
                for k in range(8):
                    last = nc.vector.bn_stats(stats[:, t * 8 + k, :], xt[:, t, 512 * k:512 * k + 512])
                    last.then_inc(chain, 1)
                    n[0] += 1
            dve.wait_ge(chain, n[0])
            for t in range(NT):
                ins = nc.vector.bn_aggr(mv[:, t, :], stats[:, t * 8:t * 8 + 8, :].rearrange("p a b -> p (a b)"))
                ins.then_inc(chain, 1)
                n[0] += 1
            dve.wait_ge(chain, n[0])
            step(nc.vector.tensor_tensor(sq[:, :, 0], mv[:, :, 0], mv[:, :, 0], ALU.mult))
            nc.vector.tensor_tensor(mv[:, :, 1], mv[:, :, 1], sq[:, :, 0], ALU.add).then_inc(stat_done, 1)
            dve.wait_ge(averaged, L + 1)
            step(nc.vector.tensor_copy(gst, ps[:, 0:NT, 0:2]))
            step(nc.vector.tensor_tensor(msq, gst[:, :, 0], gst[:, :, 0], ALU.mult))
            step(nc.vector.tensor_tensor(var, gst[:, :, 1], msq, ALU.subtract))
            step(nc.vector.tensor_scalar(var, var, EPS_GN, None, ALU.add))
            nc.vector.tensor_copy(t1, var).then_inc(ready, 1)
            dve.wait_ge(rooted, L + 1)
            step(nc.vector.reciprocal(rs, sd))
            step(nc.vector.tensor_tensor(sd, rs, rs, ALU.mult))
            step(nc.vector.tensor_tensor(sd, sd, var, ALU.mult))
            step(nc.vector.tensor_scalar(sd, sd, -0.5, 1.5, ALU.mult, ALU.add))
            step(nc.vector.tensor_tensor(rs, rs, sd, ALU.mult))
            step(nc.vector.tensor_tensor(nb, gst[:, :, 0], rs, ALU.mult))
            step(nc.vector.tensor_scalar(nb, nb, -1.0, None, ALU.mult))
            nc.vector.tensor_scalar(dest(0), source(0), rs[:, 0:1], nb[:, 0:1], ALU.mult, ALU.add).then_inc(normed[0], 1)
            nc.vector.tensor_scalar(dest(1), source(1), rs[:, 1:2], nb[:, 1:2], ALU.mult, ALU.add).then_inc(normed[1], 1)

        @block.tensor
        def _(pe):
            pe.wait_ge(consts, 32 * (L + 1))
            pe.wait_ge(stat_done, L + 1)
            for t in range(NT):
                last = linear(nc, ps[:, t, 0:2], gm[:, 0:192], gm[:, 192:384], 0, t, mv, 0, 2)
            last.then_inc(averaged, 1)

        @block.scalar
        def _(act):
            act.wait_ge(ready, L + 1)
            nc.scalar.activation(sd, var, ACT.Sqrt).then_inc(rooted, 1)
            act.wait_ge(chain, steps * (L + 1))
            nc.scalar.activation(dest(2), source(2), ACT.Identity, bias=nb[:, 2:3],
                                 scale=rs[:, 2:3]).then_inc(normed[2], 1)


def layer0_base(nc, sem, ar, ps, inp, xin, ident, base_t, base_p):
    xn = ar.take(NT, HW)
    at = ar.at
    group_norm(nc, sem, ar, ps, inp, 0, ident, xn, x_dram=xin)
    ar.at = at
    NM = 5
    w = ar.take(3, QKV)
    st = ar.take(NM, R * PADW)
    zero = ar.take(3 * PADW)
    loaded = sem("base_weights")
    cleared = sem("base_borders_cleared")
    summed = [sem("base_in_psum") for _ in range(NM)]
    copied = [sem("base_in_sbuf") for _ in range(NM)]
    stored = [sem("base_stored") for _ in range(NM)]
    high_out = [sem("base_high_part") for _ in range(3)]
    z_stored = sem("base_zero_rows_stored")

    def width(m):
        return 64 if m == 4 else 128

    def parts(m):
        return st[0:width(m), m, :].bitcast(F16).rearrange("p (a r n) -> p a r n", a=4, r=R)

    def columns(m, par, a):
        n0 = 2 if par == 0 else 1
        x = ps[0:width(m), m, :].rearrange("p (r n a) -> p a r n", r=R, a=2)
        return parts(m)[:, 2 * a + par, :, n0:n0 + W // 2], x[:, 1 - par]

    with nc.Block() as block:
        @block.sync
        def _(sp):
            sp.dma_start(w, inp["wbase"]).then_inc(loaded, 16)
            sp.wait_ge(cleared, 1)
            n = 0
            for b in range(B):
                for r0 in (0, H + 3):
                    for t in range(2):
                        sp.dma_start(base_t[b, 128 * t:128 * t + 128, r0:r0 + 3, :].rearrange("c r w -> c (r w)"),
                                     zero).then_inc(z_stored, 16)
                        n += 1
                    for k in range(3):
                        m = 16 * P_GROUPS[k]
                        sp.dma_start(base_p[b, 128 * k:128 * k + m, :, r0 * PW2:(r0 + 3) * PW2],
                                     zero.bitcast(F16)[0:m].rearrange("p (a n) -> p a n", a=4)).then_inc(z_stored, 16)
                        n += 1
            for m in range(NM):
                sp.sem_inc(stored[m], 16)
            for b in range(B):
                with sp.Fori(0, NS) as s:
                    for m in range(NM):
                        sp.wait_ge(copied[m], s + NS * b + 2)
                        if m < 2:
                            sp.dma_start(base_t[b, 128 * m:128 * m + 128, bass.ds(3 + s * R, R), :].rearrange("c r w -> c (r w)"),
                                         st[:, m, :]).then_inc(stored[m], 16)
                        else:
                            c0 = 128 * (m - 2)
                            sp.dma_start(base_p[b, c0:c0 + width(m), :, bass.ds((3 + s * R) * PW2, R * PW2)],
                                         parts(m).rearrange("p a r n -> p a (r n)")).then_inc(stored[m], 16)
            for m in range(NM):
                sp.wait_ge(stored[m], 16 * (B * NS + 1))
            sp.wait_ge(z_stored, 16 * n)

        @block.tensor
        def _(pe):
            pe.wait_ge(loaded, 16)
            for b in range(B):
                with pe.Fori(0, NS) as s:
                    for m in range(NM):
                        out = ps[0:width(m), m, :]
                        pe.wait_ge(copied[m], s + NS * b + 1)
                        pe.nop(nofuse=True)
                        nc.tensor.matmul(out, w[:, 0, 128 * m:128 * m + width(m)], xn[:, b, bass.ds(s * PX, PX)], start=True, stop=False)
                        nc.tensor.matmul(out, w[:, 1 + b, 128 * m:128 * m + width(m)], xn[:, 2, bass.ds(s * PX, PX)],
                                         start=False, stop=True).then_inc(summed[m], 1)

        @block.scalar
        def _(act):
            act.wait_ge(cleared, 2)
            for b in range(B):
                with act.Fori(0, NS) as s:
                    i = s + NS * b
                    for m in (2, 3, 4):
                        act.wait_ge(summed[m], i + 1)
                        act.wait_ge(stored[m], 16 * (i + 1))
                        for par in range(2):
                            d, x = columns(m, par, 0)
                            ins = nc.scalar.copy(d, x)
                        ins.then_inc(high_out[m - 2], 1)

        @block.vector
        def _(dve):
            nc.vector.memset(zero, 0.0).then_inc(cleared, 1)
            nc.vector.memset(st, 0.0).then_inc(cleared, 1)
            dve.wait_ge(cleared, 2)
            for m in range(NM):
                dve.sem_inc(copied[m], 1)
            for b in range(B):
                with dve.Fori(0, NS) as s:
                    i = s + NS * b
                    for m in (0, 1):
                        dve.wait_ge(summed[m], i + 1)
                        dve.wait_ge(stored[m], 16 * (i + 1))
                        nc.vector.tensor_copy(st[:, m, :].rearrange("p (r w) -> p r w", r=R)[:, :, 3:3 + W],
                                              ps[:, m, :].rearrange("p (r w) -> p r w", r=R)).then_inc(copied[m], 1)
                    for m in (2, 3, 4):
                        dve.wait_ge(high_out[m - 2], i + 1)
                        for par in range(2):
                            hi, x = columns(m, par, 0)
                            ins = nc.vector.tensor_tensor(columns(m, par, 1)[0], x, hi, ALU.subtract)
                        ins.then_inc(copied[m], 1)


def layer0_conv(nc, sem, ar, ps, inp, base_t, base_p, gacc, v_dram, dram):
    wt = ar.take(NTT * NTAP)
    pw = ar.take(KT, QKV)
    diag = ar.take16(NG * 7, 2, MG, dt=F16)
    mask16 = ar.take(CG)
    gbuf = ar.take16(NG, 2, RB * PW2, dt=F16)
    tbuf = ar.take(NTT, RB * PADW)
    dt_ = ar.take(3 * NTT, PX)
    dp = ar.take(8, PX)
    stg = ar.take(8, PX // 2)
    qk = ar.take(4, 2 * C)
    vst = ar.take(4, C)
    gtmp = ar.take(2, 3 * HC)
    NW = NG * 7 * 6
    dp1 = dp.rearrange("p a b -> p (a b)")
    wd, wd_hi, wd_lo, wd16 = dp1[:, 0:NW], dp1[:, NW:2 * NW], dp1[:, 2 * NW:3 * NW], dp1[:, 3 * NW:3 * NW + NW // 2].bitcast(F16)

    d_dram = [dram(f"depthwise_P{k}", [MG, P_GROUPS[k], PX // 2]) for k in range(3)]

    psa = ps[:, 0:4, :]
    psv = ps[:, 4, 0:256].rearrange("p (a c) -> p a c", a=4)
    psg = [ps[:, 5 + n, :].rearrange("p (g n) -> p g n", g=2) for n in range(2)]
    psk = ps[:, 4, 256:256 + 2 * HC]
    psq = ps[:, 7, :]

    weights = sem("l0_weights_loaded")
    diag_ready = sem("l0_diagonals_ready")
    wd_split = sem("l0_P_weights_split")
    gcleared = sem("l0_gram_cleared")
    t_loaded = [sem("l0_T_loaded") for _ in range(NTT)]
    p_loaded = [sem("l0_P_loaded") for _ in range(3)]
    dw_ops = sem("l0_vector_depthwise_ops")
    t_used = sem("l0_T_results_used")
    gdw_sum = sem("l0_group_in_psum")
    gdw_out = sem("l0_group_in_sbuf")
    d_stored = [sem("l0_P_result_stored") for _ in range(3)]
    d_loaded = [sem("l0_P_result_gathered") for _ in range(3)]
    acc_done = sem("l0_pconv_done")
    qkv_out = sem("l0_qkv_in_sbuf")
    v_stored = sem("l0_v_stored")
    gram_sum = sem("l0_gram_in_psum")
    gram_out = sem("l0_gram_in_sbuf")
    gram_add = sem("l0_gram_added")
    NPAIR = NG // 2
    ND = [1, 1, 3]

    with nc.Block() as block:
        @block.sync
        def _(sp):
            for dst, name in ((wt, "wt"), (wd, "wd"), (mask16, "mask16"), (pw, "pw")):
                sp.dma_start(dst, inp[name]).then_inc(weights, 16)

            def load_t(b, s, t):
                sp.dma_start(tbuf[:, t, :], base_t[b, 128 * t:128 * t + 128, bass.ds(s * R, RB), :].rearrange("c r w -> c (r w)")
                             ).then_inc(t_loaded[t], 16)

            def load_p(b, s, k):
                n = P_GROUPS[k]
                for sh in range(NSH):
                    src = base_p[b, 128 * k:128 * k + CG * n, sh % 2:4:2, bass.ds(s * R * PW2 + sh // 2, GW)]
                    sp.dma_start(gbuf[CG * sh:CG * sh + CG, G0[k]:G0[k] + n, :, 0:GW].rearrange("c g h n -> c (g h) n"),
                                 src.rearrange("(c g) h n -> c (g h) n", g=n)).then_inc(p_loaded[k], 16)

            def exchange(i, k):
                n = P_GROUPS[k]
                sp.wait_ge(gdw_out, NPAIR * i + (G0[k] + n) // 2 + 2)
                sp.nop(nofuse=True)
                sp.wait_ge(d_loaded[k], 16 * ND[k] * (i + 1))
                sp.dma_start(d_dram[k], stg[0:MG, 0:n, :]).then_inc(d_stored[k], 16)
                sp.wait_ge(d_stored[k], 16 * (i + 2))
                src = d_dram[k].rearrange("(q c) g n -> (c g) q n", q=6)
                if k < 2:
                    sp.dma_start(dp[:, 3 * k:3 * k + 3, :].rearrange("p k (a n) -> p (k a) n", a=2), src).then_inc(d_loaded[k], 16)
                else:
                    for q, (slot, p0) in enumerate(((6, 0), (7, 0), (7, 64))):
                        sp.dma_start(dp[p0:p0 + 64, slot, :].rearrange("p (a n) -> p a n", a=2), src[:, 2 * q:2 * q + 2, :]
                                     ).then_inc(d_loaded[k], 16)

            def body(b, s, last):
                i = s + NS * b
                nb, ns = (b, s + 1) if not isinstance(s, int) else (b, s + 1)
                exchange(i, 0)
                if not last:
                    load_p(nb, ns, 0)
                exchange(i, 1)
                if not last:
                    load_p(nb, ns, 1)
                exchange(i, 2)
                if not last:
                    load_p(nb, ns, 2)
                    for t in range(NTT):
                        sp.wait_ge(dw_ops, OPS * (i + 1) + NTAP * (t + 1))
                        load_t(nb, ns, t)
                sp.wait_ge(qkv_out, i + 2)
                sp.dma_start(v_dram[bass.ds(i, 1)].rearrange("o p n -> p (o n)"), vst.rearrange("p a c -> p (a c)")).then_inc(v_stored, 16)

            for k in range(3):
                sp.sem_inc(d_loaded[k], 16 * ND[k])
                sp.sem_inc(d_stored[k], 16)
            sp.sem_inc(v_stored, 16)
            for t in range(NTT):
                load_t(0, 0, t)
            for k in range(3):
                load_p(0, 0, k)
            for b in range(B):
                with sp.Fori(0, NS - 1) as s:
                    body(b, s, False)
                if b + 1 < B:
                    i = NS * (b + 1) - 1
                    for k in range(3):
                        exchange(i, k)
                        load_p(b + 1, 0, k)
                    for t in range(NTT):
                        sp.wait_ge(dw_ops, OPS * (i + 1) + NTAP * (t + 1))
                        load_t(b + 1, 0, t)
                    sp.wait_ge(qkv_out, i + 2)
                    sp.dma_start(v_dram[i], vst.rearrange("p a c -> p (a c)")).then_inc(v_stored, 16)
                else:
                    body(b, NS - 1, True)
            sp.wait_ge(v_stored, 16 * (B * NS + 1))
            for k in range(3):
                sp.wait_ge(d_stored[k], 16 * (B * NS + 1))

        @block.gpsimd
        def _(pool):
            nc.gpsimd.memset(gacc, 0.0).then_inc(gcleared, 1)
            pool.wait_ge(weights, 64)
            pool.wait_ge(wd_split, 3)
            for k in range(3):
                r0, n = 7 * G0[k], 7 * P_GROUPS[k]
                for a, w in enumerate((wd_hi, wd_lo)):
                    nc.gpsimd.tensor_tensor(diag[:, r0:r0 + n, a, :].rearrange("p r (q c) -> p r q c", q=6),
                                            mask16.unsqueeze(1).unsqueeze(1).to_broadcast([128, n, 6, CG]),
                                            w[:, 6 * r0:6 * (r0 + n)].rearrange("p (r q) -> p r q", q=6).unsqueeze(3).to_broadcast([128, n, 6, CG]),
                                            ALU.mult).then_inc(diag_ready, 1)
            pool.wait_ge(gcleared, 1)
            pool.sem_inc(gram_add, 1)
            for b in range(B):
                with pool.Fori(0, NS) as s:
                    i = s + NS * b
                    pool.wait_ge(gram_out, i + 2)
                    nc.gpsimd.tensor_tensor(gacc[0:HC, 2 * b:2 * b + 2, :], gacc[0:HC, 2 * b:2 * b + 2, :],
                                            gtmp[0:HC], ALU.add).then_inc(gram_add, 1)
                    pool.wait_ge(gram_add, i + 2)

        @block.vector
        def _(dve):
            dve.sem_inc(dw_ops, OPS)
            dve.wait_ge(weights, 64)
            nc.vector.tensor_copy(wd16, wd).then_inc(wd_split, 1)
            dve.wait_ge(wd_split, 1)
            nc.vector.tensor_copy(wd_hi, wd16).then_inc(wd_split, 1)
            dve.wait_ge(wd_split, 2)
            nc.vector.tensor_tensor(wd_lo, wd, wd_hi, ALU.subtract).then_inc(wd_split, 1)
            with dve.Fori(0, B * NS) as i:
                for n, (src, ktile, first, r0, c0, w) in enumerate(PLAN):
                    t = src[1]
                    if n == NTAP * t:
                        dve.wait_ge(t_loaded[t], 16 * (i + 1))
                        dve.wait_ge(t_used, 2 * i + t + 1)
                    x = tbuf[:, t, :].rearrange("p (r w) -> p r w", r=RB)[:, r0:r0 + R, c0:c0 + W]
                    o = dt_[:, ktile, :].rearrange("p (r w) -> p r w", r=R)
                    if first:
                        ins = nc.vector.tensor_scalar(o, x, wt[:, w:w + 1], None, ALU.mult)
                    else:
                        dve.wait_ge(dw_ops, OPS * (i + 1) + PREV[n])
                        ins = nc.vector.scalar_tensor_tensor(out=o, in0=x, scalar=wt[:, w:w + 1], in1=o, op0=ALU.mult, op1=ALU.add)
                    ins.then_inc(dw_ops, 1)

        @block.scalar
        def _(act):
            act.sem_inc(gdw_out, 2)
            act.sem_inc(gram_out, 1)
            act.sem_inc(qkv_out, 1)

            def pair_copy(i, u):
                g = 2 * u
                k = 0 if g < G0[1] else 1 if g < G0[2] else 2
                if g == G0[k]:
                    if k:
                        act.wait_ge(d_stored[k - 1], 16 * (i + 2))
                    else:
                        act.wait_ge(d_stored[2], 16 * (i + 1))
                act.wait_ge(gdw_sum, NPAIR * i + u + 1)
                nc.scalar.copy(stg[0:MG, g - G0[k]:g - G0[k] + 2, :], psg[u % 2][0:MG]).then_inc(gdw_out, 1)

            def body(i, last):
                for u in range(2, NPAIR):
                    pair_copy(i, u)
                if not last:
                    for u in range(2):
                        pair_copy(i + 1, u)
                act.wait_ge(acc_done, i + 1)
                nc.scalar.copy(qk, psa[:, :, 0:2 * C])
                act.wait_ge(v_stored, 16 * (i + 1))
                nc.scalar.copy(vst[:, :, 0:128], psa[:, :, 2 * C:512])
                nc.scalar.copy(vst[:, :, 128:192], psv).then_inc(qkv_out, 1)
                act.wait_ge(gram_sum, i + 1)
                act.wait_ge(gram_add, i + 1)
                nc.scalar.copy(gtmp[0:HC, :, 0:2 * HC], psq[0:HC, 0:4 * HC].rearrange("p (a c) -> p a c", a=2))
                nc.scalar.copy(gtmp[0:HC, :, 2 * HC:3 * HC], psk[0:HC].rearrange("p (a c) -> p a c", a=2)
                               ).then_inc(gram_out, 1)

            for u in range(2):
                pair_copy(0, u)
            with act.Fori(0, B * NS - 1) as i:
                body(i, False)
            body(B * NS - 1, True)

        @block.tensor
        def _(pe):
            pe.sem_inc(t_used, 2)

            def group(i, g):
                k = 0 if g < G0[1] else 1 if g < G0[2] else 2
                if g == G0[k]:
                    pe.wait_ge(p_loaded[k], 16 * NSH * (i + 1))
                if g % 2 == 0:
                    pe.wait_ge(gdw_out, NPAIR * i + g // 2 + 1)
                for dy in range(7):
                    for n, (a, xa) in enumerate(((0, 0), (1, 0), (0, 1))):
                        x = gbuf[:, g, xa, :].rearrange("p (r m) -> p r m", r=RB)[:, dy:dy + R, 0:W // 2]
                        ins = nc.tensor.matmul(psg[g // 2 % 2][0:MG, g % 2, :].rearrange("p (r m) -> p r m", r=R),
                                               diag[:, 7 * g + dy, a, :], x,
                                               start=(dy == 0 and n == 0), stop=(dy == 6 and n == 2), skip_group_check=True)
                if g % 2:
                    ins.then_inc(gdw_sum, 1)

            def pconv(k, rows, block_of, first=False, last=False):
                for p in range(4):
                    d = block_of(p)
                    nc.tensor.matmul(psa[:, p, :], d, pw[0:rows, k, 0:512], start=first, stop=last)
                    ins = nc.tensor.matmul(psv[:, p, :], d, pw[0:rows, k, 512:QKV],
                                           start=first and p == 0, stop=last, skip_group_check=True)
                return ins

            def p_tile(i, k):
                pe.wait_ge(d_loaded[k], 16 * ND[k] * (i + 2))
                for n in range(3 if k < 2 else 2):
                    slot, rows = 3 * k + n, 64 if 3 * k + n == 6 else 128
                    ins = pconv(6 + slot, rows, lambda p: dp[0:rows, slot, 128 * p:128 * p + 128],
                                first=(slot == 0), last=(slot == 7))
                return ins

            def t_tile(i, t):
                for n in range(3):
                    k = 3 * t + n
                    pe.wait_ge(dw_ops, OPS * (i + 1) + LAST[k])
                    ins = pconv(k, 128, lambda p: dt_[:, k, :].rearrange("p (h r m a) -> p a h r m", h=2, r=R // 2, a=2)[:, p // 2, p % 2])
                ins.then_inc(t_used, 1)

            def gram(i):
                pe.wait_ge(qkv_out, i + 2)
                for p in range(4):
                    for h in range(2):
                        sel = qk[:, p, :].rearrange("p (a c) -> p a c", a=2)[:, :, h * HC:(h + 1) * HC]
                        nc.tensor.matmul(psq[0:HC, 2 * HC * h:2 * HC * (h + 1)].rearrange("p (a c) -> p a c", a=2),
                                         qk[:, p, h * HC:(h + 1) * HC], sel,
                                         start=(p == 0 and h == 0), stop=(p == 3), skip_group_check=True)
                        ks = qk[:, p, C + h * HC:C + (h + 1) * HC]
                        ins = nc.tensor.matmul(psk[0:HC, HC * h:HC * (h + 1)], ks, ks,
                                               start=(p == 0 and h == 0), stop=(p == 3), skip_group_check=True)
                ins.then_inc(gram_sum, 1)

            def body(i, last):
                for g in range(4, NG):
                    group(i, g)
                pe.wait_ge(qkv_out, i + 1)
                pe.wait_ge(gram_out, i + 1)
                p_tile(i, 0)
                t_tile(i, 0)
                p_tile(i, 1)
                t_tile(i, 1)
                p_tile(i, 2).then_inc(acc_done, 1)
                if not last:
                    for g in range(4):
                        group(i + 1, g)
                gram(i)

            pe.wait_ge(weights, 64)
            pe.wait_ge(diag_ready, 6)
            for g in range(4):
                group(0, g)
            with pe.Fori(0, B * NS - 1) as i:
                body(i, False)
            body(B * NS - 1, True)

def layer0_attention(nc, sem, ar, ps, inp, v_dram, ident, gacc, attn_w, xin, xt):
    x_loaded = sem("l0_x_loaded")
    attention(nc, sem, ar, ps, inp, ident, gacc, attn_w, 0, (xt, xin, x_loaded))

    NV = 4
    vl = ar.take(NV, 4 * C)
    m0 = ar.take(BH, C)
    wp = ar.take(2, C)
    vs = ar.take(4, PX)
    wp_loaded = sem("l0_wproj_loaded")
    m_sum = sem("l0_m_in_psum")
    m_out = sem("l0_m_in_sbuf")
    v_loaded = [sem("l0_v_loaded") for _ in range(NV)]
    v_sum = sem("l0_v_transposed")
    v_out = sem("l0_v_in_sbuf")
    o_sum = sem("l0_out_in_psum")
    o_add = sem("l0_out_added")

    with nc.Block() as block:
        @block.sync
        def _(sp):
            sp.dma_start(wp[0:HC], inp["wproj0"]).then_inc(wp_loaded, 16)
            for i in range(B * NS):
                if i >= NV:
                    sp.wait_ge(v_sum, i - NV + 1)
                sp.dma_start(vl[:, i % NV, :], v_dram[i]).then_inc(v_loaded[i % NV], 16)

        @block.tensor
        def _(pe):
            pe.wait_ge(wp_loaded, 16)
            for bh in range(BH):
                ins = nc.tensor.matmul(ps[0:HC, bh, 0:C], attn_w[0:HC, bh, :], wp[0:HC, bh % 2, :], start=True, stop=True)
            ins.then_inc(m_sum, 1)
            pe.wait_ge(m_out, 1)
            for i in range(B * NS + 1):
                if i < B * NS:
                    if i >= 2:
                        pe.wait_ge(v_out, 2 * (i - 1))
                    pe.wait_ge(v_loaded[i % NV], 16 * (i // NV + 1))
                    for h in range(2):
                        for p in range(4):
                            ins = nc.tensor.transpose(ps[0:HC, 2 * (i % 2) + h, 128 * p:128 * p + 128],
                                                      vl[:, i % NV, C * p + HC * h:C * p + HC * h + HC], ident)
                    ins.then_inc(v_sum, 1)
                if i >= 1:
                    k = i - 1
                    b, bank = k // NS, 4 + 2 * (k % 2)
                    pe.wait_ge(v_out, 2 * (k + 1))
                    if k >= 2:
                        pe.wait_ge(o_add, 2 * (k - 1))
                    for out, c0, n in ((ps[:, bank, :], 0, 128), (ps[64 * b:64 * b + 64, bank + 1, :], 128, 64)):
                        for h in range(2):
                            ins = nc.tensor.matmul(out, m0[0:HC, 2 * b + h, c0:c0 + n], vs[0:HC, 2 * (k % 2) + h, :],
                                                   start=(h == 0), stop=(h == 1))
                    ins.then_inc(o_sum, 1)

        @block.scalar
        def _(act):
            act.wait_ge(m_sum, 1)
            nc.scalar.copy(m0[0:HC], ps[0:HC, 0:BH, 0:C]).then_inc(m_out, 1)
            for i in range(B * NS):
                act.wait_ge(v_sum, i + 1)
                if i >= 2:
                    act.wait_ge(o_sum, i - 1)
                for h in range(2):
                    k = 2 * (i % 2) + h
                    nc.scalar.copy(vs[0:HC, k, :].rearrange("p (r m a) -> p a r m", r=R, a=2),
                                   ps[0:HC, k, :].rearrange("p (a r m) -> p a r m", a=2, r=R)).then_inc(v_out, 1)

        @block.vector
        def _(dve):
            dve.wait_ge(x_loaded, 16 * 4)
            for i in range(B * NS):
                b, s, bank = i // NS, i % NS, 4 + 2 * (i % 2)
                dve.wait_ge(o_sum, i + 1)
                n0, lo = s * PX, 64 * b
                nc.vector.tensor_tensor(xt[:, b, n0:n0 + PX], ps[:, bank, :], xt[:, b, n0:n0 + PX], ALU.add).then_inc(o_add, 1)
                nc.vector.tensor_tensor(xt[lo:lo + 64, 2, n0:n0 + PX], ps[lo:lo + 64, bank + 1, :],
                                        xt[lo:lo + 64, 2, n0:n0 + PX], ALU.add).then_inc(o_add, 1)


def attention(nc, sem, ar, ps, inp, ident, gacc, attn_w, layer, load=None):
    at = ar.at
    tmp = ar.take(BH, HC)
    ssq = ar.take(2, BH)
    nrm = ar.take(2, BH)
    rcp = ar.take(2, BH)
    dg = ar.take(BH, HC)
    sc = ar.take(BH, HC)
    bm = ar.take(HH)
    a = ar.take(BH, HD)
    e = ar.take(BH, HD)
    mx = ar.take(BH)
    ones = ar.take(HC)
    temp = ar.take(2)
    scl = ar.take(3)
    tri = ar.take(HD, HD)
    cmp = ar.take(BH * HD, HD)
    eq = ar.take(BH * HD, HD)
    rank = ar.take(BH, HD)
    em = ar.take(BH, HD)
    se = ar.take(BH)
    wsum = ar.take(BH, HD)
    ar.at = at

    consts = sem(f"attn{layer}_consts")
    chain = sem(f"attn{layer}_chain")
    sums = sem(f"attn{layer}_square_sums")
    roots = sem(f"attn{layer}_roots")
    diag_k = sem(f"attn{layer}_k_diagonal")
    bcast = sem(f"attn{layer}_k_broadcast")
    centred = sem(f"attn{layer}_centred")
    exped = sem(f"attn{layer}_exp")
    P_ = slice(0, HC)

    def bc(v, shape):
        return v.to_broadcast(shape)

    with nc.Block() as block:
        @block.sync
        def _(sp):
            sp.dma_start(bm[P_], inp["head_mask"]).then_inc(consts, 16)
            sp.dma_start(temp[P_], inp["temperature_rows"]).then_inc(consts, 16)
            sp.dma_start(scl[P_], inp["scales_rows"]).then_inc(consts, 16)
            sp.dma_start(tri[P_], inp["tri"]).then_inc(consts, 16)
            if load is not None:
                for t in range(NT):
                    for p0, b, c0, n in pieces(t):
                        sp.dma_start(load[0][p0:p0 + n, t, :], load[1][b, c0:c0 + n, :]).then_inc(load[2], 16)

        @block.tensor
        def _(pe):
            pe.wait_ge(diag_k, 1)
            nc.tensor.matmul(ps[P_, 0, 0:BH * HC], ones[P_, :], dg[P_].rearrange("p a c -> p (a c)"),
                             start=True, stop=True).then_inc(bcast, 1)

        @block.scalar
        def _(act):
            act.wait_ge(sums, 1)
            nc.scalar.activation(nrm[P_], ssq[P_], ACT.Sqrt).then_inc(roots, 1)
            act.wait_ge(centred, 1)
            nc.scalar.activation(e[P_], em[P_], ACT.Exp).then_inc(exped, 1)

        @block.vector
        def _(dve):
            n = [0]

            def step(ins):
                ins.then_inc(chain, 1)
                n[0] += 1
                dve.wait_ge(chain, n[0])

            V = nc.vector
            dve.wait_ge(consts, 64)
            step(V.memset(ones[P_], 1.0))
            idb = bc(ident[P_, 0:HC].unsqueeze(1), [HC, BH, HC])
            for x, lo in ((0, 0), (1, 2 * HC)):
                step(V.tensor_tensor(tmp[P_], gacc[P_, :, lo:lo + HC], idb, ALU.mult))
                step(V.tensor_reduce(ssq[P_, x, :], tmp[P_], AX, ALU.add))
            V.tensor_copy(rcp[P_], ssq[P_]).then_inc(sums, 1)
            dve.wait_ge(roots, 1)
            step(V.tensor_scalar(nrm[P_], nrm[P_], 1e-12, None, ALU.max))
            step(V.reciprocal(rcp[P_], nrm[P_]))
            V.tensor_tensor(dg[P_], idb, bc(rcp[P_, 1, :].unsqueeze(2), [HC, BH, HC]), ALU.mult).then_inc(diag_k, 1)
            dve.wait_ge(bcast, 1)
            step(V.tensor_tensor(sc[P_], gacc[P_, :, HC:2 * HC], ps[P_, 0, 0:BH * HC].rearrange("p (a c) -> p a c", a=BH), ALU.mult))
            step(V.tensor_tensor(sc[P_].rearrange("p b (h j) -> p b h j", h=HH), sc[P_].rearrange("p b (h j) -> p b h j", h=HH),
                                 bc(bm[P_].unsqueeze(1).unsqueeze(3), [HC, BH, HH, HD]), ALU.mult))
            step(V.tensor_reduce(a[P_], sc[P_].rearrange("p b (h j) -> p b j h", h=HH), AX, ALU.add))
            step(V.tensor_tensor(a[P_], a[P_], bc(rcp[P_, 0, :].unsqueeze(2), [HC, BH, HD]), ALU.mult))
            if layer == 0:
                step(V.tensor_tensor(a[P_].rearrange("p (b h) j -> p b h j", b=B), a[P_].rearrange("p (b h) j -> p b h j", b=B),
                                     bc(temp[P_].unsqueeze(1).unsqueeze(3), [HC, B, 2, HD]), ALU.mult))
            else:
                step(V.tensor_scalar(a[P_], a[P_], 1.0 / float(HW) ** 0.5, None, ALU.mult))
            step(V.tensor_reduce(mx[P_], a[P_], AX, ALU.max))
            V.tensor_tensor(em[P_], a[P_], bc(mx[P_].unsqueeze(2), [HC, BH, HD]), ALU.subtract).then_inc(centred, 1)
            if layer == 0:
                for b in range(BH):
                    ai = bc(a[P_, b, :].unsqueeze(2), [HC, HD, HD])
                    aj = bc(a[P_, b, :].unsqueeze(1), [HC, HD, HD])
                    cb, eb = cmp[P_, b * HD:(b + 1) * HD, :], eq[P_, b * HD:(b + 1) * HD, :]
                    step(V.tensor_tensor(cb, aj, ai, ALU.is_gt))
                    step(V.tensor_tensor(eb, aj, ai, ALU.is_equal))
                    step(V.tensor_tensor(eb, eb, tri[P_], ALU.mult))
                    step(V.tensor_tensor(cb, cb, eb, ALU.add))
                step(V.tensor_reduce(rank[P_], cmp[P_].rearrange("p (b i) j -> p b i j", b=BH), AX, ALU.add))
            dve.wait_ge(exped, 1)
            parts = [HD // 2, HD * 2 // 3, HD * 3 // 4] if layer == 0 else [HD]
            for k, top in enumerate(parts):
                if layer == 0:
                    step(V.tensor_scalar(em[P_], rank[P_], float(top), None, ALU.is_lt))
                    step(V.tensor_tensor(em[P_], em[P_], e[P_], ALU.mult))
                else:
                    step(V.tensor_copy(em[P_], e[P_]))
                step(V.tensor_reduce(se[P_], em[P_], AX, ALU.add))
                step(V.reciprocal(se[P_], se[P_]))
                if layer == 0:
                    step(V.tensor_scalar(se[P_], se[P_], scl[P_, k:k + 1], None, ALU.mult))
                dst = wsum if k == 0 else em
                step(V.tensor_tensor(dst[P_], em[P_], bc(se[P_].unsqueeze(2), [HC, BH, HD]), ALU.mult))
                if k:
                    step(V.tensor_tensor(wsum[P_], wsum[P_], em[P_], ALU.add))
            for b in range(BH):
                step(V.tensor_tensor(attn_w[P_, b, :].rearrange("p (h j) -> p h j", h=HH),
                                     bc(wsum[P_, b, :].unsqueeze(1), [HC, HH, HD]),
                                     bc(bm[P_].unsqueeze(2), [HC, HH, HD]), ALU.mult))


def residual_block(nc, sem, ps, tag, xt, linear_of, x_from=None, x_to=None, xr=None, bias=None):
    NP = NT * 2
    loaded = [sem(f"{tag}_residual_loaded") for _ in range(2)]
    summed = sem(f"{tag}_sum_in_psum")
    added = sem(f"{tag}_added")
    stored = sem(f"{tag}_stored")

    with nc.Block() as block:
        @block.sync
        def _(sp):
            n_st = 0
            for i in range(NP):
                t, n0 = i // 2, (i % 2) * 2048
                if x_from is not None:
                    if i >= 2:
                        sp.wait_ge(added, 4 * (i - 1))
                    for p0, b, c0, n in pieces(t):
                        sp.dma_start(xr[p0:p0 + n, i % 2, :], x_from[b, c0:c0 + n, n0:n0 + 2048]).then_inc(loaded[i % 2], 16)
                if x_to is not None:
                    sp.wait_ge(added, 4 * (i + 1))
                    for p0, b, c0, n in pieces(t):
                        sp.dma_start(x_to[b, c0:c0 + n, n0:n0 + 2048], xt[p0:p0 + n, t, n0:n0 + 2048]).then_inc(stored, 16)
                        n_st += 1
            if n_st:
                sp.wait_ge(stored, 16 * n_st)

        @block.tensor
        def _(pe):
            for m in range(NP * 4):
                if m >= 8:
                    pe.wait_ge(added, m - 7)
                linear_of(ps[:, m % 8, :], m // 8, (m % 8) * 512).then_inc(summed, 1)

        @block.vector
        def _(dve):
            need = [0, 0]
            for m in range(NP * 4):
                i = m // 4
                if x_from is not None and m % 4 == 0:
                    need[i % 2] += 16 * len(pieces(i // 2))
                    dve.wait_ge(loaded[i % 2], need[i % 2])
                dve.wait_ge(summed, m + 1)
                o = xt[:, m // 8, (m % 8) * 512:(m % 8) * 512 + 512]
                x = o if x_from is None else xr[:, i % 2, (m % 4) * 512:(m % 4) * 512 + 512]
                if bias is None:
                    ins = nc.vector.tensor_tensor(o, ps[:, m % 8, :], x, ALU.add)
                else:
                    ins = nc.vector.scalar_tensor_tensor(out=o, in0=ps[:, m % 8, :], scalar=bias[:, m // 8:m // 8 + 1],
                                                         in1=x, op0=ALU.add, op1=ALU.add)
                ins.then_inc(added, 1)


def layer1(nc, sem, ar, ps, inp, xt_, x2, ident, gacc, attn_w):
    xn = ar.take(NT, HW)
    at = ar.at
    group_norm(nc, sem, ar, ps, inp, 1, ident, xt_, dst=xn)
    ar.at = at
    SRC = [0, 2, 1]
    NB = HW // 128
    xt = ar.take(2, 2 * C)
    xx = ar.take(B * 2, C)
    wqk = ar.take(2, 2 * C)
    tt = ar.take(B * 2, 2 * C)
    wv = ar.take(2, C)
    wload = sem("l1_weights")
    tsum = sem("l1_transposed")
    tout = sem("l1_transposed_out")
    xxsum = sem("l1_xx_sum")
    xxout = sem("l1_xx_out")
    tts = sem("l1_t_sum")
    tto = sem("l1_t_out")
    gsum = sem("l1_gram_sum")

    def parts(b):
        if b == 0:
            return [(0, 0, 0, 128), (1, 128, 128, 64)]
        return [(0, 256, 64, 128), (1, 192, 0, 64)]

    with nc.Block() as block:
        @block.sync
        def _(sp):
            sp.dma_start(wqk[:, 0, :], inp["w1qk"][0:128, :]).then_inc(wload, 16)
            sp.dma_start(wqk[0:64, 1, :], inp["w1qk"][128:192, :]).then_inc(wload, 16)
            sp.dma_start(wv[0:HC], inp["w1v"]).then_inc(wload, 16)

        @block.tensor
        def _(pe):
            for k in range(NB + 1):
                if k < NB:
                    if k >= 2:
                        pe.wait_ge(tout, k - 1)
                    for m, t in enumerate(SRC):
                        ins = nc.tensor.transpose(ps[:, k % 2, 128 * m:128 * m + 128], xn[:, t, 128 * k:128 * k + 128], ident)
                    ins.then_inc(tsum, 1)
                if k >= 1:
                    j = k - 1
                    pe.wait_ge(tout, j + 1)
                    for b in range(B):
                        for rb, x0, _, n in parts(b):
                            ins = nc.tensor.matmul(ps[0:n, 2 + rb, C * b:C * b + C], xt[:, j % 2, x0:x0 + n],
                                                   xt[:, j % 2, C * b:C * b + C],
                                                   start=(j == 0 and b == 0), stop=(j == NB - 1), skip_group_check=True)
                    if j == NB - 1:
                        ins.then_inc(xxsum, 1)
            pe.wait_ge(wload, 48)
            pe.wait_ge(xxout, 2)
            for b in range(B):
                for rb, _, c0, n in parts(b):
                    for kb in range(2):
                        kn = 64 if kb else 128
                        ins = nc.tensor.matmul(ps[0:n, 4 + 2 * b + rb, 0:2 * C], xx[0:kn, 2 * b + kb, c0:c0 + n],
                                               wqk[0:kn, kb, :], start=(kb == 0), stop=(kb == 1))
            ins.then_inc(tts, 1)
            pe.wait_ge(tto, 1)
            for b in range(B):
                for h in range(2):
                    for kb in range(2):
                        kn = 64 if kb else 128
                        t = tt[0:kn, 2 * b + kb, :]
                        nc.tensor.matmul(ps[0:HC, 2 * b + h, 0:2 * HC].rearrange("p (a c) -> p a c", a=2),
                                         wqk[0:kn, kb, h * HC:(h + 1) * HC],
                                         t.rearrange("p (a c) -> p a c", a=2)[:, :, h * HC:(h + 1) * HC],
                                         start=(kb == 0), stop=(kb == 1), skip_group_check=True)
                    for kb in range(2):
                        kn = 64 if kb else 128
                        ins = nc.tensor.matmul(ps[0:HC, 4 + 2 * b + h, 0:HC], wqk[0:kn, kb, C + h * HC:C + (h + 1) * HC],
                                               tt[0:kn, 2 * b + kb, C + h * HC:C + (h + 1) * HC],
                                               start=(kb == 0), stop=(kb == 1), skip_group_check=True)
            ins.then_inc(gsum, 1)

        @block.scalar
        def _(act):
            for k in range(NB):
                act.wait_ge(tsum, k + 1)
                nc.scalar.copy(xt[:, k % 2, :], ps[:, k % 2, 0:2 * C]).then_inc(tout, 1)
            act.wait_ge(xxsum, 1)
            nc.scalar.copy(xx.rearrange("p (b r) c -> p b r c", b=B)[:, :, 0, :],
                           ps[:, 2, 0:2 * C].rearrange("p (b c) -> p b c", b=B)).then_inc(xxout, 1)
            nc.scalar.copy(xx.rearrange("p (b r) c -> p b r c", b=B)[0:64, :, 1, :],
                           ps[0:64, 3, 0:2 * C].rearrange("p (b c) -> p b c", b=B)).then_inc(xxout, 1)
            act.wait_ge(tts, 1)
            nc.scalar.copy(tt.rearrange("p (b r) c -> p b r c", b=B)[:, :, 0, :],
                           ps[:, 4:8, 0:2 * C].rearrange("p (b r) c -> p b r c", b=B)[:, :, 0, :])
            nc.scalar.copy(tt.rearrange("p (b r) c -> p b r c", b=B)[0:64, :, 1, :],
                           ps[0:64, 4:8, 0:2 * C].rearrange("p (b r) c -> p b r c", b=B)[:, :, 1, :]).then_inc(tto, 1)
            act.wait_ge(gsum, 1)
            nc.scalar.copy(gacc[0:HC, :, 0:2 * HC], ps[0:HC, 0:4, 0:2 * HC])
            nc.scalar.copy(gacc[0:HC, :, 2 * HC:3 * HC], ps[0:HC, 4:8, 0:HC])

    ar.at = at + 2 * 2 * C
    keep_wv = ar.take(2, C)
    wv_at = ar.at
    del keep_wv
    ar.at = at + 2 * 2 * C + B * 2 * C + 2 * 2 * C + B * 2 * 2 * C + 2 * C
    attention(nc, sem, ar, ps, inp, ident, gacc, attn_w, 1)

    awt = ar.take(BH, HC)
    ma = ar.take(B, C)
    mc = ar.take(C)
    a_sum = sem("l1_attn_transposed")
    a_out = sem("l1_attn_out")
    m_sum = sem("l1_m_sum")
    m_out = sem("l1_m_out")
    with nc.Block() as block:
        @block.tensor
        def _(pe):
            for bh in range(BH):
                ins = nc.tensor.transpose(ps[0:HC, 0, bh * HC:(bh + 1) * HC], attn_w[0:HC, bh, :], ident[0:HC, 0:HC])
            ins.then_inc(a_sum, 1)
            pe.wait_ge(a_out, 1)
            for b in range(B):
                for h in range(2):
                    nc.tensor.matmul(ps[:, 1 + b, h * HC:(h + 1) * HC], wv[0:HC, h, 0:128], awt[0:HC, 2 * b + h, :],
                                     start=(h == 0), stop=True, skip_group_check=True)
                    ins = nc.tensor.matmul(ps[64 * b:64 * b + 64, 3 + b, h * HC:(h + 1) * HC], wv[0:HC, h, 128:192],
                                           awt[0:HC, 2 * b + h, :], start=(h == 0), stop=True, skip_group_check=True)
            ins.then_inc(m_sum, 1)

        @block.scalar
        def _(act):
            act.wait_ge(a_sum, 1)
            nc.scalar.copy(awt[0:HC], ps[0:HC, 0, 0:BH * HC].rearrange("p (a c) -> p a c", a=BH)).then_inc(a_out, 1)
            act.wait_ge(m_sum, 1)
            nc.scalar.copy(ma, ps[:, 1:3, 0:C])
            for b in range(B):
                nc.scalar.copy(mc[64 * b:64 * b + 64], ps[64 * b:64 * b + 64, 3 + b, 0:C]).then_inc(m_out, 1)

    def lin(out, t, n0):
        if t < 2:
            lo = 64 * t
            nc.tensor.matmul(out, ma[:, t, 0:128], xn[:, t, n0:n0 + 512], start=True, stop=False)
            return nc.tensor.matmul(out, mc[lo:lo + 64, 0:128], xn[lo:lo + 64, 2, n0:n0 + 512], start=False, stop=True)
        for b in range(B):
            lo = 64 * b
            nc.tensor.matmul(out[lo:lo + 64], ma[:, b, 128:192], xn[:, b, n0:n0 + 512], start=True, stop=False)
            ins = nc.tensor.matmul(out[lo:lo + 64], mc[lo:lo + 64, 128:192], xn[lo:lo + 64, 2, n0:n0 + 512],
                                   start=False, stop=True)
        return ins

    residual_block(nc, sem, ps, "l1", xt_, lin, x_to=x2)


def layer2(nc, sem, ar, ps, inp, xt, x2, ident):
    xn = xt
    at = ar.at
    group_norm(nc, sem, ar, ps, inp, 2, ident, xt)
    ar.at = at
    NP2 = 2 * C + 4 * 32
    y = ar.take(NT, HW)
    wa = ar.take(NP2)
    wc = ar.take(NP2)
    woa = ar.take(C)
    woc = ar.take(C)
    cols = ar.take(16)
    na = ar.take(NT, N_STATE)
    sel32 = ar.take(NT * N_STATE * 128 // 2)
    sel = sel32.bitcast(BF16).rearrange("p (a c) -> p a c", a=NT * N_STATE)
    bc3 = ar.take16(2, HW)
    hs = ar.take(N_STATE)
    z = ar.take(HW)
    dx = ar.take(HW)
    ring_at = ar.at
    bias_s = ar.take(8)

    loaded = sem("l2_weights")
    selc = sem("l2_selector_ready")
    bcs = sem("l2_bc_sum")
    bch = sem("l2_bc_parts")
    bcv = sem("l2_bc_chain")
    moved = sem("l2_bc_moved")
    prep = sem("l2_prepared")

    scratch = Arena(ar.mem, at + 2 * HW)
    scratch.at = at
    parts = scratch.take16(3, HW)
    full = scratch.take(512)
    scratch = Arena(ar.mem, ring_at)
    scratch.at = ring_at - 2 * HW
    stage = scratch.take(NT * N_STATE * 128)
    with nc.Block() as block:
        @block.sync
        def _(sp):
            for dst, name in ((wa, "w2a"), (wc, "w2c"), (woa, "wo2a"), (woc, "wo2c"), (cols[:, 0:15], "cols2"),
                              (na, "alog2"), (stage[0:96], "sel2"), (bias_s[0:64, 0:1], "bcbias2")):
                sp.dma_start(dst, inp[name]).then_inc(loaded, 16)
            sp.wait_ge(bcv, 5 * 8)
            for part in range(3):
                for x in range(2):
                    sp.dma_start(bc3[32 * part:32 * part + 32, x, :], parts[32 * x:32 * x + 32, part, :]).then_inc(moved, 16)
            sp.wait_ge(moved, 96)

        @block.tensor
        def _(pe):
            pe.wait_ge(loaded, 128)
            for k in range(8):
                if k >= 2:
                    pe.wait_ge(bch, k - 1)
                for x in range(2):
                    o0 = 2 * C + 64 * x
                    for b in range(B):
                        nc.tensor.matmul(ps[32 * x:32 * x + 32, k % 2, :], wa[:, o0 + 32 * b:o0 + 32 * b + 32],
                                         xn[:, b, 512 * k:512 * k + 512], start=(b == 0), stop=False)
                    ins = nc.tensor.matmul(ps[32 * x:32 * x + 32, k % 2, :], wc[:, o0:o0 + 32],
                                           xn[:, 2, 512 * k:512 * k + 512], start=False, stop=True)
                ins.then_inc(bcs, 1)

        @block.scalar
        def _(act):
            act.wait_ge(loaded, 128)
            nc.scalar.activation(na, na, ACT.Exp).then_inc(prep, 1)
            nc.scalar.copy(sel32.bitcast(BF16)[0:96], stage[0:96]).then_inc(selc, 1)

        @block.vector
        def _(dve):
            V = nc.vector
            dve.wait_ge(loaded, 128)
            dve.wait_ge(prep, 1)
            V.tensor_scalar(na, na, -1.0, None, ALU.mult).then_inc(prep, 1)
            for t in range(NT):
                V.tensor_tensor(cols[:, 5 * t + 1:5 * t + 2], cols[:, 5 * t + 1:5 * t + 2], cols[:, 5 * t + 2:5 * t + 3], ALU.add).then_inc(prep, 1)
            n = 0
            for k in range(8):
                s = slice(512 * k, 512 * k + 512)
                dve.wait_ge(bcs, k + 1)
                if k:
                    dve.wait_ge(bcv, 5 * k)
                V.tensor_scalar(full[0:64], ps[0:64, k % 2, :], bias_s[0:64, 0:1], None, ALU.add).then_inc(bch, 1)
                dve.wait_ge(bch, k + 1)
                for part in range(3):
                    if part:
                        dve.wait_ge(bcv, n)
                        V.tensor_tensor(full[0:64], full[0:64], parts[0:64, part - 1, s], ALU.subtract).then_inc(bcv, 1)
                        n += 1
                        dve.wait_ge(bcv, n)
                    V.tensor_copy(parts[0:64, part, s], full[0:64]).then_inc(bcv, 1)
                    n += 1

    ar.at = ring_at
    da = ar.take(2, CH)
    dbx = ar.take(2, CH)
    hh = ar.take(2, CH)
    hc = ar.take(2, CH)
    l2_sems = [sem(n) for n in ("l2_proj_sum", "l2_xin_out", "l2_delta_out", "l2_vector_chain", "l2_scalar_chain", "l2_b_broadcast", "l2_c_broadcast", "l2_decay", "l2_input", "l2_scan", "l2_h_times_c", "l2_y_accumulated", "l2_state_carried", "l2_y_added")]
    for t in range(NT):
        layer2_tile(nc, l2_sems, ps, t, xn, y, wa, wc, cols, na, sel, bc3, hs, z, dx, da, dbx, hh, hc, ident)

    ar.at = ring_at
    xr = ar.take(2, 2048)

    def lin(out, t, n0):
        return linear(nc, out, woa, woc, 0, t, y, n0, 512)

    bo = cols[:, 0:15].rearrange("p (t k) -> p t k", t=NT)[:, :, 4]
    residual_block(nc, sem, ps, "l2", xt, lin, x_from=x2, xr=xr, bias=bo)


def layer2_tile(nc, sems, ps, t, xn, y, wa, wc, cols, na, sel, bc3, hs, z, dx, da, dbx, hh, hc, ident):
    NC = HW // 512
    psum_in, x_out, d_out, vch, ach = sems[0:5]
    bsum, csum, exp_done, dbx_done, scan_done, hc_done, ysum, carried, yadd = sems[5:]
    m0, j0 = N_STATE * (HW // CH) * t, (HW // CH) * t
    lg = [(da.rearrange("p a b -> p (a b)"), 0), (dbx.rearrange("p a b -> p (a b)"), 2 * CH)]

    with nc.Block() as block:
        @block.tensor
        def _(pe):
            for k in range(NC):
                for x in range(2):
                    if k >= 4:
                        pe.wait_ge(x_out if x == 0 else d_out, NC * t + k - 3)
                    linear(nc, ps[:, 2 * (k % 4) + x, :], wa, wc, C * x, t, xn, 512 * k, 512).then_inc(psum_in, 1)

        @block.scalar
        def _(act):
            for k in range(NC):
                s = slice(512 * k, 512 * k + 512)
                act.wait_ge(psum_in, 2 * NC * t + 2 * k + 2)
                nc.scalar.activation(z[:, s], ps[:, 2 * (k % 4) + 1, :], ACT.Identity, bias=cols[:, 5 * t + 1:5 * t + 2]
                                     ).then_inc(d_out, 1)
            act.wait_ge(d_out, NC * (t + 1))
            n = 6 * t
            for func, kw in ((ACT.Abs, {}), (ACT.Exp, dict(scale=-1.0)), (ACT.Ln, dict(bias=1.0))):
                for buf, c0 in lg:
                    src = z[:, c0:c0 + 2 * CH] if func == ACT.Abs else buf
                    if func != ACT.Abs:
                        act.wait_ge(ach, n - 1)
                    nc.scalar.activation(buf, src, func, **kw).then_inc(ach, 1)
                    n += 1

        @block.vector
        def _(dve):
            V = nc.vector
            for k in range(NC):
                s = slice(512 * k, 512 * k + 512)
                dve.wait_ge(psum_in, 2 * NC * t + 2 * k + 1)
                V.tensor_scalar(y[:, t, s], ps[:, 2 * (k % 4), :], cols[:, 5 * t:5 * t + 1], None, ALU.add).then_inc(x_out, 1)
            n = 6 * t
            for i, (buf, c0) in enumerate(lg):
                s = slice(c0, c0 + 2 * CH)
                dve.wait_ge(ach, 6 * t + 5 + i)
                V.scalar_tensor_tensor(out=z[:, s], in0=z[:, s], scalar=0.0, in1=buf, op0=ALU.max, op1=ALU.add).then_inc(vch, 1)
                n += 1
                dve.wait_ge(vch, n)
                dve.wait_ge(x_out, NC * (t + 1))
                V.tensor_tensor(dx[:, s], z[:, s], y[:, t, s], ALU.mult).then_inc(vch, 1)
                n += 1
                dve.wait_ge(vch, n)
                V.tensor_scalar(y[:, t, s], y[:, t, s], cols[:, 5 * t + 3:5 * t + 4], None, ALU.mult).then_inc(vch, 1)
                n += 1
            V.memset(hs, 0.0)

    N = N_STATE
    pb = [ps[:, 0:2, :], ps[:, 2:4, :]]
    pc = ps[:, 4:6, :]
    py = ps[:, 6:8, :]

    def halves(v):
        return v.rearrange("p (a c) -> p a c", a=2)

    with nc.Block() as block:
        @block.tensor
        def _(pe):
            def b_bcast(j, n):
                m = m0 + N * j + n
                pe.wait_ge(dbx_done, m + 1)
                for a in range(2):
                    ins = nc.tensor.matmul(pb[n % 2][:, a, :], sel[0:96, N * t + n, :], bc3[0:96, 0, bass.ds(j * CH + 512 * a, 512)],
                                           start=True, stop=True)
                ins.then_inc(bsum, 1)

            def c_bcast(j, n):
                pe.wait_ge(hc_done, m0 + N * j + n + 2)
                for a in range(2):
                    ins = nc.tensor.matmul(pc[:, a, :], sel[0:96, N * t + n, :], bc3[0:96, 1, bass.ds(j * CH + 512 * a, 512)],
                                           start=True, stop=True)
                ins.then_inc(csum, 1)

            def accumulate(j, n):
                pe.wait_ge(hc_done, m0 + N * j + n + 3)
                if n == 0:
                    pe.wait_ge(yadd, j0 + j + 1)
                for a in range(2):
                    ins = nc.tensor.matmul(py[:, a, :], ident, hc[:, n % 2, 512 * a:512 * a + 512], start=(n == 0), stop=(n == N - 1))
                ins.then_inc(ysum, 1)

            with pe.Fori(0, HW // CH) as j:
                b_bcast(j, 0)
                for n in range(N):
                    if n + 1 < N:
                        b_bcast(j, n + 1)
                    c_bcast(j, n)
                    if n:
                        accumulate(j, n - 1)
                accumulate(j, N - 1)

        @block.scalar
        def _(act):
            with act.Fori(0, HW // CH) as j:
                for n in range(N):
                    m = m0 + N * j + n
                    act.wait_ge(scan_done, m + 1)
                    act.nop(nofuse=True)
                    nc.scalar.activation(da[:, n % 2, :], z[:, bass.ds(j * CH, CH)], ACT.Exp, scale=na[:, t, n:n + 1]
                                         ).then_inc(exp_done, 1)
                    if n >= 1:
                        act.wait_ge(scan_done, m + 2)
                        nc.scalar.copy(hs[:, n - 1:n], hh[:, (n - 1) % 2, CH - 1:CH]).then_inc(carried, 1)
                act.wait_ge(scan_done, m0 + N * j + N + 2)
                nc.scalar.copy(hs[:, N - 1:N], hh[:, (N - 1) % 2, CH - 1:CH]).then_inc(carried, 1)

        @block.vector
        def _(dve):
            V = nc.vector
            if t == 0:
                for s in (dbx_done, scan_done, hc_done, carried, ysum):
                    dve.sem_inc(s, 2)
                dve.sem_inc(yadd, 1)

            def product(j, n):
                m = m0 + N * j + n
                dve.wait_ge(bsum, m + 1)
                dve.wait_ge(scan_done, m + 1)
                V.tensor_tensor(halves(dbx[:, n % 2, :]), pb[n % 2], halves(dx[:, bass.ds(j * CH, CH)]), ALU.mult).then_inc(dbx_done, 1)

            def scan(j, n):
                m = m0 + N * j + n
                dve.wait_ge(dbx_done, m + 3)
                dve.wait_ge(exp_done, m + 1)
                dve.wait_ge(hc_done, m + 1)
                dve.wait_ge(carried, m + 1)
                V.tensor_tensor_scan(hh[:, n % 2, :], da[:, n % 2, :], dbx[:, n % 2, :], hs[:, n:n + 1],
                                     ALU.mult, ALU.add).then_inc(scan_done, 1)

            def times_c(j, n):
                m = m0 + N * j + n
                dve.wait_ge(csum, m + 1)
                dve.wait_ge(scan_done, m + 3)
                dve.wait_ge(ysum, m + 1)
                V.tensor_tensor(halves(hc[:, n % 2, :]), halves(hh[:, n % 2, :]), pc, ALU.mult).then_inc(hc_done, 1)

            with dve.Fori(0, HW // CH) as j:
                product(j, 0)
                for n in range(N):
                    if n + 1 < N:
                        product(j, n + 1)
                    scan(j, n)
                    times_c(j, n)
                dve.wait_ge(ysum, m0 + N * j + N + 2)
                V.tensor_tensor(halves(y[:, t, bass.ds(j * CH, CH)]), py, halves(y[:, t, bass.ds(j * CH, CH)]), ALU.add).then_inc(yadd, 1)


def layer3(nc, sem, ar, ps, inp, xt, xout, ident):
    pad = ar.take(NT * 4900)
    at = ar.at
    group_norm(nc, sem, ar, ps, inp, 3, ident, xt, padded=pad)
    ar.at = at
    wts = ar.take(NT, 49)
    bias = ar.take(NT)
    diag = ar.take(2 * 49, 128)
    loaded = sem("l3_weights")
    chain = sem("l3_mirror_chain")
    diag_ready = sem("l3_diagonals")
    psum_done = sem("l3_sum_in_psum")
    added = sem("l3_added")
    biased = sem("l3_biased")
    taps = sem("l3_taps")
    stored = sem("l3_stored")
    VP = ROWS_V * W
    NCH = (H - ROWS_V) // R

    def img(t):
        return pad[:, t * 4900:(t + 1) * 4900].rearrange("p (r w) -> p r w", r=70)

    with nc.Block() as block:
        @block.sync
        def _(sp):
            sp.dma_start(wts, inp["w3"]).then_inc(loaded, 16)
            sp.dma_start(bias, inp["b3"]).then_inc(loaded, 16)
            n = 0
            for t in range(NT):
                sp.wait_ge(added, NCH * (t + 1))
                for p0, b, c0, m in pieces(t):
                    sp.dma_start(xout[b, c0:c0 + m, VP:HW], xt[p0:p0 + m, t, VP:HW]).then_inc(stored, 16)
                    n += 1
            sp.wait_ge(taps, NT * 49)
            for t in range(NT):
                for p0, b, c0, m in pieces(t):
                    sp.dma_start(xout[b, c0:c0 + m, 0:VP], xt[p0:p0 + m, t, 0:VP]).then_inc(stored, 16)
                    n += 1
            sp.wait_ge(stored, 16 * n)

        @block.gpsimd
        def _(pool):
            pool.wait_ge(loaded, 32)
            for t in range(NT):
                if t >= 2:
                    pool.wait_ge(psum_done, NCH * (t - 1))
                nc.gpsimd.tensor_tensor(diag[:, 49 * (t % 2):49 * (t % 2) + 49, :],
                                        ident.unsqueeze(1).to_broadcast([128, 49, 128]),
                                        wts[:, t, :].unsqueeze(2).to_broadcast([128, 49, 128]), ALU.mult).then_inc(diag_ready, 1)

        @block.scalar
        def _(act):
            act.wait_ge(loaded, 32)
            for t in range(NT):
                nc.scalar.activation(xt[:, t, :], xt[:, t, :], ACT.Identity, bias=bias[:, t:t + 1]).then_inc(biased, 1)

        @block.tensor
        def _(pe):
            pe.wait_ge(chain, 12 * NT)
            for m in range(NT * NCH):
                t, k = m // NCH, m % NCH
                pe.wait_ge(diag_ready, t + 1)
                if m >= 8:
                    pe.wait_ge(added, m - 7)
                r0 = ROWS_V + R * k
                for a in range(49):
                    ins = nc.tensor.matmul(ps[:, m % 8, :].rearrange("p (r w) -> p r w", r=R), diag[:, 49 * (t % 2) + a, :],
                                           img(t)[:, r0 + a // 7:r0 + a // 7 + R, a % 7:a % 7 + W], start=(a == 0), stop=(a == 48))
                ins.then_inc(psum_done, 1)

        @block.vector
        def _(dve):
            V = nc.vector
            n = 0
            for t in range(NT):
                for i in range(3):
                    V.tensor_copy(img(t)[:, 3:67, i], img(t)[:, 3:67, 6 - i]).then_inc(chain, 1)
                    V.tensor_copy(img(t)[:, 3:67, 69 - i], img(t)[:, 3:67, 63 + i]).then_inc(chain, 1)
                    n += 2
                dve.wait_ge(chain, n)
                for i in range(3):
                    V.tensor_copy(img(t)[:, i, :], img(t)[:, 6 - i, :]).then_inc(chain, 1)
                    V.tensor_copy(img(t)[:, 69 - i, :], img(t)[:, 63 + i, :]).then_inc(chain, 1)
                    n += 2
                dve.wait_ge(chain, n)
            dve.wait_ge(biased, NT)
            m = 0
            for a in range(49):
                for t in range(NT):
                    o = xt[:, t, 0:VP].rearrange("p (r w) -> p r w", w=W)
                    if a:
                        dve.wait_ge(taps, NT * (a - 1) + t + 1)
                    V.scalar_tensor_tensor(out=o, in0=img(t)[:, a // 7:a // 7 + ROWS_V, a % 7:a % 7 + W], scalar=wts[:, t, a:a + 1],
                                           in1=o, op0=ALU.mult, op1=ALU.add).then_inc(taps, 1)
                if a % 5 == 4 and m < NT * NCH:
                    tail_add(nc, dve, ps, xt, m, NCH, VP, psum_done, added)
                    m += 1
            while m < NT * NCH:
                tail_add(nc, dve, ps, xt, m, NCH, VP, psum_done, added)
                m += 1


def tail_add(nc, dve, ps, xt, m, NCH, VP, psum_done, added):
    t, k = m // NCH, m % NCH
    x = xt[:, t, VP + k * PX:VP + (k + 1) * PX]
    dve.wait_ge(psum_done, m + 1)
    nc.vector.tensor_tensor(x, ps[:, m % 8, :], x, ALU.add).then_inc(added, 1)


def layouts(v):
    import numpy as np
    f = np.float32
    o = {"x": v["x"], "ident": np.eye(128, dtype=f)}

    def packed_rows(w):
        return w[0:128], np.concatenate([w[128:192], w[128:192]], 0)

    def packed_vec(w):
        return np.stack([w[0:128], w[0:128], np.concatenate([w[128:192], w[128:192]], 0)], 1)

    g = np.kron(np.eye(32), np.full((6, 6), 1.0 / 6.0)).astype(f)
    o["gmat"] = np.concatenate(packed_rows(g), 1)

    wq = v["L0_conv_w_qkv"].T
    wide = np.zeros((128, 3, QKV), f)
    wide[:, 0] = wq[0:128]
    wide[0:64, 1] = wq[128:192]
    wide[64:128, 2] = wq[128:192]
    o["wbase"] = wide
    dws = [v["L0_conv_w_dw3"][:, 0], v["L0_conv_w_dw5"][:, 0], v["L0_conv_w_dw7"][:, 0]]
    flat = np.concatenate([d.reshape(QKV, -1) for d in dws], 1)
    o["wt"] = flat[0:TCH].reshape(NTT, 128, NTAP).transpose(1, 0, 2).reshape(128, NTT * NTAP)
    wd = np.zeros((NSH, CG, NG, 7, 3, 2), f)
    for k in range(3):
        for g in range(P_GROUPS[k]):
            c0, n = TCH + 128 * k, P_GROUPS[k]
            ch = slice(c0 + g, c0 + CG * n, n)
            for s in range(NSH):
                for ph in range(2):
                    dx = s - ph - 3
                    for q, d in enumerate(dws):
                        r = KS[q] // 2
                        if abs(dx) <= r:
                            wd[s, :, G0[k] + g, 3 - r:4 + r, q, ph] = d[ch, :, dx + r]
    o["wd"] = wd.reshape(128, NG * 7 * 6)
    o["mask16"] = np.concatenate([np.eye(CG, dtype=f)] * NSH, 0)
    pT = v["L0_conv_w_pconv"].T
    tiles = [pT[k * QKV + 128 * t:k * QKV + 128 * t + 128] for t in range(4) for k in range(3)]
    c = QKV - 64
    tiles.append(np.concatenate([pT[c:c + 64], np.zeros((64, QKV), f)], 0))
    tiles.append(np.concatenate([pT[QKV + c:QKV + c + 64], pT[2 * QKV + c:2 * QKV + c + 64]], 0))
    o["pw"] = np.stack(tiles, 1)
    o["wproj0"] = v["L0_conv_w_proj"].T.reshape(2, HC, C).transpose(1, 0, 2)
    o["head_mask"] = np.kron(np.eye(HH), np.ones((HD, 1))).astype(f)
    o["temperature_rows"] = np.repeat(v["L0_conv_temperature"].reshape(2, HH), HD, 1).T
    o["scales_rows"] = np.broadcast_to(v["L0_conv_attn_scales"], (HC, 3))
    o["tri"] = np.broadcast_to(np.tril(np.ones((HD, HD), f), -1), (HC, HD, HD))

    w1 = v["L1_conv_w_qkv"]
    o["w1qk"] = w1[0:2 * C].T
    o["w1v"] = w1[2 * C:].reshape(2, HC, C).transpose(1, 0, 2)

    w2 = v["L2_conv_W_proj"].T
    z = np.zeros((C, N_STATE), f)
    bm, cm = w2[:, 2 * C:2 * C + N_STATE], w2[:, 2 * C + N_STATE:]
    w2p = np.concatenate([w2[:, 0:2 * C], bm, z, z, bm, cm, z, z, cm], 1)
    o["w2a"], o["w2c"] = packed_rows(w2p)
    for n, m in enumerate((bm, cm)):
        c0 = 2 * C + 64 * n
        o["w2c"][:, c0:c0 + 64] = 0
        o["w2c"][0:64, c0:c0 + N_STATE] = m[128:192]
        o["w2c"][64:128, c0 + N_STATE:c0 + 2 * N_STATE] = m[128:192]
    o["wo2a"], o["wo2c"] = packed_rows(v["L2_conv_W_out"].T)
    bp = v["L2_conv_b_proj"]
    five = np.stack([bp[0:C], bp[C:2 * C], v["L2_conv_dt_bias"], v["L2_conv_D"], v["L2_conv_b_out"]], 1)
    o["cols2"] = packed_vec(five).reshape(128, 15)
    bb, cb = bp[2 * C:2 * C + N_STATE], bp[2 * C + N_STATE:]
    o["bcbias2"] = np.concatenate([bb, bb, cb, cb]).reshape(64, 1)
    o["alog2"] = packed_vec(v["L2_conv_A_log"])
    sel = np.zeros((3, 32, NT, N_STATE, 128), f)
    for n in range(N_STATE):
        sel[:, n, 0, n, :] = 1
        sel[:, 16 + n, 1, n, :] = 1
        sel[:, n, 2, n, 0:64] = 1
        sel[:, 16 + n, 2, n, 64:128] = 1
    o["sel2"] = sel.reshape(96, NT * N_STATE * 128)
    o["w3"] = packed_vec(v["L3_conv_w"].reshape(C, 49))
    o["b3"] = packed_vec(v["L3_conv_b"])
    return o


def kernel(**inputs):
    import numpy as np
    import concourse.bacc as bacc
    from concourse.bass_utils import run_bass_kernel_spmd

    nc = bacc.Bacc("TRN2", target_bir_lowering=False, num_devices=1)
    arrays, aps = {}, {}
    for name, a in layouts({k: np.asarray(a) for k, a in inputs.items()}).items():
        a = np.ascontiguousarray(a)
        arrays[f"in_{name}"] = a
        aps[name] = nc.dram_tensor(f"in_{name}", a.shape, mybir.dt.from_np(a.dtype), kind="ExternalInput").ap()
    res = nc.dram_tensor("out_0", (B, C, H, W), F32, kind="ExternalOutput").ap()
    build(nc, aps, res)
    r = run_bass_kernel_spmd(nc, [arrays], core_ids=[0])
    return r.results[0]["out_0"]
```

```python
import concourse.bass as bass
from concourse import mybir
from contextlib import ExitStack

F32 = mybir.dt.float32
BF16 = mybir.dt.bfloat16
F16 = mybir.dt.float16
ALU = mybir.AluOpType
ACT = mybir.ActivationFunctionType
AX = mybir.AxisListType.X

B, C, H, W = 2, 192, 64, 64
HW = H * W
HC = C // 2
QKV = 3 * C
HD = 24
HH = HC // HD
EPS_GN = 1e-5
BH = 2 * B

NT = 3

NTT, TCH = 2, 192
CG = 8
NSH = 8
NO = 4
P_GROUPS = [16, 16, 16]
G0 = [0, 16, 32]
NG = sum(P_GROUPS)
NQ = 3 * 2 * 2
MG = NQ * CG
R = 8
NS = H // R
RB = R + 6
PADW = W + 6
PW2 = PADW // 2
PX = R * W
PQ = R * W // 4
GW = (RB // 2 - 1) * PW2 + W // 2
KS = [3, 5, 7]
TAPS = [k * k for k in KS]
NTAP = sum(TAPS)
KT = 14
OPS = NTT * NTAP

N_STATE = 16
CH = 1024
VECTOR_STATES = (5, 11)

ROWS_V = 24
PH, CP = 4, 32
G3 = (H - ROWS_V) // PH
NU = B * C // CP
TW = 3 * 7
ADD_FROM, ADD_EVERY = 7, 2


def depthwise_plan():
    def chain(src, ktile, taps):
        return [(src, ktile, n == 0, dy, dx, w) for n, (dy, dx, w) in enumerate(taps)]

    def tile(t):
        cs, w0 = [], 0
        for k in range(3):
            s, p = KS[k], KS[k] // 2
            cs.append(chain(("T", t), 3 * t + k,
                            [(3 - p + a, 3 - p + b, t * NTAP + w0 + a * s + b) for a in range(s) for b in range(s)]))
            w0 += TAPS[k]
        return cs[0] + cs[1], cs[2]

    def merge(a, b):
        out = []
        for n in range(max(len(a), len(b))):
            out += a[n:n + 1] + b[n:n + 1]
        return out

    return merge(*tile(0)) + merge(*tile(1))


PLAN = depthwise_plan()
LAST = {}
PREV = []
for _n, _o in enumerate(PLAN):
    PREV.append(LAST.get(_o[1], 0))
    LAST[_o[1]] = _n + 1


class Arena:

    def __init__(self, mem, size):
        self.mem, self.size, self.at = mem, size, 0

    def take(self, *dims):
        n = 1
        for d in dims:
            n *= d
        v = self.mem[:, self.at:self.at + n]
        self.at += n
        assert self.at <= self.size, (self.at, self.size)
        if len(dims) == 2:
            v = v.rearrange("p (a b) -> p a b", a=dims[0])
        if len(dims) == 3:
            v = v.rearrange("p (a b c) -> p a b c", a=dims[0], b=dims[1])
        return v

    def take16(self, *dims, dt=BF16):
        n = 1
        for d in dims:
            n *= d
        v = self.mem[:, self.at:self.at + n // 2].bitcast(dt)
        self.at += n // 2
        assert self.at <= self.size
        if len(dims) == 2:
            v = v.rearrange("p (a b) -> p a b", a=dims[0])
        if len(dims) == 3:
            v = v.rearrange("p (a b c) -> p a b c", a=dims[0], b=dims[1])
        return v


def pieces(t):
    if t < 2:
        return [(0, t, 0, 128)]
    return [(0, 0, 128, 64), (64, 1, 128, 64)]


def linear(nc, out, wa, wc, o0, t, src, n0, n):
    last = None
    if t < 2:
        lo = 64 * t
        nc.tensor.matmul(out, wa[:, o0:o0 + 128], src[:, t, n0:n0 + n], start=True, stop=False)
        return nc.tensor.matmul(out, wc[lo:lo + 64, o0:o0 + 128], src[lo:lo + 64, 2, n0:n0 + n], start=False, stop=True)
    for b in range(B):
        lo = 64 * b
        nc.tensor.matmul(out[lo:lo + 64], wa[:, o0 + 128:o0 + 192], src[:, b, n0:n0 + n], start=True, stop=False)
        last = nc.tensor.matmul(out[lo:lo + 64], wc[lo:lo + 64, o0 + 128:o0 + 192], src[lo:lo + 64, 2, n0:n0 + n],
                                start=False, stop=True)
    return last


def build(nc, inp, out):
    with ExitStack() as ctx:
        SIZE = 53100
        mem = ctx.enter_context(nc.sbuf_tensor("mem", [128, SIZE], F32))
        ps = ctx.enter_context(nc.psum_tensor("ps", [128, 8, 512], F32))
        n_sem = [0]

        def sem(name):
            n_sem[0] += 1
            return ctx.enter_context(nc.semaphore(f"{name}_{n_sem[0]}"))

        sem.norm = ([sem("norm_x_loaded") for _ in range(NT)], sem("norm_consts"), sem("norm_moments"),
                    sem("norm_vector_chain"), sem("norm_averaged"), sem("norm_rooted"), sem("norm_var_ready"),
                    [sem("norm_tile_done") for _ in range(NT)])

        def dram(name, shape):
            return nc.dram_tensor(name, shape, F32).ap()

        base_t = dram("base_T", [B, TCH, H + 6, PADW])
        base_p = nc.dram_tensor("base_P", [B, 2, QKV - TCH, 4, (H + 6) // 2 * PW2], F16).ap()
        x2 = dram("x_after_1", [B, C, HW])
        xin = inp["x"].rearrange("b c h w -> b c (h w)")
        xout = out.rearrange("b c h w -> b c (h w)")

        ar = Arena(mem, SIZE)
        ident = ar.take(128)
        gacc = ar.take(BH, 3 * HC)
        attn_w = ar.take(BH, HC)
        keep = ar.at

        def fresh():
            a = Arena(mem, SIZE)
            a.at = keep
            return a

        layer0_base(nc, sem, fresh(), ps, inp, xin, ident, base_t, base_p)
        v_dram = dram("v_pixels", [B * NS, 128, 4 * C])
        layer0_conv(nc, sem, fresh(), ps, inp, base_t, base_p, gacc, v_dram)
        ar = fresh()
        xt = ar.take(NT, HW)
        keep = ar.at
        layer0_attention(nc, sem, fresh(), ps, inp, v_dram, ident, gacc, attn_w, xin, xt)
        layer1(nc, sem, fresh(), ps, inp, xt, x2, ident, gacc, attn_w)
        layer2(nc, sem, fresh(), ps, inp, xt, x2, ident)
        layer3(nc, sem, fresh(), ps, inp, xt, xout, ident, dram("lower_rows_padded", [B, C, H - ROWS_V + 8, PADW]),
               dram("lower_rows", [B, C, H - ROWS_V, W]))


def group_norm(nc, sem, ar, ps, inp, layer, ident, xt, x_dram=None, padded=None, dst=None):
    gm = ar.take(2 * 192)
    stats = ar.take(NT * 8, 6)
    mv = ar.take(NT, 2)
    sq = ar.take(NT, 1)
    gst = ar.take(NT, 2)
    var = ar.take(NT)
    msq = ar.take(NT)
    sd = ar.take(NT)
    rs = ar.take(NT)
    t1 = ar.take(NT)
    nb = ar.take(NT)
    (loaded, consts, stat_done, chain, averaged, rooted, ready, normed) = sem.norm
    steps = NT * 8 + NT + 1 + 4 + 7
    L = layer

    def dest(t):
        if padded is None:
            return (xt if dst is None else dst)[:, t, :]
        return padded[:, t * 4900:(t + 1) * 4900].rearrange("p (r w) -> p r w", r=70)[:, 3:67, 3:67]

    def source(t):
        if padded is None:
            return xt[:, t, :]
        return xt[:, t, :].rearrange("p (r w) -> p r w", r=H)

    with nc.Block() as block:
        @block.sync
        def _(sp):
            if x_dram is not None:
                for t in range(NT):
                    for p0, b, c0, n in pieces(t):
                        sp.dma_start(xt[p0:p0 + n, t, :], x_dram[b, c0:c0 + n, :]).then_inc(loaded[t], 16)
            sp.dma_start(ident, inp["ident"]).then_inc(consts, 16)
            sp.dma_start(gm, inp["gmat"]).then_inc(consts, 16)
        @block.vector
        def _(dve):
            n = [steps * L]

            def step(ins):
                ins.then_inc(chain, 1)
                n[0] += 1
                dve.wait_ge(chain, n[0])

            for t in range(NT):
                if x_dram is not None:
                    dve.wait_ge(loaded[t], 16 * len(pieces(t)))
                for k in range(8):
                    last = nc.vector.bn_stats(stats[:, t * 8 + k, :], xt[:, t, 512 * k:512 * k + 512])
                    last.then_inc(chain, 1)
                    n[0] += 1
            dve.wait_ge(chain, n[0])
            for t in range(NT):
                ins = nc.vector.bn_aggr(mv[:, t, :], stats[:, t * 8:t * 8 + 8, :].rearrange("p a b -> p (a b)"))
                ins.then_inc(chain, 1)
                n[0] += 1
            dve.wait_ge(chain, n[0])
            step(nc.vector.tensor_tensor(sq[:, :, 0], mv[:, :, 0], mv[:, :, 0], ALU.mult))
            nc.vector.tensor_tensor(mv[:, :, 1], mv[:, :, 1], sq[:, :, 0], ALU.add).then_inc(stat_done, 1)
            dve.wait_ge(averaged, L + 1)
            step(nc.vector.tensor_copy(gst, ps[:, 0:NT, 0:2]))
            step(nc.vector.tensor_tensor(msq, gst[:, :, 0], gst[:, :, 0], ALU.mult))
            step(nc.vector.tensor_tensor(var, gst[:, :, 1], msq, ALU.subtract))
            step(nc.vector.tensor_scalar(var, var, EPS_GN, None, ALU.add))
            nc.vector.tensor_copy(t1, var).then_inc(ready, 1)
            dve.wait_ge(rooted, L + 1)
            step(nc.vector.reciprocal(rs, sd))
            step(nc.vector.tensor_tensor(sd, rs, rs, ALU.mult))
            step(nc.vector.tensor_tensor(sd, sd, var, ALU.mult))
            step(nc.vector.tensor_scalar(sd, sd, -0.5, 1.5, ALU.mult, ALU.add))
            step(nc.vector.tensor_tensor(rs, rs, sd, ALU.mult))
            step(nc.vector.tensor_tensor(nb, gst[:, :, 0], rs, ALU.mult))
            step(nc.vector.tensor_scalar(nb, nb, -1.0, None, ALU.mult))
            nc.vector.tensor_scalar(dest(0), source(0), rs[:, 0:1], nb[:, 0:1], ALU.mult, ALU.add).then_inc(normed[0], 1)
            nc.vector.tensor_scalar(dest(1), source(1), rs[:, 1:2], nb[:, 1:2], ALU.mult, ALU.add).then_inc(normed[1], 1)

        @block.tensor
        def _(pe):
            pe.wait_ge(consts, 32 * (L + 1))
            pe.wait_ge(stat_done, L + 1)
            for t in range(NT):
                last = linear(nc, ps[:, t, 0:2], gm[:, 0:192], gm[:, 192:384], 0, t, mv, 0, 2)
            last.then_inc(averaged, 1)

        @block.scalar
        def _(act):
            act.wait_ge(ready, L + 1)
            nc.scalar.activation(sd, var, ACT.Sqrt).then_inc(rooted, 1)
            act.wait_ge(chain, steps * (L + 1))
            nc.scalar.activation(dest(2), source(2), ACT.Identity, bias=nb[:, 2:3],
                                 scale=rs[:, 2:3]).then_inc(normed[2], 1)


def layer0_base(nc, sem, ar, ps, inp, xin, ident, base_t, base_p):
    xn = ar.take(NT, HW)
    at = ar.at
    group_norm(nc, sem, ar, ps, inp, 0, ident, xn, x_dram=xin)
    ar.at = at
    NM = 5
    w = ar.take(3, QKV)
    st = ar.take(NM, R * PADW)
    zero = ar.take(3 * PADW)
    loaded = sem("base_weights")
    cleared = sem("base_borders_cleared")
    summed = [sem("base_in_psum") for _ in range(NM)]
    copied = [sem("base_in_sbuf") for _ in range(NM)]
    stored = [sem("base_stored") for _ in range(NM)]
    high_out = [sem("base_high_part") for _ in range(3)]
    z_stored = sem("base_zero_rows_stored")

    def width(m):
        return 64 if m == 1 else 128

    def first_channel(m):
        return [0, 128, TCH, TCH + 128, TCH + 256][m]

    def parts(m):
        return st[0:width(m), m, :].bitcast(F16).rearrange("p (q a r n) -> p q a r n", q=2, a=4, r=R // 2)

    def columns(m, par, a):
        n0 = 2 if par == 0 else 1
        x = ps[0:width(m), m, :].rearrange("p (r q n a) -> p a q r n", r=R // 2, q=2, a=2)
        return parts(m)[:, :, 2 * a + par, :, n0:n0 + W // 2], x[:, 1 - par]

    with nc.Block() as block:
        @block.sync
        def _(sp):
            sp.dma_start(w, inp["wbase"]).then_inc(loaded, 16)
            sp.wait_ge(cleared, 1)
            n = 0
            for b in range(B):
                for r0 in (0, H + 3):
                    for t in range(2):
                        sp.dma_start(base_t[b, 128 * t:128 * t + width(t), r0:r0 + 3, :].rearrange("c r w -> c (r w)"),
                                     zero[0:width(t)]).then_inc(z_stored, 16)
                        n += 1
                    for k in range(3):
                        m = CG * P_GROUPS[k]
                        for q in range(2):
                            first = (r0 + 1 - q) // 2
                            rows = (r0 + 3 + 1 - q) // 2 - first
                            sp.dma_start(base_p[b, q, 128 * k:128 * k + m, :, first * PW2:(first + rows) * PW2],
                                         zero.bitcast(F16)[0:m, 0:4 * rows * PW2].rearrange("p (a n) -> p a n", a=4)).then_inc(z_stored, 16)
                            n += 1
            for m in range(NM):
                sp.sem_inc(stored[m], 16 if m < 2 else 32)
            for b in range(B):
                with sp.Fori(0, NS) as s:
                    for m in range(NM):
                        sp.wait_ge(copied[m], s + NS * b + 2)
                        if m < 2:
                            sp.dma_start(base_t[b, 128 * m:128 * m + width(m), bass.ds(3 + s * R, R), :].rearrange("c r w -> c (r w)"),
                                         st[0:width(m), m, :]).then_inc(stored[m], 16)
                        else:
                            c0 = 128 * (m - 2)
                            for q in range(2):
                                sp.dma_start(base_p[b, 1 - q, c0:c0 + width(m), :, bass.ds((s * (R // 2) + 1 + q) * PW2, R // 2 * PW2)],
                                             parts(m)[:, q].rearrange("p a r n -> p a (r n)")).then_inc(stored[m], 16)
            for m in range(NM):
                sp.wait_ge(stored[m], (16 if m < 2 else 32) * (B * NS + 1))
            sp.wait_ge(z_stored, 16 * n)

        @block.tensor
        def _(pe):
            pe.wait_ge(loaded, 16)
            for b in range(B):
                with pe.Fori(0, NS) as s:
                    for m in range(NM):
                        out = ps[0:width(m), m, :]
                        pe.wait_ge(copied[m], s + NS * b + 1)
                        pe.nop(nofuse=True)
                        nc.tensor.matmul(out, w[:, 0, first_channel(m):first_channel(m) + width(m)], xn[:, b, bass.ds(s * PX, PX)], start=True, stop=False)
                        nc.tensor.matmul(out, w[:, 1 + b, first_channel(m):first_channel(m) + width(m)], xn[:, 2, bass.ds(s * PX, PX)],
                                         start=False, stop=True).then_inc(summed[m], 1)

        @block.scalar
        def _(act):
            act.wait_ge(cleared, 2)
            for b in range(B):
                with act.Fori(0, NS) as s:
                    i = s + NS * b
                    for m in (2, 3, 4):
                        act.wait_ge(summed[m], i + 1)
                        act.wait_ge(stored[m], 32 * (i + 1))
                        for par in range(2):
                            d, x = columns(m, par, 0)
                            ins = nc.scalar.copy(d, x)
                        ins.then_inc(high_out[m - 2], 1)

        @block.vector
        def _(dve):
            nc.vector.memset(zero, 0.0).then_inc(cleared, 1)
            nc.vector.memset(st, 0.0).then_inc(cleared, 1)
            dve.wait_ge(cleared, 2)
            for m in range(NM):
                dve.sem_inc(copied[m], 1)
            for b in range(B):
                with dve.Fori(0, NS) as s:
                    i = s + NS * b
                    for m in (0, 1):
                        dve.wait_ge(summed[m], i + 1)
                        dve.wait_ge(stored[m], 16 * (i + 1))
                        nc.vector.tensor_copy(st[0:width(m), m, :].rearrange("p (r w) -> p r w", r=R)[:, :, 3:3 + W],
                                              ps[0:width(m), m, :].rearrange("p (r w) -> p r w", r=R)).then_inc(copied[m], 1)
                    for m in (2, 3, 4):
                        dve.wait_ge(high_out[m - 2], i + 1)
                        for par in range(2):
                            hi, x = columns(m, par, 0)
                            ins = nc.vector.tensor_tensor(columns(m, par, 1)[0], x, hi, ALU.subtract)
                        ins.then_inc(copied[m], 1)


def layer0_conv(nc, sem, ar, ps, inp, base_t, base_p, gacc, v_dram):
    wt = ar.take(NTT * NTAP)
    pw = ar.take16(2, KT, QKV, dt=F16)
    diag = ar.take16(NG * NO, 2, MG, dt=F16)
    mask8 = ar.take(CG)
    pw_at = ar.at
    gbuf = ar.take16(2 * P_GROUPS[0], 2, RB // 2 * PW2, dt=F16)
    RT = [R, R // 2]
    tbuf = [ar.take(RT[0] + 6, PADW), ar.take(RT[1] + 6, PADW)]
    stage = Arena(ar.mem, ar.at)
    stage.at = pw_at
    pw32 = stage.take(KT, QKV)
    dt_ = [ar.take(3, RT[0] * W), ar.take(3, RT[1] * W)]
    tq = ar.take16(2, 3, PX, dt=F16)
    t1s = ar.take16(3, 2, PX // 2, dt=F16)
    before_loop = ar.at
    t1q = ar.take16(2, 2, PX, dt=F16)
    dp = ar.take16(3, 2, 3 * PX, dt=F16)
    stg = ar.take16(2, P_GROUPS[0], PQ, dt=F16)
    qk = ar.take(4, 2 * C)
    quad = qk.rearrange("p a c -> p (a c)")[:, 0:2 * PX].rearrange("p (u g n) -> p u g n", u=2, g=4)
    vst = ar.take(4, C)
    gtmp = ar.take(2, 3 * HC)
    NW = NG * NO * NQ
    at = ar.at
    ar.at = before_loop
    dp1 = ar.take(7 * NW // 2)
    assert ar.at <= at
    ar.at = at
    wd, wd_hi, wd_lo, wd16 = dp1[:, 0:NW], dp1[:, NW:2 * NW], dp1[:, 2 * NW:3 * NW], dp1[:, 3 * NW:3 * NW + NW // 2].bitcast(F16)

    d_dram = [nc.dram_tensor(f"depthwise_P{k}", [2, MG, P_GROUPS[k], PQ], F16).ap() for k in range(3)]

    psa = ps[:, 0:4, :]
    psv = ps[:, 4, 0:256].rearrange("p (a c) -> p a c", a=4)
    psg = [ps[:, 5 + n, :].rearrange("p (g n) -> p g n", g=4) for n in range(2)]
    psk = ps[:, 4, 256:256 + 2 * HC]
    psq = ps[:, 7, :]

    weights = sem("l0_weights_loaded")
    diag_ready = sem("l0_diagonals_ready")
    wd_split = sem("l0_P_weights_split")
    gcleared = sem("l0_gram_cleared")
    t_loaded = [sem("l0_T_loaded") for _ in range(NTT)]
    p_loaded = [sem("l0_P_loaded") for _ in range(3)]
    dw_ops = sem("l0_vector_depthwise_ops")
    t_copied = sem("l0_T_results_copied")
    t_used = sem("l0_T0_results_used")
    t1_moved = sem("l0_T1_results_moved")
    gdw_sum = sem("l0_group_in_psum")
    gdw_out = sem("l0_group_in_sbuf")
    gdw_split = sem("l0_group_split")
    t1_split = sem("l0_T1_results_split")
    pw_loaded = sem("l0_pconv_weights_loaded")
    pw_split = sem("l0_pconv_weights_split")
    diag0_ready = sem("l0_diagonals_0_ready")
    d_stored = [sem("l0_P_result_stored") for _ in range(3)]
    d_loaded = [sem("l0_P_result_gathered") for _ in range(3)]
    acc_done = sem("l0_pconv_done")
    qkv_out = sem("l0_qkv_in_sbuf")
    v_stored = sem("l0_v_stored")
    gram_sum = sem("l0_gram_in_psum")
    gram_out = sem("l0_gram_in_sbuf")
    gram_add = sem("l0_gram_added")
    NQUAD = NG // 4
    halved = sem("l0_high_parts")

    def build_diag(eng, k, a):
        r0, n = NO * G0[k], NO * P_GROUPS[k]
        return eng.tensor_tensor(diag[:, r0:r0 + n, a, :].rearrange("p r (q c) -> p r q c", q=NQ),
                                 mask8.unsqueeze(1).unsqueeze(1).to_broadcast([128, n, NQ, CG]),
                                 (wd_hi, wd_lo)[a][:, NQ * r0:NQ * (r0 + n)].rearrange("p (r q) -> p r q", q=NQ).unsqueeze(3).to_broadcast([128, n, NQ, CG]),
                                 ALU.mult)

    with nc.Block() as block:
        @block.sync
        def _(sp):
            for dst, name in ((wt, "wt"), (wd, "wd"), (mask8, "mask8")):
                sp.dma_start(dst, inp[name]).then_inc(weights, 16)
            sp.dma_start(pw32, inp["pw"]).then_inc(pw_loaded, 16)

            def load_t(b, s, t):
                if t == 0:
                    sp.dma_start(tbuf[0], base_t[b, 0:128, bass.ds(s * R, RB), :]).then_inc(t_loaded[0], 16)
                    return
                for h in range(2):
                    sp.dma_start(tbuf[1][64 * h:64 * h + 64], base_t[b, 128:TCH, bass.ds(s * R + RT[1] * h, RT[1] + 6), :]
                                 ).then_inc(t_loaded[1], 16)

            def move_t1(i):
                sp.wait_ge(t1_split, 6 * (i + 2))
                for k, (slot, p0) in enumerate(((0, 0), (1, 0), (1, 64))):
                    for h in range(2):
                        sp.dma_start(t1q[p0:p0 + 64, slot].rearrange("p a (q n) -> p (a q) n", q=2)[:, :, 128 * h:128 * h + 128],
                                     t1s[64 * h:64 * h + 64, k].rearrange("p a (q n) -> p (a q) n", q=2)).then_inc(t1_moved, 16)

            def load_p(b, s, k):
                n = P_GROUPS[k]
                for q in range(2):
                    for sh in range(NSH):
                        p0 = CG * (NSH * q + sh)
                        src = base_p[b, q, 128 * k:128 * k + CG * n, sh % 2:4:2, bass.ds(s * (R // 2) * PW2 + sh // 2, GW)]
                        sp.dma_start(gbuf[p0:p0 + CG, n * (k % 2):n * (k % 2) + n, :, 0:GW].rearrange("c g h n -> c (g h) n"),
                                     src.rearrange("(c g) h n -> c (g h) n", g=n)).then_inc(p_loaded[k], 16)

            def exchange(i, k):
                n = P_GROUPS[k]
                sp.wait_ge(gdw_split, NQUAD * i + (G0[k] + n) // 4 + 2)
                sp.nop(nofuse=True)
                sp.wait_ge(d_loaded[k], 32 * (i + 1))
                sp.dma_start(d_dram[k].rearrange("a m g n -> m a (g n)"), stg[0:MG].rearrange("m a g n -> m a (g n)")
                             ).then_inc(d_stored[k], 16)
                sp.wait_ge(d_stored[k], 16 * (i + 2))
                for a in range(2):
                    sp.dma_start(dp[:, k, a, :].rearrange("p (q n) -> p q n", q=NQ),
                                 d_dram[k][a].rearrange("(q c) g n -> (c g) q n", q=NQ)).then_inc(d_loaded[k], 16)

            def strip(i, b, s, following):
                exchange(i, 0)
                load_p(b, s, 2)
                if following:
                    sp.wait_ge(dw_ops, OPS * (i + 1) + NTAP)
                    load_t(*following, 0)
                exchange(i, 1)
                if following:
                    load_p(*following, 1)
                exchange(i, 2)
                if following:
                    load_p(*following, 0)
                move_t1(i)
                if following:
                    load_t(*following, 1)
                sp.wait_ge(qkv_out, i + 2)
                sp.dma_start(v_dram[bass.ds(i, 1)].rearrange("o p n -> p (o n)"), vst.rearrange("p a c -> p (a c)")).then_inc(v_stored, 16)

            def body(b, s, last):
                i = s + NS * b
                nb, ns = b, s + 1
                strip(i, b, s, (nb, ns) if not last else None)

            for k in range(3):
                sp.sem_inc(d_loaded[k], 32)
                sp.sem_inc(d_stored[k], 16)
            sp.sem_inc(v_stored, 16)
            sp.wait_ge(pw_split, 2)
            for t in range(NTT):
                load_t(0, 0, t)
            for k in range(2):
                load_p(0, 0, k)
            for b in range(B):
                with sp.Fori(0, NS - 1) as s:
                    body(b, s, False)
                if b + 1 < B:
                    strip(NS * (b + 1) - 1, b, NS - 1, (b + 1, 0))
                else:
                    body(b, NS - 1, True)
            sp.wait_ge(v_stored, 16 * (B * NS + 1))
            for k in range(3):
                sp.wait_ge(d_stored[k], 16 * (B * NS + 1))

        @block.gpsimd
        def _(pool):
            nc.gpsimd.memset(gacc, 0.0).then_inc(gcleared, 1)
            pool.wait_ge(weights, 48)
            pool.wait_ge(wd_split, 3)
            for k in (1, 2):
                for a in range(2):
                    build_diag(nc.gpsimd, k, a).then_inc(diag_ready, 1)
            pool.wait_ge(gcleared, 1)
            pool.sem_inc(gram_add, 1)
            pool.sem_inc(t_copied, 3)
            pool.sem_inc(gdw_split, 2)

            def split_quad(i, u):
                g = 4 * u % G0[1]
                pool.wait_ge(gdw_out, NQUAD * i + u + 3)
                high, low = (stg[0:MG, a, g:g + 4, :] for a in range(2))
                nc.gpsimd.tensor_tensor(low, quad[0:MG, u % 2], high, ALU.subtract).then_inc(gdw_split, 1)

            def split_t(i, t, n):
                src = dt_[t][:, n, :].rearrange("p (r q w) -> p q r w", q=2, w=W)
                pool.wait_ge(dw_ops, OPS * (i + 1) + LAST[3 * t + n])
                if t == 0:
                    pool.wait_ge(t_used, i + 1)
                    parts, done = [tq[:, a, n, :] for a in range(2)], t_copied
                else:
                    pool.wait_ge(t1_moved, 16 * 6 * (i + 1))
                    parts, done = [t1s[:, n, a, :] for a in range(2)], t1_split
                high, low = (x.rearrange("p (q r w) -> p q r w", q=2, w=W) for x in parts)
                pool.nop(nofuse=True)
                nc.gpsimd.tensor_copy(high, src).then_inc(halved, 1)
                pool.wait_ge(halved, 6 * i + 3 * t + n + 1)
                nc.gpsimd.tensor_tensor(low, src, high, ALU.subtract).then_inc(done, 1 if t == 0 else 2)

            def strip(i, b, last=False):
                for u in range(2, 8):
                    split_quad(i, u)
                for n in range(3):
                    split_t(i, 0, n)
                for u in range(8, NQUAD):
                    split_quad(i, u)
                for n in range(3):
                    split_t(i, 1, n)
                if not last:
                    for u in range(2):
                        split_quad(i + 1, u)
                pool.wait_ge(gram_out, i + 2)
                nc.gpsimd.tensor_tensor(gacc[0:HC, 2 * b:2 * b + 2, :], gacc[0:HC, 2 * b:2 * b + 2, :],
                                        gtmp[0:HC], ALU.add).then_inc(gram_add, 1)
                pool.wait_ge(gram_add, i + 2)

            for u in range(2):
                split_quad(0, u)
            for b in range(B):
                with pool.Fori(0, NS - (b == B - 1)) as s:
                    strip(s + NS * b, b)
            strip(B * NS - 1, B - 1, True)

        @block.vector
        def _(dve):
            dve.sem_inc(dw_ops, OPS)
            dve.sem_inc(t1_moved, 16 * 6)
            dve.sem_inc(t1_split, 6)
            dve.wait_ge(weights, 48)
            nc.vector.tensor_copy(wd16, wd).then_inc(wd_split, 1)
            dve.wait_ge(wd_split, 1)
            nc.vector.tensor_copy(wd_hi, wd16).then_inc(wd_split, 1)
            dve.wait_ge(wd_split, 2)
            nc.vector.tensor_tensor(wd_lo, wd, wd_hi, ALU.subtract).then_inc(wd_split, 1)
            dve.wait_ge(wd_split, 3)
            for a in range(2):
                build_diag(nc.vector, 0, a).then_inc(diag0_ready, 1)
            dve.wait_ge(pw_split, 1)
            nc.vector.tensor_tensor(pw[:, 1], pw32, pw[:, 0], ALU.subtract).then_inc(pw_split, 1)
            with dve.Fori(0, B * NS) as i:
                for n, (src, ktile, first, r0, c0, w) in enumerate(PLAN):
                    t = src[1]
                    if n == NTAP * t:
                        dve.wait_ge(t_loaded[t], (16 if t == 0 else 32) * (i + 1))
                        if t == 0:
                            dve.wait_ge(t_copied, 3 * (i + 1))
                        else:
                            dve.wait_ge(t1_split, 6 * i + 6)
                    x = tbuf[t][:, r0:r0 + RT[t], c0:c0 + W]
                    o = dt_[t][:, ktile - 3 * t, :].rearrange("p (r w) -> p r w", w=W)
                    if first:
                        ins = nc.vector.tensor_scalar(o, x, wt[:, w:w + 1], None, ALU.mult)
                    else:
                        dve.wait_ge(dw_ops, OPS * (i + 1) + PREV[n])
                        ins = nc.vector.scalar_tensor_tensor(out=o, in0=x, scalar=wt[:, w:w + 1], in1=o, op0=ALU.mult, op1=ALU.add)
                    ins.then_inc(dw_ops, 1)

        @block.scalar
        def _(act):
            act.sem_inc(gdw_out, 2)
            act.wait_ge(pw_loaded, 16)
            nc.scalar.copy(pw[:, 0], pw32).then_inc(pw_split, 1)
            act.sem_inc(gram_out, 1)
            act.sem_inc(qkv_out, 1)

            def quad_copy(i, u):
                act.wait_ge(gdw_sum, NQUAD * i + u + 1)
                act.wait_ge(gdw_split, NQUAD * i + u + 1)
                nc.scalar.copy(quad[0:MG, u % 2], psg[u % 2][0:MG])
                g = 4 * u
                k = g // G0[1]
                if g == G0[k]:
                    if k:
                        act.wait_ge(d_stored[k - 1], 16 * (i + 2))
                    else:
                        act.wait_ge(d_stored[2], 16 * (i + 1))
                nc.scalar.copy(stg[0:MG, 0, g - G0[k]:g - G0[k] + 4, :], psg[u % 2][0:MG]).then_inc(gdw_out, 1)

            def body(i, last):
                for u in range(2, NQUAD):
                    quad_copy(i, u)
                if not last:
                    for u in range(2):
                        quad_copy(i + 1, u)
                act.wait_ge(acc_done, i + 1)
                act.wait_ge(gdw_split, NQUAD * (i + 1) + (2 if last else 4))
                nc.scalar.copy(qk, psa[:, :, 0:2 * C])
                act.wait_ge(v_stored, 16 * (i + 1))
                nc.scalar.copy(vst[:, :, 0:128], psa[:, :, 2 * C:512])
                nc.scalar.copy(vst[:, :, 128:192], psv).then_inc(qkv_out, 1)
                act.wait_ge(gram_sum, i + 1)
                act.wait_ge(gram_add, i + 1)
                nc.scalar.copy(gtmp[0:HC, :, 0:2 * HC], psq[0:HC, 0:4 * HC].rearrange("p (a c) -> p a c", a=2))
                nc.scalar.copy(gtmp[0:HC, :, 2 * HC:3 * HC], psk[0:HC].rearrange("p (a c) -> p a c", a=2)
                               ).then_inc(gram_out, 1)

            act.wait_ge(diag_ready, 4)
            for u in range(2):
                quad_copy(0, u)
            with act.Fori(0, B * NS - 1) as i:
                body(i, False)
            body(B * NS - 1, True)

        @block.tensor
        def _(pe):
            pe.sem_inc(t_used, 1)

            def group(i, g):
                k = 0 if g < G0[1] else 1 if g < G0[2] else 2
                if g == G0[k]:
                    pe.wait_ge(p_loaded[k], 16 * 2 * NSH * (i + 1))
                if g % 4 == 0:
                    pe.wait_ge(gdw_out, NQUAD * i + g // 4 + 1)
                for o in range(NO):
                    for n, (a, xa) in enumerate(((0, 0), (1, 0), (0, 1))):
                        x = gbuf[:, g - G0[k] + P_GROUPS[0] * (k % 2), xa, :].rearrange("p (r m) -> p r m", r=RB // 2)[:, o:o + R // 2, 0:W // 2]
                        ins = nc.tensor.matmul(psg[g // 4 % 2][0:MG, g % 4, :].rearrange("p (r m) -> p r m", r=R // 2),
                                               diag[:, NO * g + o, a, :], x,
                                               start=(o == 0 and n == 0), stop=(o == NO - 1 and n == 2), skip_group_check=True)
                if g % 4 == 3:
                    ins.then_inc(gdw_sum, 1)

            def pconv(k, rows, block_of, first=False, last=False):
                for p in range(4):
                    for n, (a, wa) in enumerate(((0, 0), (0, 1), (1, 0))):
                        d = block_of(a, p)
                        start, stop = first and n == 0, last and n == 2
                        nc.tensor.matmul(psa[:, p, :], d, pw[0:rows, wa, k, 0:512], start=start, stop=stop)
                        ins = nc.tensor.matmul(psv[:, p, :], d, pw[0:rows, wa, k, 512:QKV],
                                               start=start and p == 0, stop=stop, skip_group_check=True)
                return ins

            def p_tile(i, k):
                pe.wait_ge(d_loaded[k], 32 * (i + 2))
                for n in range(3):
                    pconv(3 + 3 * k + n, 128, lambda a, p: dp[:, k, a, PX * n + 128 * p:PX * n + 128 * p + 128], first=(k == 0 and n == 0))

            def by_rows(v):
                return lambda a, p: v[:, a, :].rearrange("p (q n a) -> p q a n", q=2, a=2)[:, p // 2, p % 2]

            def t0_tile(i):
                for k in range(3):
                    pe.wait_ge(t_copied, 3 * (i + 1) + k + 1)
                    ins = pconv(k, 128, by_rows(tq[:, :, k, :]))
                ins.then_inc(t_used, 1)

            def t1_tile(i):
                pe.wait_ge(t1_moved, 16 * 6 * (i + 2))
                pconv(12, 64, by_rows(t1q[0:64, 0]))
                return pconv(13, 128, by_rows(t1q[:, 1]), last=True)

            def gram(i):
                pe.wait_ge(qkv_out, i + 2)
                for p in range(4):
                    for h in range(2):
                        sel = qk[:, p, :].rearrange("p (a c) -> p a c", a=2)[:, :, h * HC:(h + 1) * HC]
                        nc.tensor.matmul(psq[0:HC, 2 * HC * h:2 * HC * (h + 1)].rearrange("p (a c) -> p a c", a=2),
                                         qk[:, p, h * HC:(h + 1) * HC], sel,
                                         start=(p == 0 and h == 0), stop=(p == 3), skip_group_check=True)
                        ks = qk[:, p, C + h * HC:C + (h + 1) * HC]
                        ins = nc.tensor.matmul(psk[0:HC, HC * h:HC * (h + 1)], ks, ks,
                                               start=(p == 0 and h == 0), stop=(p == 3), skip_group_check=True)
                ins.then_inc(gram_sum, 1)

            def body(i, last):
                for g in range(16, G0[2]):
                    group(i, g)
                pe.wait_ge(qkv_out, i + 1)
                pe.wait_ge(gram_out, i + 1)
                p_tile(i, 0)
                for g in range(G0[2], NG):
                    group(i, g)
                t0_tile(i)
                p_tile(i, 1)
                p_tile(i, 2)
                t1_tile(i).then_inc(acc_done, 1)
                if not last:
                    for g in range(16):
                        group(i + 1, g)
                gram(i)

            pe.wait_ge(weights, 48)
            pe.wait_ge(diag0_ready, 2)
            for g in range(16):
                group(0, g)
            pe.wait_ge(diag_ready, 4)
            pe.wait_ge(pw_split, 2)
            with pe.Fori(0, B * NS - 1) as i:
                body(i, False)
            body(B * NS - 1, True)

def layer0_attention(nc, sem, ar, ps, inp, v_dram, ident, gacc, attn_w, xin, xt):
    x_loaded = sem("l0_x_loaded")
    attention(nc, sem, ar, ps, inp, ident, gacc, attn_w, 0, (xt, xin, x_loaded))

    NV = 4
    vl = ar.take(NV, 4 * C)
    m0 = ar.take(BH, C)
    wp = ar.take(2, C)
    vs = ar.take(4, PX)
    wp_loaded = sem("l0_wproj_loaded")
    m_sum = sem("l0_m_in_psum")
    m_out = sem("l0_m_in_sbuf")
    v_loaded = [sem("l0_v_loaded") for _ in range(NV)]
    v_sum = sem("l0_v_transposed")
    v_out = sem("l0_v_in_sbuf")
    o_sum = sem("l0_out_in_psum")
    o_add = sem("l0_out_added")

    with nc.Block() as block:
        @block.sync
        def _(sp):
            sp.dma_start(wp[0:HC], inp["wproj0"]).then_inc(wp_loaded, 16)
            for i in range(B * NS):
                if i >= NV:
                    sp.wait_ge(v_sum, i - NV + 1)
                sp.dma_start(vl[:, i % NV, :], v_dram[i]).then_inc(v_loaded[i % NV], 16)

        @block.tensor
        def _(pe):
            pe.wait_ge(wp_loaded, 16)
            for bh in range(BH):
                ins = nc.tensor.matmul(ps[0:HC, bh, 0:C], attn_w[0:HC, bh, :], wp[0:HC, bh % 2, :], start=True, stop=True)
            ins.then_inc(m_sum, 1)
            pe.wait_ge(m_out, 1)
            for i in range(B * NS + 1):
                if i < B * NS:
                    if i >= 2:
                        pe.wait_ge(v_out, 2 * (i - 1))
                    pe.wait_ge(v_loaded[i % NV], 16 * (i // NV + 1))
                    for h in range(2):
                        for p in range(4):
                            ins = nc.tensor.transpose(ps[0:HC, 2 * (i % 2) + h, 128 * p:128 * p + 128],
                                                      vl[:, i % NV, C * p + HC * h:C * p + HC * h + HC], ident)
                    ins.then_inc(v_sum, 1)
                if i >= 1:
                    k = i - 1
                    b, bank = k // NS, 4 + 2 * (k % 2)
                    pe.wait_ge(v_out, 2 * (k + 1))
                    if k >= 2:
                        pe.wait_ge(o_add, 2 * (k - 1))
                    for out, c0, n in ((ps[:, bank, :], 0, 128), (ps[64 * b:64 * b + 64, bank + 1, :], 128, 64)):
                        for h in range(2):
                            ins = nc.tensor.matmul(out, m0[0:HC, 2 * b + h, c0:c0 + n], vs[0:HC, 2 * (k % 2) + h, :],
                                                   start=(h == 0), stop=(h == 1))
                    ins.then_inc(o_sum, 1)

        @block.scalar
        def _(act):
            act.wait_ge(m_sum, 1)
            nc.scalar.copy(m0[0:HC], ps[0:HC, 0:BH, 0:C]).then_inc(m_out, 1)
            for i in range(B * NS):
                act.wait_ge(v_sum, i + 1)
                if i >= 2:
                    act.wait_ge(o_sum, i - 1)
                for h in range(2):
                    k = 2 * (i % 2) + h
                    for q in range(2):
                        ins = nc.scalar.copy(vs[0:HC, k, :].rearrange("p (r q m a) -> p q a r m", r=R // 2, q=2, a=2)[:, q],
                                             ps[0:HC, k, :].rearrange("p (q a r m) -> p q a r m", q=2, a=2, r=R // 2)[:, q])
                    ins.then_inc(v_out, 1)

        @block.vector
        def _(dve):
            dve.wait_ge(x_loaded, 16 * 4)
            for i in range(B * NS):
                b, s, bank = i // NS, i % NS, 4 + 2 * (i % 2)
                dve.wait_ge(o_sum, i + 1)
                n0, lo = s * PX, 64 * b
                nc.vector.tensor_tensor(xt[:, b, n0:n0 + PX], ps[:, bank, :], xt[:, b, n0:n0 + PX], ALU.add).then_inc(o_add, 1)
                nc.vector.tensor_tensor(xt[lo:lo + 64, 2, n0:n0 + PX], ps[lo:lo + 64, bank + 1, :],
                                        xt[lo:lo + 64, 2, n0:n0 + PX], ALU.add).then_inc(o_add, 1)


def attention(nc, sem, ar, ps, inp, ident, gacc, attn_w, layer, load=None):
    at = ar.at
    tmp = ar.take(BH, HC)
    ssq = ar.take(2, BH)
    nrm = ar.take(2, BH)
    rcp = ar.take(2, BH)
    dg = ar.take(BH, HC)
    sc = ar.take(BH, HC)
    bm = ar.take(HH)
    a = ar.take(BH, HD)
    e = ar.take(BH, HD)
    mx = ar.take(BH)
    ones = ar.take(HC)
    temp = ar.take(2)
    scl = ar.take(3)
    tri = ar.take(HD, HD)
    cmp = ar.take(BH * HD, HD)
    eq = ar.take(BH * HD, HD)
    rank = ar.take(BH, HD)
    em = ar.take(BH, HD)
    se = ar.take(BH)
    wsum = ar.take(BH, HD)
    ar.at = at

    consts = sem(f"attn{layer}_consts")
    chain = sem(f"attn{layer}_chain")
    sums = sem(f"attn{layer}_square_sums")
    roots = sem(f"attn{layer}_roots")
    diag_k = sem(f"attn{layer}_k_diagonal")
    bcast = sem(f"attn{layer}_k_broadcast")
    centred = sem(f"attn{layer}_centred")
    exped = sem(f"attn{layer}_exp")
    P_ = slice(0, HC)

    def bc(v, shape):
        return v.to_broadcast(shape)

    with nc.Block() as block:
        @block.sync
        def _(sp):
            sp.dma_start(bm[P_], inp["head_mask"]).then_inc(consts, 16)
            sp.dma_start(temp[P_], inp["temperature_rows"]).then_inc(consts, 16)
            sp.dma_start(scl[P_], inp["scales_rows"]).then_inc(consts, 16)
            sp.dma_start(tri[P_], inp["tri"]).then_inc(consts, 16)
            if load is not None:
                for t in range(NT):
                    for p0, b, c0, n in pieces(t):
                        sp.dma_start(load[0][p0:p0 + n, t, :], load[1][b, c0:c0 + n, :]).then_inc(load[2], 16)

        @block.tensor
        def _(pe):
            pe.wait_ge(diag_k, 1)
            nc.tensor.matmul(ps[P_, 0, 0:BH * HC], ones[P_, :], dg[P_].rearrange("p a c -> p (a c)"),
                             start=True, stop=True).then_inc(bcast, 1)

        @block.scalar
        def _(act):
            act.wait_ge(sums, 1)
            nc.scalar.activation(nrm[P_], ssq[P_], ACT.Sqrt).then_inc(roots, 1)
            act.wait_ge(centred, 1)
            nc.scalar.activation(e[P_], em[P_], ACT.Exp).then_inc(exped, 1)

        @block.vector
        def _(dve):
            n = [0]

            def step(ins):
                ins.then_inc(chain, 1)
                n[0] += 1
                dve.wait_ge(chain, n[0])

            V = nc.vector
            dve.wait_ge(consts, 64)
            step(V.memset(ones[P_], 1.0))
            idb = bc(ident[P_, 0:HC].unsqueeze(1), [HC, BH, HC])
            for x, lo in ((0, 0), (1, 2 * HC)):
                step(V.tensor_tensor(tmp[P_], gacc[P_, :, lo:lo + HC], idb, ALU.mult))
                step(V.tensor_reduce(ssq[P_, x, :], tmp[P_], AX, ALU.add))
            V.tensor_copy(rcp[P_], ssq[P_]).then_inc(sums, 1)
            dve.wait_ge(roots, 1)
            step(V.tensor_scalar(nrm[P_], nrm[P_], 1e-12, None, ALU.max))
            step(V.reciprocal(rcp[P_], nrm[P_]))
            V.tensor_tensor(dg[P_], idb, bc(rcp[P_, 1, :].unsqueeze(2), [HC, BH, HC]), ALU.mult).then_inc(diag_k, 1)
            dve.wait_ge(bcast, 1)
            step(V.tensor_tensor(sc[P_], gacc[P_, :, HC:2 * HC], ps[P_, 0, 0:BH * HC].rearrange("p (a c) -> p a c", a=BH), ALU.mult))
            step(V.tensor_tensor(sc[P_].rearrange("p b (h j) -> p b h j", h=HH), sc[P_].rearrange("p b (h j) -> p b h j", h=HH),
                                 bc(bm[P_].unsqueeze(1).unsqueeze(3), [HC, BH, HH, HD]), ALU.mult))
            step(V.tensor_reduce(a[P_], sc[P_].rearrange("p b (h j) -> p b j h", h=HH), AX, ALU.add))
            step(V.tensor_tensor(a[P_], a[P_], bc(rcp[P_, 0, :].unsqueeze(2), [HC, BH, HD]), ALU.mult))
            if layer == 0:
                step(V.tensor_tensor(a[P_].rearrange("p (b h) j -> p b h j", b=B), a[P_].rearrange("p (b h) j -> p b h j", b=B),
                                     bc(temp[P_].unsqueeze(1).unsqueeze(3), [HC, B, 2, HD]), ALU.mult))
            else:
                step(V.tensor_scalar(a[P_], a[P_], 1.0 / float(HW) ** 0.5, None, ALU.mult))
            step(V.tensor_reduce(mx[P_], a[P_], AX, ALU.max))
            V.tensor_tensor(em[P_], a[P_], bc(mx[P_].unsqueeze(2), [HC, BH, HD]), ALU.subtract).then_inc(centred, 1)
            if layer == 0:
                for b in range(BH):
                    ai = bc(a[P_, b, :].unsqueeze(2), [HC, HD, HD])
                    aj = bc(a[P_, b, :].unsqueeze(1), [HC, HD, HD])
                    cb, eb = cmp[P_, b * HD:(b + 1) * HD, :], eq[P_, b * HD:(b + 1) * HD, :]
                    step(V.tensor_tensor(cb, aj, ai, ALU.is_gt))
                    step(V.tensor_tensor(eb, aj, ai, ALU.is_equal))
                    step(V.tensor_tensor(eb, eb, tri[P_], ALU.mult))
                    step(V.tensor_tensor(cb, cb, eb, ALU.add))
                step(V.tensor_reduce(rank[P_], cmp[P_].rearrange("p (b i) j -> p b i j", b=BH), AX, ALU.add))
            dve.wait_ge(exped, 1)
            parts = [HD // 2, HD * 2 // 3, HD * 3 // 4] if layer == 0 else [HD]
            for k, top in enumerate(parts):
                if layer == 0:
                    step(V.tensor_scalar(em[P_], rank[P_], float(top), None, ALU.is_lt))
                    step(V.tensor_tensor(em[P_], em[P_], e[P_], ALU.mult))
                else:
                    step(V.tensor_copy(em[P_], e[P_]))
                step(V.tensor_reduce(se[P_], em[P_], AX, ALU.add))
                step(V.reciprocal(se[P_], se[P_]))
                if layer == 0:
                    step(V.tensor_scalar(se[P_], se[P_], scl[P_, k:k + 1], None, ALU.mult))
                dst = wsum if k == 0 else em
                step(V.tensor_tensor(dst[P_], em[P_], bc(se[P_].unsqueeze(2), [HC, BH, HD]), ALU.mult))
                if k:
                    step(V.tensor_tensor(wsum[P_], wsum[P_], em[P_], ALU.add))
            for b in range(BH):
                step(V.tensor_tensor(attn_w[P_, b, :].rearrange("p (h j) -> p h j", h=HH),
                                     bc(wsum[P_, b, :].unsqueeze(1), [HC, HH, HD]),
                                     bc(bm[P_].unsqueeze(2), [HC, HH, HD]), ALU.mult))


def residual_block(nc, sem, ps, tag, xt, linear_of, x_from=None, x_to=None, xr=None, bias=None):
    NP = NT * 2
    loaded = [sem(f"{tag}_residual_loaded") for _ in range(2)]
    summed = sem(f"{tag}_sum_in_psum")
    added = sem(f"{tag}_added")
    stored = sem(f"{tag}_stored")

    with nc.Block() as block:
        @block.sync
        def _(sp):
            n_st = 0
            for i in range(NP):
                t, n0 = i // 2, (i % 2) * 2048
                if x_from is not None:
                    if i >= 2:
                        sp.wait_ge(added, 4 * (i - 1))
                    for p0, b, c0, n in pieces(t):
                        sp.dma_start(xr[p0:p0 + n, i % 2, :], x_from[b, c0:c0 + n, n0:n0 + 2048]).then_inc(loaded[i % 2], 16)
                if x_to is not None:
                    sp.wait_ge(added, 4 * (i + 1))
                    for p0, b, c0, n in pieces(t):
                        sp.dma_start(x_to[b, c0:c0 + n, n0:n0 + 2048], xt[p0:p0 + n, t, n0:n0 + 2048]).then_inc(stored, 16)
                        n_st += 1
            if n_st:
                sp.wait_ge(stored, 16 * n_st)

        @block.tensor
        def _(pe):
            for m in range(NP * 4):
                if m >= 8:
                    pe.wait_ge(added, m - 7)
                linear_of(ps[:, m % 8, :], m // 8, (m % 8) * 512).then_inc(summed, 1)

        @block.vector
        def _(dve):
            need = [0, 0]
            for m in range(NP * 4):
                i = m // 4
                if x_from is not None and m % 4 == 0:
                    need[i % 2] += 16 * len(pieces(i // 2))
                    dve.wait_ge(loaded[i % 2], need[i % 2])
                dve.wait_ge(summed, m + 1)
                o = xt[:, m // 8, (m % 8) * 512:(m % 8) * 512 + 512]
                x = o if x_from is None else xr[:, i % 2, (m % 4) * 512:(m % 4) * 512 + 512]
                if bias is None:
                    ins = nc.vector.tensor_tensor(o, ps[:, m % 8, :], x, ALU.add)
                else:
                    ins = nc.vector.scalar_tensor_tensor(out=o, in0=ps[:, m % 8, :], scalar=bias[:, m // 8:m // 8 + 1],
                                                         in1=x, op0=ALU.add, op1=ALU.add)
                ins.then_inc(added, 1)


def layer1(nc, sem, ar, ps, inp, xt_, x2, ident, gacc, attn_w):
    xn = ar.take(NT, HW)
    at = ar.at
    group_norm(nc, sem, ar, ps, inp, 1, ident, xt_, dst=xn)
    ar.at = at
    SRC = [0, 2, 1]
    NB = HW // 128
    xt = ar.take(2, 2 * C)
    xx = ar.take(B * 2, C)
    wqk = ar.take(2, 2 * C)
    tt = ar.take(B * 2, 2 * C)
    wv = ar.take(2, C)
    wload = sem("l1_weights")
    tsum = sem("l1_transposed")
    tout = sem("l1_transposed_out")
    xxsum = sem("l1_xx_sum")
    xxout = sem("l1_xx_out")
    tts = sem("l1_t_sum")
    tto = sem("l1_t_out")
    gsum = sem("l1_gram_sum")

    def parts(b):
        if b == 0:
            return [(0, 0, 0, 128), (1, 128, 128, 64)]
        return [(0, 256, 64, 128), (1, 192, 0, 64)]

    with nc.Block() as block:
        @block.sync
        def _(sp):
            sp.dma_start(wqk[:, 0, :], inp["w1qk"][0:128, :]).then_inc(wload, 16)
            sp.dma_start(wqk[0:64, 1, :], inp["w1qk"][128:192, :]).then_inc(wload, 16)
            sp.dma_start(wv[0:HC], inp["w1v"]).then_inc(wload, 16)

        @block.tensor
        def _(pe):
            for k in range(NB + 1):
                if k < NB:
                    if k >= 2:
                        pe.wait_ge(tout, k - 1)
                    for m, t in enumerate(SRC):
                        ins = nc.tensor.transpose(ps[:, k % 2, 128 * m:128 * m + 128], xn[:, t, 128 * k:128 * k + 128], ident)
                    ins.then_inc(tsum, 1)
                if k >= 1:
                    j = k - 1
                    pe.wait_ge(tout, j + 1)
                    for b in range(B):
                        for rb, x0, _, n in parts(b):
                            ins = nc.tensor.matmul(ps[0:n, 2 + rb, C * b:C * b + C], xt[:, j % 2, x0:x0 + n],
                                                   xt[:, j % 2, C * b:C * b + C],
                                                   start=(j == 0 and b == 0), stop=(j == NB - 1), skip_group_check=True)
                    if j == NB - 1:
                        ins.then_inc(xxsum, 1)
            pe.wait_ge(wload, 48)
            pe.wait_ge(xxout, 2)
            for b in range(B):
                for rb, _, c0, n in parts(b):
                    for kb in range(2):
                        kn = 64 if kb else 128
                        ins = nc.tensor.matmul(ps[0:n, 4 + 2 * b + rb, 0:2 * C], xx[0:kn, 2 * b + kb, c0:c0 + n],
                                               wqk[0:kn, kb, :], start=(kb == 0), stop=(kb == 1))
            ins.then_inc(tts, 1)
            pe.wait_ge(tto, 1)
            for b in range(B):
                for h in range(2):
                    for kb in range(2):
                        kn = 64 if kb else 128
                        t = tt[0:kn, 2 * b + kb, :]
                        nc.tensor.matmul(ps[0:HC, 2 * b + h, 0:2 * HC].rearrange("p (a c) -> p a c", a=2),
                                         wqk[0:kn, kb, h * HC:(h + 1) * HC],
                                         t.rearrange("p (a c) -> p a c", a=2)[:, :, h * HC:(h + 1) * HC],
                                         start=(kb == 0), stop=(kb == 1), skip_group_check=True)
                    for kb in range(2):
                        kn = 64 if kb else 128
                        ins = nc.tensor.matmul(ps[0:HC, 4 + 2 * b + h, 0:HC], wqk[0:kn, kb, C + h * HC:C + (h + 1) * HC],
                                               tt[0:kn, 2 * b + kb, C + h * HC:C + (h + 1) * HC],
                                               start=(kb == 0), stop=(kb == 1), skip_group_check=True)
            ins.then_inc(gsum, 1)

        @block.scalar
        def _(act):
            for k in range(NB):
                act.wait_ge(tsum, k + 1)
                nc.scalar.copy(xt[:, k % 2, :], ps[:, k % 2, 0:2 * C]).then_inc(tout, 1)
            act.wait_ge(xxsum, 1)
            nc.scalar.copy(xx.rearrange("p (b r) c -> p b r c", b=B)[:, :, 0, :],
                           ps[:, 2, 0:2 * C].rearrange("p (b c) -> p b c", b=B)).then_inc(xxout, 1)
            nc.scalar.copy(xx.rearrange("p (b r) c -> p b r c", b=B)[0:64, :, 1, :],
                           ps[0:64, 3, 0:2 * C].rearrange("p (b c) -> p b c", b=B)).then_inc(xxout, 1)
            act.wait_ge(tts, 1)
            nc.scalar.copy(tt.rearrange("p (b r) c -> p b r c", b=B)[:, :, 0, :],
                           ps[:, 4:8, 0:2 * C].rearrange("p (b r) c -> p b r c", b=B)[:, :, 0, :])
            nc.scalar.copy(tt.rearrange("p (b r) c -> p b r c", b=B)[0:64, :, 1, :],
                           ps[0:64, 4:8, 0:2 * C].rearrange("p (b r) c -> p b r c", b=B)[:, :, 1, :]).then_inc(tto, 1)
            act.wait_ge(gsum, 1)
            nc.scalar.copy(gacc[0:HC, :, 0:2 * HC], ps[0:HC, 0:4, 0:2 * HC])
            nc.scalar.copy(gacc[0:HC, :, 2 * HC:3 * HC], ps[0:HC, 4:8, 0:HC])

    ar.at = at + 2 * 2 * C + B * 2 * C + 2 * 2 * C + B * 2 * 2 * C + 2 * C
    attention(nc, sem, ar, ps, inp, ident, gacc, attn_w, 1)

    awt = ar.take(BH, HC)
    ma = ar.take(B, C)
    mc = ar.take(C)
    a_sum = sem("l1_attn_transposed")
    a_out = sem("l1_attn_out")
    m_sum = sem("l1_m_sum")
    m_out = sem("l1_m_out")
    with nc.Block() as block:
        @block.tensor
        def _(pe):
            for bh in range(BH):
                ins = nc.tensor.transpose(ps[0:HC, 0, bh * HC:(bh + 1) * HC], attn_w[0:HC, bh, :], ident[0:HC, 0:HC])
            ins.then_inc(a_sum, 1)
            pe.wait_ge(a_out, 1)
            for b in range(B):
                for h in range(2):
                    nc.tensor.matmul(ps[:, 1 + b, h * HC:(h + 1) * HC], wv[0:HC, h, 0:128], awt[0:HC, 2 * b + h, :],
                                     start=(h == 0), stop=True, skip_group_check=True)
                    ins = nc.tensor.matmul(ps[64 * b:64 * b + 64, 3 + b, h * HC:(h + 1) * HC], wv[0:HC, h, 128:192],
                                           awt[0:HC, 2 * b + h, :], start=(h == 0), stop=True, skip_group_check=True)
            ins.then_inc(m_sum, 1)

        @block.scalar
        def _(act):
            act.wait_ge(a_sum, 1)
            nc.scalar.copy(awt[0:HC], ps[0:HC, 0, 0:BH * HC].rearrange("p (a c) -> p a c", a=BH)).then_inc(a_out, 1)
            act.wait_ge(m_sum, 1)
            nc.scalar.copy(ma, ps[:, 1:3, 0:C])
            for b in range(B):
                nc.scalar.copy(mc[64 * b:64 * b + 64], ps[64 * b:64 * b + 64, 3 + b, 0:C]).then_inc(m_out, 1)

    def lin(out, t, n0):
        if t < 2:
            lo = 64 * t
            nc.tensor.matmul(out, ma[:, t, 0:128], xn[:, t, n0:n0 + 512], start=True, stop=False)
            return nc.tensor.matmul(out, mc[lo:lo + 64, 0:128], xn[lo:lo + 64, 2, n0:n0 + 512], start=False, stop=True)
        for b in range(B):
            lo = 64 * b
            nc.tensor.matmul(out[lo:lo + 64], ma[:, b, 128:192], xn[:, b, n0:n0 + 512], start=True, stop=False)
            ins = nc.tensor.matmul(out[lo:lo + 64], mc[lo:lo + 64, 128:192], xn[lo:lo + 64, 2, n0:n0 + 512],
                                   start=False, stop=True)
        return ins

    residual_block(nc, sem, ps, "l1", xt_, lin, x_to=x2)


def layer2(nc, sem, ar, ps, inp, xt, x2, ident):
    xn = xt
    at = ar.at
    group_norm(nc, sem, ar, ps, inp, 2, ident, xt)
    ar.at = at
    NP2 = 2 * C + 4 * 32
    y = ar.take(NT, HW)
    wa = ar.take(2 * C)
    wc = ar.take(2 * C)
    woa = ar.take(C)
    woc = ar.take(C)
    cols = ar.take(16)
    na = ar.take(NT, N_STATE)
    sel32 = ar.take(NT * N_STATE * 128 // 2)
    sel = sel32.bitcast(BF16).rearrange("p (a c) -> p a c", a=NT * N_STATE)
    bc3 = ar.take16(2, HW)
    hs = ar.take(N_STATE)
    z = ar.take(HW)
    dx = ar.take(HW)
    ring_at = ar.at
    wba = ar.take(NP2 - 2 * C)
    wbc = ar.take(NP2 - 2 * C)
    bias_s = ar.take(8)
    stage = ar.take(NT * N_STATE * 128)

    loaded = sem("l2_weights")
    selc = sem("l2_selector_ready")
    bcs = sem("l2_bc_sum")
    bch = sem("l2_bc_parts")
    bcv = sem("l2_bc_chain")
    moved = sem("l2_bc_moved")
    prep = sem("l2_prepared")

    scratch = Arena(ar.mem, at + 2 * HW)
    scratch.at = at
    parts = scratch.take16(3, HW)
    full = scratch.take(512)
    with nc.Block() as block:
        @block.sync
        def _(sp):
            for dst, src in ((wba, inp["w2a"][:, 2 * C:NP2]), (wbc, inp["w2c"][:, 2 * C:NP2]), (wa, inp["w2a"][:, 0:2 * C]),
                              (wc, inp["w2c"][:, 0:2 * C]), (woa, inp["wo2a"]), (woc, inp["wo2c"]), (cols[:, 0:15], inp["cols2"]),
                              (na, inp["alog2"]), (stage[0:96], inp["sel2"]), (bias_s[0:64, 0:1], inp["bcbias2"])):
                sp.dma_start(dst, src).then_inc(loaded, 16)
            sp.wait_ge(bcv, 5 * 8)
            for part in range(3):
                for x in range(2):
                    sp.dma_start(bc3[32 * part:32 * part + 32, x, :], parts[32 * x:32 * x + 32, part, :]).then_inc(moved, 16)
            sp.wait_ge(moved, 96)

        @block.tensor
        def _(pe):
            pe.wait_ge(loaded, 160)
            for k in range(8):
                if k >= 2:
                    pe.wait_ge(bch, k - 1)
                for b in range(B):
                    nc.tensor.matmul(ps[0:64, k % 2, :], wba[:, 64 * b:64 * b + 64],
                                     xn[:, b, 512 * k:512 * k + 512], start=(b == 0), stop=False)
                ins = nc.tensor.matmul(ps[0:64, k % 2, :], wbc[:, 0:64], xn[:, 2, 512 * k:512 * k + 512], start=False, stop=True)
                ins.then_inc(bcs, 1)

        @block.scalar
        def _(act):
            act.wait_ge(loaded, 160)
            nc.scalar.activation(na, na, ACT.Exp).then_inc(prep, 1)
            nc.scalar.copy(sel32.bitcast(BF16)[0:96], stage[0:96]).then_inc(selc, 1)

        @block.vector
        def _(dve):
            V = nc.vector
            dve.wait_ge(loaded, 160)
            dve.wait_ge(prep, 1)
            V.tensor_scalar(na, na, -1.0, None, ALU.mult).then_inc(prep, 1)
            for t in range(NT):
                V.tensor_tensor(cols[:, 5 * t + 1:5 * t + 2], cols[:, 5 * t + 1:5 * t + 2], cols[:, 5 * t + 2:5 * t + 3], ALU.add).then_inc(prep, 1)
            n = 0
            for k in range(8):
                s = slice(512 * k, 512 * k + 512)
                dve.wait_ge(bcs, k + 1)
                if k:
                    dve.wait_ge(bcv, 5 * k)
                V.tensor_scalar(full[0:64], ps[0:64, k % 2, :], bias_s[0:64, 0:1], None, ALU.add).then_inc(bch, 1)
                dve.wait_ge(bch, k + 1)
                for part in range(3):
                    if part:
                        dve.wait_ge(bcv, n)
                        V.tensor_tensor(full[0:64], full[0:64], parts[0:64, part - 1, s], ALU.subtract).then_inc(bcv, 1)
                        n += 1
                        dve.wait_ge(bcv, n)
                    V.tensor_copy(parts[0:64, part, s], full[0:64]).then_inc(bcv, 1)
                    n += 1

    ar.at = ring_at
    da = ar.take(2, CH)
    dbx = ar.take(2, CH)
    hh = ar.take(4, CH)
    cs = ar.take(2, CH)
    l2_sems = [sem(n) for n in ("l2_proj_sum", "l2_xin_out", "l2_delta_out", "l2_vector_chain", "l2_scalar_chain", "l2_b_broadcast",
                                "l2_c_broadcast", "l2_decay", "l2_input", "l2_scan", "l2_h_times_c_pool", "l2_h_times_c_vector",
                                "l2_c_copied", "l2_y_accumulated", "l2_state_carried", "l2_y_added")]
    for t in range(NT):
        layer2_tile(nc, l2_sems, ps, t, xn, y, wa, wc, cols, na, sel, bc3, hs, z, dx, da, dbx, hh, cs, ident)

    ar.at = ring_at
    xr = ar.take(2, 2048)

    def lin(out, t, n0):
        return linear(nc, out, woa, woc, 0, t, y, n0, 512)

    bo = cols[:, 0:15].rearrange("p (t k) -> p t k", t=NT)[:, :, 4]
    residual_block(nc, sem, ps, "l2", xt, lin, x_from=x2, xr=xr, bias=bo)


def layer2_tile(nc, sems, ps, t, xn, y, wa, wc, cols, na, sel, bc3, hs, z, dx, da, dbx, hh, cs, ident):
    NC = HW // 512
    psum_in, x_out, d_out, vch, ach = sems[0:5]
    bsum, csum, exp_done, dbx_done, scan_done, hc_pool, hc_vector, c_copied, ysum, carried, yadd = sems[5:]
    m0, j0 = N_STATE * (HW // CH) * t, (HW // CH) * t
    lg = [(da.rearrange("p a b -> p (a b)"), 0), (dbx.rearrange("p a b -> p (a b)"), 2 * CH)]

    with nc.Block() as block:
        @block.tensor
        def _(pe):
            for k in range(NC):
                for x in range(2):
                    if k >= 4:
                        pe.wait_ge(x_out if x == 0 else d_out, NC * t + k - 3)
                    linear(nc, ps[:, 2 * (k % 4) + x, :], wa, wc, C * x, t, xn, 512 * k, 512).then_inc(psum_in, 1)

        @block.scalar
        def _(act):
            for k in range(NC):
                s = slice(512 * k, 512 * k + 512)
                act.wait_ge(psum_in, 2 * NC * t + 2 * k + 2)
                nc.scalar.activation(z[:, s], ps[:, 2 * (k % 4) + 1, :], ACT.Identity, bias=cols[:, 5 * t + 1:5 * t + 2]
                                     ).then_inc(d_out, 1)
            act.wait_ge(d_out, NC * (t + 1))
            n = 6 * t
            for func, kw in ((ACT.Abs, {}), (ACT.Exp, dict(scale=-1.0)), (ACT.Ln, dict(bias=1.0))):
                for buf, c0 in lg:
                    src = z[:, c0:c0 + 2 * CH] if func == ACT.Abs else buf
                    if func != ACT.Abs:
                        act.wait_ge(ach, n - 1)
                    nc.scalar.activation(buf, src, func, **kw).then_inc(ach, 1)
                    n += 1

        @block.vector
        def _(dve):
            V = nc.vector
            for k in range(NC):
                s = slice(512 * k, 512 * k + 512)
                dve.wait_ge(psum_in, 2 * NC * t + 2 * k + 1)
                V.tensor_scalar(y[:, t, s], ps[:, 2 * (k % 4), :], cols[:, 5 * t:5 * t + 1], None, ALU.add).then_inc(x_out, 1)
            n = 6 * t
            for i, (buf, c0) in enumerate(lg):
                s = slice(c0, c0 + 2 * CH)
                dve.wait_ge(ach, 6 * t + 5 + i)
                V.scalar_tensor_tensor(out=z[:, s], in0=z[:, s], scalar=0.0, in1=buf, op0=ALU.max, op1=ALU.add).then_inc(vch, 1)
                n += 1
                dve.wait_ge(vch, n)
                dve.wait_ge(x_out, NC * (t + 1))
                V.tensor_tensor(dx[:, s], z[:, s], y[:, t, s], ALU.mult).then_inc(vch, 1)
                n += 1
                dve.wait_ge(vch, n)
                V.tensor_scalar(y[:, t, s], y[:, t, s], cols[:, 5 * t + 3:5 * t + 4], None, ALU.mult).then_inc(vch, 1)
                n += 1
            V.memset(hs, 0.0)

    N = N_STATE
    pb = [ps[:, 0:2, :], ps[:, 2:4, :]]
    pc = ps[:, 4:6, :]
    py = ps[:, 6:8, :]

    def halves(v):
        return v.rearrange("p (a c) -> p a c", a=2)

    pool_states = [n for n in range(N) if n not in VECTOR_STATES]

    def wait_times_c(eng, j, n):
        q, r = n // N, n % N
        done, states = (hc_vector, list(VECTOR_STATES)) if r in VECTOR_STATES else (hc_pool, pool_states)
        eng.wait_ge(done, len(states) * (j + j0 + q + 1) + states.index(r) + 1)

    with nc.Block() as block:
        @block.tensor
        def _(pe):
            def b_bcast(j, n):
                m = m0 + N * j + n
                pe.wait_ge(dbx_done, m + 1)
                for a in range(2):
                    ins = nc.tensor.matmul(pb[n % 2][:, a, :], sel[0:96, N * t + n, :], bc3[0:96, 0, bass.ds(j * CH + 512 * a, 512)],
                                           start=True, stop=True)
                ins.then_inc(bsum, 1)

            def c_bcast(j, n):
                pe.wait_ge(c_copied, m0 + N * j + n + 1)
                for a in range(2):
                    ins = nc.tensor.matmul(pc[:, a, :], sel[0:96, N * t + n, :], bc3[0:96, 1, bass.ds(j * CH + 512 * a, 512)],
                                           start=True, stop=True)
                ins.then_inc(csum, 1)

            def accumulate(j, n):
                wait_times_c(pe, j, n)
                if n == 0:
                    pe.wait_ge(yadd, j + (j0 + 1))
                for a in range(2):
                    ins = nc.tensor.matmul(py[:, a, :], ident, hh[:, n % 4, 512 * a:512 * a + 512],
                                           start=(n % N == 0), stop=(n % N == N - 1))
                ins.then_inc(ysum, 1)

            def chunk(j, first=False):
                b_bcast(j, 0)
                for n in range(N):
                    if n + 1 < N:
                        b_bcast(j, n + 1)
                    c_bcast(j, n)
                    if n >= 2 or not first:
                        accumulate(j, n - 2)

            chunk(0, first=True)
            with pe.Fori(1, HW // CH) as j:
                chunk(j)
            for n in (-2, -1):
                accumulate(HW // CH, n)

        @block.scalar
        def _(act):
            def keep_state(j, n):
                act.wait_ge(scan_done, m0 + N * j + n + 3)
                nc.scalar.copy(hs[:, n:n + 1], hh[:, n % 4, CH - 1:CH]).then_inc(carried, 1)

            with act.Fori(0, HW // CH) as j:
                for n in range(N):
                    act.wait_ge(scan_done, m0 + N * j + n + 1)
                    act.nop(nofuse=True)
                    nc.scalar.activation(da[:, n % 2, :], z[:, bass.ds(j * CH, CH)], ACT.Exp, scale=na[:, t, n:n + 1]
                                         ).then_inc(exp_done, 1)
                    if n >= 1:
                        keep_state(j, n - 1)
                    act.wait_ge(csum, m0 + N * j + n + 1)
                    wait_times_c(act, j, n - 2)
                    nc.scalar.copy(halves(cs[:, n % 2, :]), pc).then_inc(c_copied, 1)
                keep_state(j, N - 1)

        @block.gpsimd
        def _(pool):
            with pool.Fori(0, HW // CH) as j:
                for n in pool_states:
                    m = m0 + N * j + n
                    pool.wait_ge(carried, m + 3)
                    pool.wait_ge(c_copied, m + 2)
                    nc.gpsimd.tensor_tensor(hh[:, n % 4, :], hh[:, n % 4, :], cs[:, n % 2, :], ALU.mult).then_inc(hc_pool, 1)

        @block.vector
        def _(dve):
            V = nc.vector
            if t == 0:
                for s, k in ((dbx_done, 2), (scan_done, 2), (carried, 2), (ysum, 4), (c_copied, 1), (yadd, 1),
                             (hc_pool, len(pool_states)), (hc_vector, len(VECTOR_STATES))):
                    dve.sem_inc(s, k)

            def product(j, n):
                m = m0 + N * j + n
                dve.wait_ge(bsum, m + 1)
                dve.wait_ge(scan_done, m + 1)
                V.tensor_tensor(halves(dbx[:, n % 2, :]), pb[n % 2], halves(dx[:, bass.ds(j * CH, CH)]), ALU.mult).then_inc(dbx_done, 1)

            def scan(j, n):
                m = m0 + N * j + n
                dve.wait_ge(dbx_done, m + 3)
                dve.wait_ge(exp_done, m + 1)
                dve.wait_ge(ysum, m + 1)
                if n == 0:
                    dve.wait_ge(carried, m + 2)
                V.tensor_tensor_scan(hh[:, n % 4, :], da[:, n % 2, :], dbx[:, n % 2, :], hs[:, n:n + 1],
                                     ALU.mult, ALU.add).then_inc(scan_done, 1)

            def times_c(j, n):
                m = m0 + N * j + n
                dve.wait_ge(c_copied, m + 2)
                dve.wait_ge(carried, m + 3)
                V.tensor_tensor(hh[:, n % 4, :], hh[:, n % 4, :], cs[:, n % 2, :], ALU.mult).then_inc(hc_vector, 1)

            def add_y(j, s):
                dve.wait_ge(ysum, m0 + N * j + 4)
                V.tensor_tensor(s, py, s, ALU.add).then_inc(yadd, 1)

            def chunk(j, first=False):
                product(j, 0)
                for n in range(N):
                    if n + 1 < N:
                        product(j, n + 1)
                    scan(j, n)
                    if n - 1 in VECTOR_STATES:
                        times_c(j, n - 1)
                    if n == 1 and not first:
                        add_y(j, halves(y[:, t, bass.ds((j - 1) * CH, CH)]))

            chunk(0, first=True)
            with dve.Fori(1, HW // CH) as j:
                chunk(j)
            add_y(HW // CH, halves(y[:, t, HW - CH:HW]))


def layer3(nc, sem, ar, ps, inp, xt, xout, ident, pad_dram, low_dram):
    pad = ar.take(NT * 4900)
    at = ar.at
    group_norm(nc, sem, ar, ps, inp, 3, ident, xt, padded=pad)
    ar.at = at
    SLOTS, HG = 4, G3 // 2
    GI = G3 + 2
    NB = 2 * NU
    wts = ar.take(NT, 49)
    bias = ar.take(NT)
    biasp = ar.take(NU // B)
    wph = ar.take(NU // B, TW * CP * PH)
    pin = ar.take(SLOTS, GI * PADW)
    xs = ar.take(SLOTS, G3 * W)
    loaded = sem("l3_weights")
    w_first = sem("l3_matrices_first")
    w_rest = sem("l3_matrices_rest")
    chain = sem("l3_mirror_chain")
    zeroed = sem("l3_zeroed")
    spilled = sem("l3_spilled")
    unit_in = [sem("l3_unit_in") for _ in range(SLOTS)]
    unit_out = [sem("l3_unit_out") for _ in range(SLOTS)]
    psum_done = sem("l3_sum_in_psum")
    added = sem("l3_added")
    biased = sem("l3_biased")
    taps = sem("l3_taps")
    VP = ROWS_V * W

    def img(t):
        return pad[:, t * 4900:(t + 1) * 4900].rearrange("p (r w) -> p r w", r=70)

    def by_phase(rows):
        return rows.rearrange("c (g p) w -> c p g w", p=PH)

    with nc.Block() as block:
        @block.sync
        def _(sp):
            sp.dma_start(wts, inp["w3"]).then_inc(loaded, 16)
            sp.dma_start(bias, inp["b3"]).then_inc(loaded, 16)
            sp.dma_start(biasp, inp["b3p"]).then_inc(loaded, 16)
            sp.dma_start(wph[:, 0, :], inp["w3p"][:, 0, :]).then_inc(w_first, 16)
            for t in range(NT):
                for p0, b, c0, m in pieces(t):
                    sp.dma_start(low_dram[b, c0:c0 + m], xt[p0:p0 + m, t, VP:HW].rearrange("p (r w) -> p r w", w=W)).then_inc(spilled, 16)
            sp.wait_ge(chain, 12 * NT)
            for t in range(NT):
                for p0, b, c0, m in pieces(t):
                    sp.dma_start(pad_dram[b, c0:c0 + m, 0:70 - ROWS_V], img(t)[p0:p0 + m, ROWS_V:70]).then_inc(spilled, 16)
            sp.wait_ge(spilled, 2 * 64)
            sp.wait_ge(zeroed, 1)
            for u in range(NU):
                b, c0, slot = u % B, CP * (u // B), u % SLOTS
                if u == 2:
                    for g in range(1, NU // B):
                        sp.dma_start(wph[:, g, :], inp["w3p"][:, g, :]).then_inc(w_rest, 16)
                if u >= SLOTS:
                    sp.wait_ge(psum_done, 2 * (u - SLOTS) + 2)
                    sp.wait_ge(unit_out[slot], 64 * (u // SLOTS))
                for p in range(PH):
                    n = GI if p < 2 else GI - 1
                    sp.dma_start(pin[CP * p:CP * p + CP, slot, 0:n * PADW].rearrange("c (g w) -> c g w", w=PADW),
                                 by_phase(pad_dram[b, c0:c0 + CP])[:, p, 0:n]).then_inc(unit_in[slot], 16)
                    sp.dma_start(xs[CP * p:CP * p + CP, slot, :].rearrange("c (g w) -> c g w", w=W),
                                 by_phase(low_dram[b, c0:c0 + CP])[:, p]).then_inc(unit_in[slot], 16)
            sp.wait_ge(taps, NT * 49)
            for t in range(NT):
                for p0, b, c0, m in pieces(t):
                    sp.dma_start(xout[b, c0:c0 + m, 0:VP], xt[p0:p0 + m, t, 0:VP]).then_inc(spilled, 16)
            sp.wait_ge(spilled, 3 * 64)
            for slot in range(SLOTS):
                sp.wait_ge(unit_out[slot], 64 * (NU // SLOTS))

        @block.gpsimd
        def _(pool):
            nc.gpsimd.memset(pin[:, :, (GI - 1) * PADW:GI * PADW], 0.0).then_inc(zeroed, 1)

        @block.scalar
        def _(act):
            act.wait_ge(loaded, 48)
            for t in range(NT):
                nc.scalar.activation(xt[:, t, 0:VP], xt[:, t, 0:VP], ACT.Identity, bias=bias[:, t:t + 1]).then_inc(biased, 1)
            for u in range(NU):
                b, c0, slot = u % B, CP * (u // B), u % SLOTS
                act.wait_ge(added, 2 * u + 2)
                for p in range(PH):
                    act.dma_start(by_phase(xout[b, c0:c0 + CP, VP:HW].rearrange("c (r w) -> c r w", w=W))[:, p],
                                  xs[CP * p:CP * p + CP, slot, :].rearrange("c (g w) -> c g w", w=W)).then_inc(unit_out[slot], 16)

        @block.tensor
        def _(pe):
            pe.wait_ge(w_first, 16)
            for m in range(NB):
                u, h = m // 2, m % 2
                slot = u % SLOTS
                pe.wait_ge(unit_in[slot], 128 * (u // SLOTS + 1))
                if u == B:
                    pe.wait_ge(w_rest, 16 * (NU // B - 1))
                if m >= 8:
                    pe.wait_ge(added, m - 7)
                x = pin[:, slot, :].rearrange("c (g w) -> c g w", w=PADW)
                for k in range(TW):
                    o, dx = k // 7, k % 7
                    ins = nc.tensor.matmul(ps[:, m % 8, 0:HG * W].rearrange("p (g w) -> p g w", w=W), wph[:, u // B, 128 * k:128 * k + 128],
                                           x[:, HG * h + o:HG * h + o + HG, dx:dx + W], start=(k == 0), stop=(k == TW - 1))
                ins.then_inc(psum_done, 1)

        @block.vector
        def _(dve):
            V = nc.vector
            n = 0
            for t in range(NT):
                for i in range(3):
                    V.tensor_copy(img(t)[:, 3:67, i], img(t)[:, 3:67, 6 - i]).then_inc(chain, 1)
                    V.tensor_copy(img(t)[:, 3:67, 69 - i], img(t)[:, 3:67, 63 + i]).then_inc(chain, 1)
                    n += 2
                dve.wait_ge(chain, n)
                for i in range(3):
                    V.tensor_copy(img(t)[:, i, :], img(t)[:, 6 - i, :]).then_inc(chain, 1)
                    V.tensor_copy(img(t)[:, 69 - i, :], img(t)[:, 63 + i, :]).then_inc(chain, 1)
                    n += 2
                dve.wait_ge(chain, n)
            dve.wait_ge(biased, NT)

            def add_unit(m):
                u, h = m // 2, m % 2
                dve.wait_ge(psum_done, m + 1)
                x = xs[:, u % SLOTS, HG * W * h:HG * W * (h + 1)]
                V.scalar_tensor_tensor(out=x, in0=ps[:, m % 8, 0:HG * W], scalar=biasp[:, u // B:u // B + 1], in1=x,
                                       op0=ALU.add, op1=ALU.add).then_inc(added, 1)

            m = 0
            for a in range(49):
                for t in range(NT):
                    o = xt[:, t, 0:VP].rearrange("p (r w) -> p r w", w=W)
                    if a:
                        dve.wait_ge(taps, NT * (a - 1) + t + 1)
                    V.scalar_tensor_tensor(out=o, in0=img(t)[:, a // 7:a // 7 + ROWS_V, a % 7:a % 7 + W], scalar=wts[:, t, a:a + 1],
                                           in1=o, op0=ALU.mult, op1=ALU.add).then_inc(taps, 1)
                if a >= ADD_FROM and (a - ADD_FROM) % ADD_EVERY == 0 and m < NB:
                    add_unit(m)
                    m += 1
            while m < NB:
                add_unit(m)
                m += 1


def layouts(v):
    import numpy as np
    f = np.float32
    o = {"x": v["x"], "ident": np.eye(128, dtype=f)}

    def packed_rows(w):
        return w[0:128], np.concatenate([w[128:192], w[128:192]], 0)

    def packed_vec(w):
        return np.stack([w[0:128], w[0:128], np.concatenate([w[128:192], w[128:192]], 0)], 1)

    g = np.kron(np.eye(32), np.full((6, 6), 1.0 / 6.0)).astype(f)
    o["gmat"] = np.concatenate(packed_rows(g), 1)

    wq = v["L0_conv_w_qkv"].T
    wide = np.zeros((128, 3, QKV), f)
    wide[:, 0] = wq[0:128]
    wide[0:64, 1] = wq[128:192]
    wide[64:128, 2] = wq[128:192]
    o["wbase"] = wide
    dws = [v["L0_conv_w_dw3"][:, 0], v["L0_conv_w_dw5"][:, 0], v["L0_conv_w_dw7"][:, 0]]
    flat = np.concatenate([d.reshape(QKV, -1) for d in dws], 1)
    o["wt"] = np.concatenate([flat[0:128], np.concatenate([flat[128:TCH], flat[128:TCH]], 0)], 1)
    wd = np.zeros((2, NSH, CG, NG, NO, 3, 2, 2), f)
    for k in range(3):
        for g in range(P_GROUPS[k]):
            c0, n = TCH + 128 * k, P_GROUPS[k]
            ch = slice(c0 + g, c0 + CG * n, n)
            for ri, sh, o_, qr, ph in np.ndindex(2, NSH, NO, 2, 2):
                dy, dx = 2 * o_ + ri - qr - 3, sh - ph - 3
                for q, d in enumerate(dws):
                    r = KS[q] // 2
                    if max(abs(dy), abs(dx)) <= r:
                        wd[ri, sh, :, G0[k] + g, o_, q, qr, ph] = d[ch, dy + r, dx + r]
    o["wd"] = wd.reshape(128, NG * NO * NQ)
    o["mask8"] = np.concatenate([np.eye(CG, dtype=f)] * 2 * NSH, 0)
    pT = v["L0_conv_w_pconv"].T
    tiles = [pT[k * QKV + c:k * QKV + c + 128] for c in (0, TCH, TCH + 128, TCH + 256) for k in range(3)]
    c = 128
    tiles.append(np.concatenate([pT[c:c + 64], np.zeros((64, QKV), f)], 0))
    tiles.append(np.concatenate([pT[QKV + c:QKV + c + 64], pT[2 * QKV + c:2 * QKV + c + 64]], 0))
    o["pw"] = np.stack(tiles, 1)
    o["wproj0"] = v["L0_conv_w_proj"].T.reshape(2, HC, C).transpose(1, 0, 2)
    o["head_mask"] = np.kron(np.eye(HH), np.ones((HD, 1))).astype(f)
    o["temperature_rows"] = np.repeat(v["L0_conv_temperature"].reshape(2, HH), HD, 1).T
    o["scales_rows"] = np.broadcast_to(v["L0_conv_attn_scales"], (HC, 3))
    o["tri"] = np.broadcast_to(np.tril(np.ones((HD, HD), f), -1), (HC, HD, HD))

    w1 = v["L1_conv_w_qkv"]
    o["w1qk"] = w1[0:2 * C].T
    o["w1v"] = w1[2 * C:].reshape(2, HC, C).transpose(1, 0, 2)

    w2 = v["L2_conv_W_proj"].T
    z = np.zeros((C, N_STATE), f)
    bm, cm = w2[:, 2 * C:2 * C + N_STATE], w2[:, 2 * C + N_STATE:]
    w2p = np.concatenate([w2[:, 0:2 * C], bm, z, cm, z, z, bm, z, cm], 1)
    o["w2a"], o["w2c"] = packed_rows(w2p)
    for n, m in enumerate((bm, cm)):
        c0 = 2 * C + 32 * n
        o["w2c"][:, c0:c0 + 32] = 0
        o["w2c"][0:64, c0:c0 + N_STATE] = m[128:192]
        o["w2c"][64:128, c0 + N_STATE:c0 + 2 * N_STATE] = m[128:192]
    o["wo2a"], o["wo2c"] = packed_rows(v["L2_conv_W_out"].T)
    bp = v["L2_conv_b_proj"]
    five = np.stack([bp[0:C], bp[C:2 * C], v["L2_conv_dt_bias"], v["L2_conv_D"], v["L2_conv_b_out"]], 1)
    o["cols2"] = packed_vec(five).reshape(128, 15)
    bb, cb = bp[2 * C:2 * C + N_STATE], bp[2 * C + N_STATE:]
    o["bcbias2"] = np.concatenate([bb, bb, cb, cb]).reshape(64, 1)
    o["alog2"] = packed_vec(v["L2_conv_A_log"])
    sel = np.zeros((3, 32, NT, N_STATE, 128), f)
    for n in range(N_STATE):
        sel[:, n, 0, n, :] = 1
        sel[:, 16 + n, 1, n, :] = 1
        sel[:, n, 2, n, 0:64] = 1
        sel[:, 16 + n, 2, n, 64:128] = 1
    o["sel2"] = sel.reshape(96, NT * N_STATE * 128)
    w3 = v["L3_conv_w"][:, 0]
    wp = np.zeros((PH, CP, C // CP, 3, 7, PH, CP), f)
    for c in range(C):
        for o_ in range(3):
            for p in range(PH):
                for q in range(PH):
                    i = PH * o_ + p - q
                    if 0 <= i < 7:
                        wp[p, c % CP, c // CP, o_, :, q, c % CP] = w3[c, i]
    o["w3p"] = wp.reshape(128, C // CP, TW * 128)
    o["b3p"] = np.tile(v["L3_conv_b"].reshape(C // CP, CP).T, (PH, 1))
    o["w3"] = packed_vec(v["L3_conv_w"].reshape(C, 49))
    o["b3"] = packed_vec(v["L3_conv_b"])
    return o


def kernel(**inputs):
    import numpy as np
    import concourse.bacc as bacc
    from concourse.bass_utils import run_bass_kernel_spmd

    nc = bacc.Bacc("TRN2", target_bir_lowering=False, num_devices=1)
    arrays, aps = {}, {}
    for name, a in layouts({k: np.asarray(a) for k, a in inputs.items()}).items():
        a = np.ascontiguousarray(a)
        arrays[f"in_{name}"] = a
        aps[name] = nc.dram_tensor(f"in_{name}", a.shape, mybir.dt.from_np(a.dtype), kind="ExternalInput").ap()
    res = nc.dram_tensor("out_0", (B, C, H, W), F32, kind="ExternalOutput").ap()
    build(nc, aps, res)
    r = run_bass_kernel_spmd(nc, [arrays], core_ids=[0])
    return r.results[0]["out_0"]
```
